# Optimizing a Trainium2 kernel written in Bass

```python
import numpy as np
import jax
import jax.numpy as jnp

def _softmax(x, axis=-1):
    return jax.nn.softmax(x, axis=axis)

def _gelu(x):
    return jax.nn.gelu(x, approximate=True)

def _silu(x):
    return jax.nn.silu(x)

def _sigmoid(x):
    return jax.nn.sigmoid(x)

def _layernorm(x, axis=-1, eps=1e-05):
    m = jnp.mean(x, axis=axis, keepdims=True)
    v = jnp.var(x, axis=axis, keepdims=True)
    return (x - m) / jnp.sqrt(v + eps)

def _scatter_add(tgt, idx, src, axis=0):
    return tgt.at[idx].add(src)

def _segment_sum(src, seg, n):
    return jax.ops.segment_sum(src, seg, n)
kernel_name = 'mk_gnn_preln_d4_gnn_r8_6bb7cf'

def setup_inputs(seed: int=0):
    np.random.seed(seed)
    _w = jnp.asarray

    def _rec_inputs():
        import jax
        import jax.numpy as jnp
        _gk = jax.random.key(seed)
        x = -0.0003713 + 1 * jax.random.normal(jax.random.fold_in(_gk, 1), (6250, 256), jnp.float32)
        _s = jax.random.randint(jax.random.fold_in(_gk, 2), (50000,), 0, 6250, jnp.int32)
        _d = jax.random.randint(jax.random.fold_in(_gk, 3), (50000,), 0, 6250, jnp.int32)
        _loop = jnp.arange(6250, dtype=jnp.int32)
        src = jnp.concatenate([_s, _d, _loop])
        dst = jnp.concatenate([_d, _s, _loop])
        _o = jnp.argsort(dst, stable=True)
        src = src[_o]
        dst = dst[_o]
        edge_weight = jax.random.uniform(jax.random.fold_in(_gk, 13), (106250,), jnp.float32, 0.0, 0.999998)
        node_vec = jax.random.uniform(jax.random.fold_in(_gk, 14), (6250,), jnp.float32, 0.0, 0.999833)
        return (x, src, dst, edge_weight, node_vec)
    x, src, dst, edge_weight, node_vec = _rec_inputs()

    def _L0_gnn_setup():
        import jax, jax.numpy as jnp
        import numpy as np
        N_NODES = 6250
        N_EDGES = 100000
        IN_C = 256
        OUT_C = 64
        N_HEADS = 4
        N_LAYERS = 3
        BN_EPS = 1e-05
        LEAKY_SLOPE = 0.01

        def _segment_softmax(scores, seg_ids, num_segments):
            smax = jax.vmap(lambda s: jax.ops.segment_max(s, seg_ids, num_segments=num_segments))(scores)
            e = jnp.exp(scores - smax[:, seg_ids])
            denom = jax.vmap(lambda x: jax.ops.segment_sum(x, seg_ids, num_segments=num_segments))(e)
            return e / jnp.maximum(denom[:, seg_ids], 1e-16)
        key = jax.random.key(seed)
        ks = jax.random.split(key, 9)
        return {'features': jax.random.normal(ks[0], (N_NODES, IN_C), dtype=jnp.float32), 'edge_src': jax.random.randint(ks[1], (N_EDGES,), 0, N_NODES, dtype=jnp.int32), 'edge_dst': jax.random.randint(ks[2], (N_EDGES,), 0, N_NODES, dtype=jnp.int32), 'bn_gamma': jax.random.uniform(ks[3], (N_LAYERS, IN_C), dtype=jnp.float32), 'bn_beta': jax.random.normal(ks[4], (N_LAYERS, IN_C), dtype=jnp.float32) * 0.1, 'W': jax.random.normal(ks[5], (N_LAYERS, N_HEADS, IN_C, OUT_C), dtype=jnp.float32) / np.sqrt(IN_C), 'attn_l': jax.random.normal(ks[6], (N_LAYERS, N_HEADS, OUT_C), dtype=jnp.float32) / np.sqrt(OUT_C), 'attn_r': jax.random.normal(ks[7], (N_LAYERS, N_HEADS, OUT_C), dtype=jnp.float32) / np.sqrt(OUT_C), 'res_W': jax.random.normal(ks[8], (N_LAYERS, N_HEADS, IN_C, OUT_C), dtype=jnp.float32) / np.sqrt(IN_C)}
    _L0_gnn_all = _L0_gnn_setup()
    _L0_gnn_in = {k: v for k, v in _L0_gnn_all.items() if k in ('bn_gamma', 'bn_beta', 'W', 'attn_l', 'attn_r', 'res_W')}
    del _L0_gnn_all

    def _L1_gnn_setup():
        import jax, jax.numpy as jnp
        import numpy as np
        from jax import lax
        N, E, D = (1024, 32768, 256)
        NH, FOUT = (4, 64)
        D_STATE, D_CONV, DT_RANK = (16, 4, 16)

        def _layer_norm(x, g, b, eps=1e-05):
            mu = jnp.mean(x, -1, keepdims=True)
            var = jnp.var(x, -1, keepdims=True)
            return (x - mu) * lax.rsqrt(var + eps) * g + b

        def _mamba(xs, in_proj_w, conv_w, conv_b, x_proj_w, dt_proj_w, dt_proj_b, A_log, D_param, out_proj_w):
            n = xs.shape[0]
            xz = xs @ in_proj_w.T
            xc, z = jnp.split(xz, 2, axis=-1)
            K = conv_w.shape[1]
            xp = jnp.pad(xc, ((K - 1, 0), (0, 0)))
            xc = sum((xp[k:k + n] * conv_w[:, k] for k in range(K))) + conv_b
            xc = jax.nn.silu(xc)
            dbc = xc @ x_proj_w.T
            dt = jax.nn.softplus(dbc[:, :DT_RANK] @ dt_proj_w.T + dt_proj_b)
            Bm = dbc[:, DT_RANK:DT_RANK + D_STATE]
            Cm = dbc[:, DT_RANK + D_STATE:]
            A = -jnp.exp(A_log)
            dA = jnp.exp(dt[:, :, None] * A)
            dBx = (dt * xc)[:, :, None] * Bm[:, None, :]

            def step(h, t):
                dA_t, dBx_t, C_t = t
                h = dA_t * h + dBx_t
                return (h, h @ C_t)
            _, y = lax.scan(step, jnp.zeros((xc.shape[1], D_STATE), xs.dtype), (dA, dBx, Cm))
            y = y + xc * D_param
            y = y * jax.nn.silu(z)
            return y @ out_proj_w.T

        def _forward(x, edge_index, deg_noise, gat_w, gat_a_src, gat_a_tgt, gat_b, ln_local_g, ln_local_b, ln_global_g, ln_global_b, ln2_g, ln2_b, in_proj_w, conv_w, conv_b, x_proj_w, dt_proj_w, dt_proj_b, A_log, D_param, out_proj_w, wl, wg, ff1_w, ff1_b, ff2_w, ff2_b):
            n = x.shape[0]
            src, tgt = (edge_index[0], edge_index[1])
            proj = (x @ gat_w.T).reshape(n, NH, FOUT)
            s_src = jnp.sum(proj * gat_a_src, -1)
            s_tgt = jnp.sum(proj * gat_a_tgt, -1)
            e = jax.nn.leaky_relu(s_src[src] + s_tgt[tgt], 0.2)
            exp_e = jnp.exp(e - jnp.max(e))
            denom = jax.ops.segment_sum(exp_e, tgt, num_segments=n)
            attn = exp_e / (denom[tgt] + 1e-16)
            agg = jax.ops.segment_sum(proj[src] * attn[:, :, None], tgt, num_segments=n)
            h_local = jax.nn.elu((agg + x.reshape(n, NH, FOUT)).reshape(n, NH * FOUT) + gat_b)
            h_local = _layer_norm(h_local, ln_local_g, ln_local_b)
            deg = jax.ops.segment_sum(jnp.ones((src.shape[0],), x.dtype), src, num_segments=n)
            perm = jnp.argsort(deg + deg_noise, stable=True)
            inv = jnp.argsort(perm)
            y = _mamba(x[perm], in_proj_w, conv_w, conv_b, x_proj_w, dt_proj_w, dt_proj_b, A_log, D_param, out_proj_w)
            h_attn = _layer_norm(x + y[inv], ln_global_g, ln_global_b)
            gate = jax.nn.sigmoid(h_local @ wl.T + h_attn @ wg.T)
            h = gate * h_local + (1.0 - gate) * h_attn
            ff = jax.nn.relu(h @ ff1_w.T + ff1_b) @ ff2_w.T + ff2_b
            return _layer_norm(h + ff, ln2_g, ln2_b)
        key = jax.random.key(seed)
        ks = jax.random.split(key, 24)
        w = lambda i, shape, s=0.05: jax.random.normal(ks[i], shape, dtype=jnp.float32) * s
        return {'x': jax.random.normal(ks[0], (N, D), dtype=jnp.float32), 'edge_index': jax.random.randint(ks[1], (2, E), 0, N, dtype=jnp.int32), 'edge_prob': jax.random.uniform(ks[2], (E,), dtype=jnp.float32), 'deg_noise': jax.random.uniform(ks[3], (N,), dtype=jnp.float32), 'gat_w': w(4, (NH * FOUT, D)), 'gat_a_src': w(5, (NH, FOUT)), 'gat_a_tgt': w(6, (NH, FOUT)), 'gat_b': jnp.zeros((NH * FOUT,), jnp.float32), 'ln_local_g': jnp.ones((D,), jnp.float32), 'ln_local_b': jnp.zeros((D,), jnp.float32), 'ln_global_g': jnp.ones((D,), jnp.float32), 'ln_global_b': jnp.zeros((D,), jnp.float32), 'ln2_g': jnp.ones((D,), jnp.float32), 'ln2_b': jnp.zeros((D,), jnp.float32), 'in_proj_w': w(7, (2 * D, D)), 'conv_w': w(8, (D, D_CONV), 0.2), 'conv_b': jnp.zeros((D,), jnp.float32), 'x_proj_w': w(9, (DT_RANK + 2 * D_STATE, D)), 'dt_proj_w': w(10, (D, DT_RANK)), 'dt_proj_b': w(11, (D,), 0.1) - 4.0, 'A_log': jnp.log(jnp.tile(jnp.arange(1, D_STATE + 1, dtype=jnp.float32), (D, 1))), 'D_param': jnp.ones((D,), jnp.float32), 'out_proj_w': w(12, (D, D)), 'wl': w(13, (D, D)), 'wg': w(14, (D, D)), 'ff1_w': w(15, (2 * D, D)), 'ff1_b': jnp.zeros((2 * D,), jnp.float32), 'ff2_w': w(16, (D, 2 * D)), 'ff2_b': jnp.zeros((D,), jnp.float32)}
    _L1_gnn_all = _L1_gnn_setup()
    _L1_gnn_in = {k: v for k, v in _L1_gnn_all.items() if k in ('gat_w', 'gat_a_src', 'gat_a_tgt', 'gat_b', 'ln_local_g', 'ln_local_b', 'ln_global_g', 'ln_global_b', 'ln2_g', 'ln2_b', 'in_proj_w', 'conv_w', 'conv_b', 'x_proj_w', 'dt_proj_w', 'dt_proj_b', 'A_log', 'D_param', 'out_proj_w', 'wl', 'wg', 'ff1_w', 'ff1_b', 'ff2_w', 'ff2_b')}
    del _L1_gnn_all

    def _L2_gnn_setup():
        import jax, jax.numpy as jnp
        import numpy as np
        N_NODES = 12500
        N_EDGES = 400000
        DIM = 256
        LEAKY_SLOPE = 0.2
        EPS = 1e-12
        key = jax.random.key(seed)
        ks = jax.random.split(key, 8)
        embeddings = jax.random.normal(ks[0], (N_NODES, DIM), dtype=jnp.float32)
        edge_src = jax.random.randint(ks[1], (N_EDGES,), 0, N_NODES, dtype=jnp.int32)
        edge_dst = jax.random.randint(ks[2], (N_EDGES,), 0, N_NODES, dtype=jnp.int32)
        edge_val = jax.random.uniform(ks[3], (N_EDGES,), dtype=jnp.float32) / 32.0
        scale = 1.0 / np.sqrt(DIM)
        W1 = jax.random.normal(ks[4], (DIM, DIM), dtype=jnp.float32) * scale
        b1 = jax.random.normal(ks[5], (DIM,), dtype=jnp.float32) * 0.01
        W2 = jax.random.normal(ks[6], (DIM, DIM), dtype=jnp.float32) * scale
        b2 = jax.random.normal(ks[7], (DIM,), dtype=jnp.float32) * 0.01
        return {'embeddings': embeddings, 'edge_src': edge_src, 'edge_dst': edge_dst, 'edge_val': edge_val, 'W1': W1, 'b1': b1, 'W2': W2, 'b2': b2}
    _L2_gnn_all = _L2_gnn_setup()
    _L2_gnn_in = {k: v for k, v in _L2_gnn_all.items() if k in ('W1', 'b1', 'W2', 'b2')}
    del _L2_gnn_all

    def _L3_gnn_setup():
        import jax, jax.numpy as jnp
        import numpy as np
        N_NODES = 1250
        N_EDGES = 40000
        D = 256
        key = jax.random.key(seed)
        k_x, k_w, k_m, k_s, k_d = jax.random.split(key, 5)
        x = jax.random.normal(k_x, (N_NODES, D), dtype=jnp.float32)
        W = jax.random.normal(k_w, (D, D), dtype=jnp.float32)
        M = jax.random.normal(k_m, (D, D), dtype=jnp.float32)
        edge_src = jax.random.randint(k_s, (N_EDGES,), 0, N_NODES, dtype=jnp.int64)
        edge_dst = jax.random.randint(k_d, (N_EDGES,), 0, N_NODES, dtype=jnp.int64)
        return {'x': x, 'W': W, 'M': M, 'edge_src': edge_src, 'edge_dst': edge_dst}
    _L3_gnn_all = _L3_gnn_setup()
    _L3_gnn_in = {k: v for k, v in _L3_gnn_all.items() if k in ('W', 'M')}
    del _L3_gnn_all
    return {'x': x, 'src': src, 'dst': dst, 'edge_weight': edge_weight, 'node_vec': node_vec, 'L0_gnn_bn_gamma': _L0_gnn_in['bn_gamma'], 'L0_gnn_bn_beta': _L0_gnn_in['bn_beta'], 'L0_gnn_W': _L0_gnn_in['W'], 'L0_gnn_attn_l': _L0_gnn_in['attn_l'], 'L0_gnn_attn_r': _L0_gnn_in['attn_r'], 'L0_gnn_res_W': _L0_gnn_in['res_W'], 'L1_gnn_gat_w': _L1_gnn_in['gat_w'], 'L1_gnn_gat_a_src': _L1_gnn_in['gat_a_src'], 'L1_gnn_gat_a_tgt': _L1_gnn_in['gat_a_tgt'], 'L1_gnn_gat_b': _L1_gnn_in['gat_b'], 'L1_gnn_ln_local_g': _L1_gnn_in['ln_local_g'], 'L1_gnn_ln_local_b': _L1_gnn_in['ln_local_b'], 'L1_gnn_ln_global_g': _L1_gnn_in['ln_global_g'], 'L1_gnn_ln_global_b': _L1_gnn_in['ln_global_b'], 'L1_gnn_ln2_g': _L1_gnn_in['ln2_g'], 'L1_gnn_ln2_b': _L1_gnn_in['ln2_b'], 'L1_gnn_in_proj_w': _L1_gnn_in['in_proj_w'], 'L1_gnn_conv_w': _L1_gnn_in['conv_w'], 'L1_gnn_conv_b': _L1_gnn_in['conv_b'], 'L1_gnn_x_proj_w': _L1_gnn_in['x_proj_w'], 'L1_gnn_dt_proj_w': _L1_gnn_in['dt_proj_w'], 'L1_gnn_dt_proj_b': _L1_gnn_in['dt_proj_b'], 'L1_gnn_A_log': _L1_gnn_in['A_log'], 'L1_gnn_D_param': _L1_gnn_in['D_param'], 'L1_gnn_out_proj_w': _L1_gnn_in['out_proj_w'], 'L1_gnn_wl': _L1_gnn_in['wl'], 'L1_gnn_wg': _L1_gnn_in['wg'], 'L1_gnn_ff1_w': _L1_gnn_in['ff1_w'], 'L1_gnn_ff1_b': _L1_gnn_in['ff1_b'], 'L1_gnn_ff2_w': _L1_gnn_in['ff2_w'], 'L1_gnn_ff2_b': _L1_gnn_in['ff2_b'], 'L2_gnn_W1': _L2_gnn_in['W1'], 'L2_gnn_b1': _L2_gnn_in['b1'], 'L2_gnn_W2': _L2_gnn_in['W2'], 'L2_gnn_b2': _L2_gnn_in['b2'], 'L3_gnn_W': _L3_gnn_in['W'], 'L3_gnn_M': _L3_gnn_in['M']}

def reference(x, src, dst, edge_weight, node_vec, L0_gnn_bn_gamma, L0_gnn_bn_beta, L0_gnn_W, L0_gnn_attn_l, L0_gnn_attn_r, L0_gnn_res_W, L1_gnn_gat_w, L1_gnn_gat_a_src, L1_gnn_gat_a_tgt, L1_gnn_gat_b, L1_gnn_ln_local_g, L1_gnn_ln_local_b, L1_gnn_ln_global_g, L1_gnn_ln_global_b, L1_gnn_ln2_g, L1_gnn_ln2_b, L1_gnn_in_proj_w, L1_gnn_conv_w, L1_gnn_conv_b, L1_gnn_x_proj_w, L1_gnn_dt_proj_w, L1_gnn_dt_proj_b, L1_gnn_A_log, L1_gnn_D_param, L1_gnn_out_proj_w, L1_gnn_wl, L1_gnn_wg, L1_gnn_ff1_w, L1_gnn_ff1_b, L1_gnn_ff2_w, L1_gnn_ff2_b, L2_gnn_W1, L2_gnn_b1, L2_gnn_W2, L2_gnn_b2, L3_gnn_W, L3_gnn_M):
    import jax
    import jax.numpy as jnp

    def _L0_gnn_ref(features, edge_src, edge_dst, bn_gamma, bn_beta, W, attn_l, attn_r, res_W):
        import jax, jax.numpy as jnp
        import numpy as np
        N_NODES = 6250
        N_EDGES = 100000
        IN_C = 256
        OUT_C = 64
        N_HEADS = 4
        N_LAYERS = 3
        BN_EPS = 1e-05
        LEAKY_SLOPE = 0.01

        def _segment_softmax(scores, seg_ids, num_segments):
            smax = jax.vmap(lambda s: jax.ops.segment_max(s, seg_ids, num_segments=num_segments))(scores)
            e = jnp.exp(scores - smax[:, seg_ids])
            denom = jax.vmap(lambda x: jax.ops.segment_sum(x, seg_ids, num_segments=num_segments))(e)
            return e / jnp.maximum(denom[:, seg_ids], 1e-16)
        N = features.shape[0]
        acts = [jax.nn.relu, jnp.tanh, jax.nn.elu]
        out = jnp.zeros((N, N_HEADS * OUT_C), dtype=features.dtype)
        for l in range(N_LAYERS):
            mu = features.mean(axis=0)
            var = features.var(axis=0)
            h = (features - mu) * jax.lax.rsqrt(var + BN_EPS) * bn_gamma[l] + bn_beta[l]
            ft = jnp.einsum('nc,hcd->hnd', h, W[l])
            a1 = jnp.einsum('hnd,hd->hn', ft, attn_l[l])
            a2 = jnp.einsum('hnd,hd->hn', ft, attn_r[l])
            s = jax.nn.leaky_relu(a1[:, edge_dst] + a2[:, edge_src], negative_slope=LEAKY_SLOPE)
            alpha = _segment_softmax(s, edge_dst, N)
            msg = alpha[..., None] * ft[:, edge_src]
            accum = jax.vmap(lambda m: jax.ops.segment_sum(m, edge_dst, num_segments=N))(msg)
            res = jnp.einsum('nc,hcd->hnd', h, res_W[l])
            head_out = acts[l](accum + res)
            out = out + head_out.transpose(1, 0, 2).reshape(N, N_HEADS * OUT_C)
        return out

    def _L1_gnn_ref(x, edge_index, edge_prob, deg_noise, gat_w, gat_a_src, gat_a_tgt, gat_b, ln_local_g, ln_local_b, ln_global_g, ln_global_b, ln2_g, ln2_b, in_proj_w, conv_w, conv_b, x_proj_w, dt_proj_w, dt_proj_b, A_log, D_param, out_proj_w, wl, wg, ff1_w, ff1_b, ff2_w, ff2_b):
        import jax, jax.numpy as jnp
        import numpy as np
        from jax import lax
        N, E, D = (1024, 32768, 256)
        NH, FOUT = (4, 64)
        D_STATE, D_CONV, DT_RANK = (16, 4, 16)

        def _layer_norm(x, g, b, eps=1e-05):
            mu = jnp.mean(x, -1, keepdims=True)
            var = jnp.var(x, -1, keepdims=True)
            return (x - mu) * lax.rsqrt(var + eps) * g + b

        def _mamba(xs, in_proj_w, conv_w, conv_b, x_proj_w, dt_proj_w, dt_proj_b, A_log, D_param, out_proj_w):
            n = xs.shape[0]
            xz = xs @ in_proj_w.T
            xc, z = jnp.split(xz, 2, axis=-1)
            K = conv_w.shape[1]
            xp = jnp.pad(xc, ((K - 1, 0), (0, 0)))
            xc = sum((xp[k:k + n] * conv_w[:, k] for k in range(K))) + conv_b
            xc = jax.nn.silu(xc)
            dbc = xc @ x_proj_w.T
            dt = jax.nn.softplus(dbc[:, :DT_RANK] @ dt_proj_w.T + dt_proj_b)
            Bm = dbc[:, DT_RANK:DT_RANK + D_STATE]
            Cm = dbc[:, DT_RANK + D_STATE:]
            A = -jnp.exp(A_log)
            dA = jnp.exp(dt[:, :, None] * A)
            dBx = (dt * xc)[:, :, None] * Bm[:, None, :]

            def step(h, t):
                dA_t, dBx_t, C_t = t
                h = dA_t * h + dBx_t
                return (h, h @ C_t)
            _, y = lax.scan(step, jnp.zeros((xc.shape[1], D_STATE), xs.dtype), (dA, dBx, Cm))
            y = y + xc * D_param
            y = y * jax.nn.silu(z)
            return y @ out_proj_w.T

        def _forward(x, edge_index, deg_noise, gat_w, gat_a_src, gat_a_tgt, gat_b, ln_local_g, ln_local_b, ln_global_g, ln_global_b, ln2_g, ln2_b, in_proj_w, conv_w, conv_b, x_proj_w, dt_proj_w, dt_proj_b, A_log, D_param, out_proj_w, wl, wg, ff1_w, ff1_b, ff2_w, ff2_b):
            n = x.shape[0]
            src, tgt = (edge_index[0], edge_index[1])
            proj = (x @ gat_w.T).reshape(n, NH, FOUT)
            s_src = jnp.sum(proj * gat_a_src, -1)
            s_tgt = jnp.sum(proj * gat_a_tgt, -1)
            e = jax.nn.leaky_relu(s_src[src] + s_tgt[tgt], 0.2)
            exp_e = jnp.exp(e - jnp.max(e))
            denom = jax.ops.segment_sum(exp_e, tgt, num_segments=n)
            attn = exp_e / (denom[tgt] + 1e-16)
            agg = jax.ops.segment_sum(proj[src] * attn[:, :, None], tgt, num_segments=n)
            h_local = jax.nn.elu((agg + x.reshape(n, NH, FOUT)).reshape(n, NH * FOUT) + gat_b)
            h_local = _layer_norm(h_local, ln_local_g, ln_local_b)
            deg = jax.ops.segment_sum(jnp.ones((src.shape[0],), x.dtype), src, num_segments=n)
            perm = jnp.argsort(deg + deg_noise, stable=True)
            inv = jnp.argsort(perm)
            y = _mamba(x[perm], in_proj_w, conv_w, conv_b, x_proj_w, dt_proj_w, dt_proj_b, A_log, D_param, out_proj_w)
            h_attn = _layer_norm(x + y[inv], ln_global_g, ln_global_b)
            gate = jax.nn.sigmoid(h_local @ wl.T + h_attn @ wg.T)
            h = gate * h_local + (1.0 - gate) * h_attn
            ff = jax.nn.relu(h @ ff1_w.T + ff1_b) @ ff2_w.T + ff2_b
            return _layer_norm(h + ff, ln2_g, ln2_b)
        return _forward(x, edge_index, deg_noise, gat_w, gat_a_src, gat_a_tgt, gat_b, ln_local_g, ln_local_b, ln_global_g, ln_global_b, ln2_g, ln2_b, in_proj_w, conv_w, conv_b, x_proj_w, dt_proj_w, dt_proj_b, A_log, D_param, out_proj_w, wl, wg, ff1_w, ff1_b, ff2_w, ff2_b)

    def _L2_gnn_ref(embeddings, edge_src, edge_dst, edge_val, W1, b1, W2, b2):
        import jax, jax.numpy as jnp
        import numpy as np
        N_NODES = 12500
        N_EDGES = 400000
        DIM = 256
        LEAKY_SLOPE = 0.2
        EPS = 1e-12
        ego_emb = embeddings @ W1.T + b1
        messages = edge_val[:, None] * embeddings[edge_src]
        neighbor_emb = jax.ops.segment_sum(messages, edge_dst, num_segments=embeddings.shape[0])
        interaction_emb = neighbor_emb * embeddings
        side_emb = (neighbor_emb + interaction_emb) @ W2.T + b2
        out = ego_emb + side_emb
        out = jnp.where(out >= 0, out, LEAKY_SLOPE * out)
        norm = jnp.sqrt(jnp.sum(out * out, axis=1, keepdims=True))
        return out / jnp.maximum(norm, EPS)

    def _L3_gnn_ref(x, W, M, edge_src, edge_dst):
        import jax, jax.numpy as jnp
        import numpy as np
        N_NODES = 1250
        N_EDGES = 40000
        D = 256
        self_term = x @ W
        msg = x @ M
        agg = jax.ops.segment_sum(msg[edge_src], edge_dst, num_segments=x.shape[0])
        return jax.nn.relu(self_term + agg)
    edge_index = jnp.stack([src, dst])
    h = jnp.maximum(_layernorm(x, axis=-1), 0.0)
    x = x + _L0_gnn_ref(h, src, dst, L0_gnn_bn_gamma, L0_gnn_bn_beta, L0_gnn_W, L0_gnn_attn_l, L0_gnn_attn_r, L0_gnn_res_W)
    h = jnp.maximum(_layernorm(x, axis=-1), 0.0)
    x = x + _L1_gnn_ref(h, edge_index, edge_weight, node_vec, L1_gnn_gat_w, L1_gnn_gat_a_src, L1_gnn_gat_a_tgt, L1_gnn_gat_b, L1_gnn_ln_local_g, L1_gnn_ln_local_b, L1_gnn_ln_global_g, L1_gnn_ln_global_b, L1_gnn_ln2_g, L1_gnn_ln2_b, L1_gnn_in_proj_w, L1_gnn_conv_w, L1_gnn_conv_b, L1_gnn_x_proj_w, L1_gnn_dt_proj_w, L1_gnn_dt_proj_b, L1_gnn_A_log, L1_gnn_D_param, L1_gnn_out_proj_w, L1_gnn_wl, L1_gnn_wg, L1_gnn_ff1_w, L1_gnn_ff1_b, L1_gnn_ff2_w, L1_gnn_ff2_b)
    h = jnp.maximum(_layernorm(x, axis=-1), 0.0)
    x = x + _L2_gnn_ref(h, src, dst, edge_weight, L2_gnn_W1, L2_gnn_b1, L2_gnn_W2, L2_gnn_b2)
    h = jnp.maximum(_layernorm(x, axis=-1), 0.0)
    x = x + _L3_gnn_ref(h, L3_gnn_W, L3_gnn_M, src, dst)
    return x

_drawn_inputs = setup_inputs


def setup_inputs(seed=0):
    import zlib

    import numpy as np

    out = dict(_drawn_inputs(seed))
    spreads = {'L1_gnn_gat_b': (0.0, 0.1),
     'L1_gnn_ln_local_g': (1.0, 0.2),
     'L1_gnn_ln_local_b': (0.0, 0.289),
     'L1_gnn_ln_global_g': (1.0, 0.2),
     'L1_gnn_ln_global_b': (0.0, 0.348),
     'L1_gnn_ln2_g': (1.0, 0.2),
     'L1_gnn_ln2_b': (0.0, 0.1),
     'L1_gnn_conv_b': (0.0, 0.8),
     'L1_gnn_D_param': (1.0, 0.6),
     'L1_gnn_ff1_b': (0.0, 0.3),
     'L1_gnn_ff2_b': (0.0, 0.1)}
    factors = {'edge_weight': 64.0,
     'node_vec': 8.0,
     'L0_gnn_attn_l': 3.52,
     'L1_gnn_gat_a_src': 8.0,
     'L1_gnn_gat_a_tgt': 37.193,
     'L1_gnn_in_proj_w': 7.63,
     'L1_gnn_conv_w': 7.849,
     'L1_gnn_x_proj_w': 8.0,
     'L1_gnn_dt_proj_w': 8.0,
     'L1_gnn_dt_proj_b': 64.0,
     'L1_gnn_A_log': 8.0,
     'L1_gnn_out_proj_w': 7.57,
     'L2_gnn_W1': 64.0,
     'L2_gnn_b1': 64.0,
     'L2_gnn_b2': 64.0}
    for name, (base, spread) in spreads.items():
        noise = np.random.default_rng([zlib.crc32(name.encode()), seed]).standard_normal(out[name].shape)
        drawn = base * np.exp(spread * noise) if base else spread * noise
        out[name] = jnp.asarray(drawn.astype(out[name].dtype))
    for name, factor in factors.items():
        out[name] = (out[name] * factor).astype(out[name].dtype)
    return out
```

```python
from contextlib import ExitStack, contextmanager

import concourse.bass as bass
from concourse import mybir

F32 = mybir.dt.float32
BF16 = mybir.dt.bfloat16
I32 = mybir.dt.int32
ALU = mybir.AluOpType
ACT = mybir.ActivationFunctionType
AX = mybir.AxisListType.X
ENG = mybir.EngineType
RMAX = bass.bass_isa.ReduceOp.max

P = 128
N, D, E = 6250, 256, 106250
T = -(-N // P)
NP = T * P
TAIL = N - (T - 1) * P
GT = 7
NG = T // GT
H, DH = 4, 64
L = 3
UE = 256
UNITS = E // UE + T
UB = 4
UC = 512
QP = 832
QB = 8
EPAD = 1 + max(P * QP, E + UE) + 256
FRONT = 1
BIG = 1.0e30
ROWS = NP + P
AW = L * D + L * H
SKIP = T + 1
TS = GT * P
HS = TS // 2
DS = 16


class Chain:

    def __init__(self, nc, sem):
        self.nc, self.sem = nc, sem
        self.base, self.local = 0, 0

    def wait(self, eng):
        value = self.base + self.local
        if not isinstance(value, int) or value:
            eng.wait_ge(self.sem, value)

    def step(self, eng, *instructions):
        self.wait(eng)
        for f in instructions:
            last = f()
        last.then_inc(self.sem, 1)
        self.local += 1

    def apart(self, *pairs):
        for eng in {id(e): e for e, _ in pairs}.values():
            self.wait(eng)
            for e, f in pairs:
                if e is eng:
                    f().then_inc(self.sem, 1)
        self.local += len(pairs)

    def dma(self, eng, *instructions):
        self.wait(eng)
        for f in instructions:
            f().then_inc(self.sem, 16)
        self.local += 16 * len(instructions)

    def gathers(self, pool, instructions, sem, value):
        self.wait(pool)
        for f in instructions:
            f().then_inc(sem, 16)
        pool.wait_ge(sem, value)
        pool.sem_inc(self.sem, 1)
        self.local += 1

    @contextmanager
    def loop(self, n, per):
        first = self.base + self.local
        assert isinstance(first, int)
        with self.nc.Fori(0, n) as i:
            self.base, self.local = first + i * per, 0
            yield i
            assert self.local < per, (self.local, per)
            self.wait(self.nc.sync)
            self.nc.sync.sem_inc(self.sem, per - self.local)
        self.base, self.local = first + n * per, 0


def at(dram, offset, pattern):
    return bass.AP(tensor=dram.tensor, offset=offset, ap=pattern)


def graph_stack_kernel(nc, a, out):
    ds = bass.ds
    sp, act, pool, dve, pe = nc.sync, nc.scalar, nc.gpsimd, nc.vector, nc.tensor

    root = ExitStack()
    with root:
        def sem(name):
            return root.enter_context(nc.semaphore(name))

        def maker(stack, kind):
            make = nc.sbuf_tensor if kind == "sb" else nc.psum_tensor
            return lambda name, shape, dt=F32: stack.enter_context(make(name, shape, dt))

        def scratch(name, shape, dt=F32):
            return nc.dram_tensor(name, shape, dt, kind="Internal").ap()

        def per_block(dram):
            return dram.rearrange("(t p) c -> p t c", p=P)

        sb = maker(root, "sb")

        src_pad = scratch("src_pad", [EPAD], I32)
        dst_pad = scratch("dst_pad", [EPAD], I32)
        w_pad = scratch("w_pad", [EPAD])
        table = scratch("table", [ROWS, AW])
        score_src = scratch("score_src", [ROWS, L * H])
        score_dst = scratch("score_dst", [ROWS, 2 * L * H])
        running = scratch("running", [P * QP, L * H])
        summed = scratch("summed", [(SKIP + 1) * P, AW])
        residual = scratch("residual", [NP, L * D])
        h_dram = scratch("h_dram", [ROWS, D])
        x_dram = scratch("x_dram", [NP, D])
        sorted_h = scratch("sorted_h", [NP, D])
        sorted_y = scratch("sorted_y", [NP, D])
        key_row = scratch("key_row", [NP])

        passed = sem("passed")
        chain = Chain(nc, sem("chain"))

        def fresh_chain(name):
            for e in (sp, act, pool, dve, pe):
                chain.wait(e)
            nc.all_engine_barrier()
            chain.sem, chain.base, chain.local = sem(name), 0, 0

        ident = sb("ident", [P, P])
        iota = sb("iota", [P, P])
        lane = sb("lane", [P, 1])
        ones = sb("ones", [P, P])
        count_in = sb("count_in", [P, T])
        count_out = sb("count_out", [P, T])
        last_edge = sb("last_edge", [P, T], I32)
        unit_src = sb("unit_src", [P, UC, 2], I32)
        unit_dst = sb("unit_dst", [P, UC, 2], I32)
        unit_rel = sb("unit_rel", [P, UC, 2])
        unit_w = sb("unit_w", [P, UC, 2])
        unit_keep = sb("unit_keep", [P, UC])
        unit_block = sb("unit_block", [1, UC], I32)
        rank_i = sb("rank_i", [P, T], I32)

        zeros = sb("zeros", [P, AW])
        chain.apart((pool, lambda: pool.iota(iota[:, :], [[1, P]], base=0, channel_multiplier=0,
                                            allow_small_or_imprecise_dtypes=True)),
                   (pool, lambda: pool.iota(lane[:, :], [[0, 1]], base=0, channel_multiplier=1,
                                            allow_small_or_imprecise_dtypes=True)),
                   (dve, lambda: dve.memset(ones[:, :], 1.0)),
                   (dve, lambda: dve.memset(zeros[:, :], 0.0)))
        chain.step(dve, lambda: dve.tensor_scalar(ident[:, :], iota[:, :], lane[:, 0:1], None, ALU.is_equal))

        with ExitStack() as local:
            lsb = maker(local, "sb")
            tail = EPAD - FRONT - E
            pad_i = lsb("pad_i", [1, tail], I32)
            pad_front = lsb("pad_front", [1, 2], I32)
            chain.apart((dve, lambda: dve.memset(pad_i[:, :], NP)),
                       (dve, lambda: dve.memset(pad_front[:, :], -1)))
            row = lambda v: v.rearrange("(o n) -> o n", o=1)
            copies = []
            for pad, given in ((src_pad, a["src"]), (dst_pad, a["dst"]), (w_pad, a["edge_weight"])):
                copies.append(lambda pad=pad, given=given: sp.dma_start(
                    pad[FRONT:FRONT + E].rearrange("(q n) -> q n", q=125), given.rearrange("(q n) -> q n", q=125)))
            for pad in (src_pad, dst_pad):
                copies.append(lambda pad=pad: sp.dma_start(row(pad[FRONT + E:EPAD]), pad_i[:, :]))
                copies.append(lambda pad=pad: sp.dma_start(row(pad[0:FRONT]), pad_front[:, 0:1]))
            copies.append(lambda: sp.dma_start(row(w_pad[FRONT + E:EPAD]), zeros[0:1, 0:tail]))
            copies.append(lambda: sp.dma_start(row(w_pad[0:FRONT]), zeros[0:1, 0:1]))
            for t in range(T + 1):
                copies.append(lambda t=t: sp.dma_start(summed[t * P:(t + 1) * P, :], zeros[:, :]))
            for d in (table, score_src, score_dst, h_dram):
                copies.append(lambda d=d: sp.dma_start(d[NP:ROWS, :], zeros[:, 0:d.shape[1]]))
            chain.dma(sp, *copies)
            fresh_chain("chain_setup")

        with ExitStack() as local:
            lsb, lps = maker(local, "sb"), maker(local, "ps")
            low = lsb("low", [P, QP])
            high = lsb("high", [P, QP])
            raw = lsb("raw", [P, QP], I32)
            part = lsb("part", [P, QP], I32)
            hot_low = lsb("hot_low", [P, 2, QB, P], BF16)
            hot_high = lsb("hot_high", [P, 2, QB, T], BF16)
            hot_zero = lsb("hot_zero", [P, P], BF16)
            counts = lps("counts", [P, T])
            made, summed_up = sem("hot_made"), sem("hot_summed")
            chain.step(dve, lambda: dve.memset(hot_zero[:, :], 0.0))
            done = 0
            for pad, count in ((dst_pad, count_in), (src_pad, count_out)):
                chain.dma(sp, lambda: sp.dma_start(raw[:, :], pad[FRONT:FRONT + P * QP].rearrange("(p j) -> p j", j=QP)))
                chain.step(dve, lambda: dve.tensor_scalar(part[:, :], raw[:, :], P - 1, None, ALU.bitwise_and))
                chain.step(dve, lambda: dve.tensor_copy(low[:, :], part[:, :]))
                chain.step(dve, lambda: dve.tensor_scalar(part[:, :], raw[:, :], 7, None, ALU.logical_shift_right))
                chain.step(dve, lambda: dve.tensor_copy(high[:, :], part[:, :]))
                chain.step(pe, lambda: pe.matmul(counts[:, :], hot_zero[:, :], hot_zero[:, 0:T], start=True, stop=False,
                                                 skip_group_check=True))
                chain.wait(dve)
                pairs = QP // QB // 2
                for e in (dve, pe):
                    with e.Fori(0, pairs) as i:
                        for b in range(2):
                            n = done + 2 * i + b
                            if e is dve:
                                dve.wait_ge(summed_up, n + 1)
                                for hot, of, width in ((hot_low, low, P), (hot_high, high, T)):
                                    dve.tensor_tensor(
                                        hot[:, b, :, :],
                                        iota[:, 0:width].unsqueeze(1).broadcast_to([P, QB, width]),
                                        of[:, ds((2 * i + b) * QB, QB)].unsqueeze(2).broadcast_to([P, QB, width]),
                                        ALU.is_equal).then_inc(made, 1)
                            else:
                                pe.wait_ge(made, 2 * n + 2)
                                for k in range(QB):
                                    mm = pe.matmul(counts[:, :], hot_low[:, b, k, :], hot_high[:, b, k, :],
                                                   start=False, stop=False, skip_group_check=True)
                                mm.then_inc(summed_up, 1)
                    if e is dve:
                        pe.sem_inc(summed_up, 2) if done == 0 else None
                done += 2 * pairs
                dve.wait_ge(summed_up, done + 2)
                chain.step(dve, lambda: dve.tensor_copy(count[:, :], counts[:, :]))
            fresh_chain("chain_schedule")

        with ExitStack() as local:
            lsb, lps = maker(local, "sb"), maker(local, "ps")
            tri = lsb("tri", [P, P])
            per_t = lsb("per_t", [P, T])
            upto_t = lsb("upto_t", [P, T])
            units_t = lsb("units_t", [P, T])
            units_i = lsb("units_i", [P, T], I32)
            upto_u = lsb("upto_u", [P, T])
            delta = lsb("delta", [P, T])
            pair = lsb("pair", [P, 2, T])
            cols = lsb("cols", [P, 2])
            ones_t = lsb("ones_t", [P, T])
            within = lsb("within", [P, T])
            unit_no = lsb("unit_no", [P, UC])
            past = lsb("past", [P, UC])
            chunk_first = lsb("chunk_first", [P, UC // P])
            block_f = lsb("block_f", [P, UC // P])
            start_f = lsb("start_f", [P, UC // P])
            start_i = lsb("start_i", [P, UC // P], I32)
            rel0 = lsb("rel0", [P, UC // P])
            row_block = lsb("row_block", [P, UC + 1])
            finished = lsb("finished", [P, UC])
            got_i = lsb("got_i", [P, 2, UE], I32)
            got_w = lsb("got_w", [P, UE])
            got_f = lsb("got_f", [P, 2, UE])
            turned = lps("turned", [P, 8, P])
            cut = sem("units_cut")
            small = lps("small", [P, 512])
            row_ps = lps("row_ps", [P, 512])

            chain.apart((dve, lambda: dve.tensor_scalar(tri[:, :], iota[:, :], lane[:, 0:1], None, ALU.is_ge)),
                       (dve, lambda: dve.memset(ones_t[:, :], 1.0)),
                       (pool, lambda: pool.iota(unit_no[:, :], [[1, UC]], base=0, channel_multiplier=0,
                                                allow_small_or_imprecise_dtypes=True)),
                       (pool, lambda: pool.iota(chunk_first[:, :], [[P, UC // P]], base=0, channel_multiplier=1,
                                                allow_small_or_imprecise_dtypes=True)))
            chain.step(pe, lambda: pe.matmul(small[:, 0:T], ones[:, :], count_in[:, :], start=True, stop=True))
            chain.step(pe, lambda: pe.matmul(small[:, 64:64 + T], tri[:, :], count_in[:, :], start=True, stop=True))
            chain.step(dve, lambda: dve.tensor_copy(per_t[:, :], small[:, 0:T]))
            chain.step(dve, lambda: dve.tensor_tensor_scan(upto_t[:, :], ones_t[:, :], per_t[:, :], 0.0, ALU.mult, ALU.add))
            chain.step(dve, lambda: dve.tensor_tensor(within[:, :], upto_t[:, :], per_t[:, :], ALU.subtract))
            chain.step(dve, lambda: dve.tensor_tensor(within[:, :], within[:, :], small[:, 64:64 + T], ALU.add))
            chain.step(dve, lambda: dve.tensor_scalar(within[:, :], within[:, :], -1.0, 0.0, ALU.add, ALU.max))
            chain.step(dve, lambda: dve.tensor_copy(last_edge[:, :], within[:, :]))
            chain.step(dve, lambda: dve.tensor_scalar(units_t[:, :], per_t[:, :], float(UE - 1), None, ALU.add))
            chain.step(dve, lambda: dve.tensor_copy(units_i[:, :], units_t[:, :]))
            chain.step(dve, lambda: dve.tensor_scalar(units_i[:, :], units_i[:, :], 8, None, ALU.logical_shift_right))
            chain.step(dve, lambda: dve.tensor_copy(units_t[:, :], units_i[:, :]))
            chain.step(dve, lambda: dve.tensor_tensor_scan(upto_u[:, :], ones_t[:, :], units_t[:, :], 0.0, ALU.mult, ALU.add))
            chain.step(dve, lambda: dve.scalar_tensor_tensor(delta[:, :], units_t[:, :], -float(UE), per_t[:, :],
                                                             ALU.mult, ALU.add))
            for k, v in enumerate((upto_u, delta)):
                chain.step(dve, lambda: dve.tensor_tensor(pair[:, k, :], v[:, :], ident[:, 0:T], ALU.mult))
                chain.step(dve, lambda: dve.tensor_reduce(cols[:, k:k + 1], pair[:, k, :], AX, ALU.add))
            chain.step(dve, lambda: dve.tensor_scalar(past[:, :], unit_no[:, :], cols[:, 0:1], None, ALU.is_ge))
            chain.step(dve, lambda: dve.memset(cols[:, 0:1], 1.0))
            chain.step(pe, *[lambda c=c: pe.matmul(small[:, 128 + 2 * c:130 + 2 * c], past[0:T, c * P:(c + 1) * P],
                                                   cols[0:T, :], start=True, stop=True) for c in range(UC // P)])
            chain.step(pe, lambda: pe.matmul(row_ps[:, :], ones[0:T, :], past[0:T, :], start=True, stop=True))
            by_chunk = small[:, 128:128 + 2 * (UC // P)].rearrange("p (c k) -> p k c", k=2)
            chain.step(dve, lambda: dve.tensor_copy(block_f[:, :], by_chunk[:, 0, :]))
            chain.step(dve, lambda: dve.scalar_tensor_tensor(start_f[:, :], chunk_first[:, :], float(UE), by_chunk[:, 1, :],
                                                             ALU.mult, ALU.add))
            chain.step(dve, lambda: dve.tensor_scalar(start_f[:, :], start_f[:, :], float(E), float(FRONT), ALU.min, ALU.add))
            chain.step(dve, lambda: dve.tensor_copy(start_i[:, :], start_f[:, :]))
            chain.step(dve, lambda: dve.tensor_scalar(rel0[:, :], block_f[:, :], -float(P), None, ALU.mult))
            chain.apart((dve, lambda: dve.tensor_copy(row_block[:, 0:UC], row_ps[:, :])),
                       (dve, lambda: dve.memset(row_block[:, UC:UC + 1], float(T))))
            chain.step(dve, lambda: dve.memset(unit_keep[:, 0:1], 0.0))
            chain.step(dve, lambda: dve.tensor_tensor(unit_keep[:, 1:UC], row_block[:, 1:UC], row_block[:, 0:UC - 1],
                                                      ALU.is_equal))
            chain.step(dve, lambda: dve.tensor_tensor(finished[:, :], row_block[:, 1:UC + 1], row_block[:, 0:UC],
                                                      ALU.is_equal))
            chain.step(dve, lambda: dve.scalar_tensor_tensor(finished[:, :], finished[:, :], float(SKIP), row_block[:, 0:UC],
                                                             ALU.mult, ALU.add))
            chain.step(dve, lambda: dve.tensor_scalar(finished[:, :], finished[:, :], float(SKIP), None, ALU.min))
            chain.step(dve, lambda: dve.tensor_copy(unit_block[:, :], finished[0:1, :]))
            for c in range(UC // P):
                idx = bass.IndirectOffsetOnAxis(start_i[:, c:c + 1], 0)
                col = lambda v: v.rearrange("(n o) -> n o", o=1)
                chain.gathers(pool, [
                    lambda: pool.indirect_dma_start(got_i[:, 0, :], None, col(src_pad), idx),
                    lambda: pool.indirect_dma_start(got_i[:, 1, :], None, col(dst_pad), idx),
                    lambda: pool.indirect_dma_start(got_w[:, :], None, col(w_pad), idx)], cut, 3 * 16 * (c + 1))
                chain.step(dve, lambda: dve.tensor_copy(got_f[:, :, :], got_i[:, :, :]))
                chain.step(pe, *[lambda k=k, v=v, h=h: pe.transpose(turned[:, 2 * k + h, :], v[:, h * P:(h + 1) * P],
                                                                    ident[:, :])
                                 for k, v in enumerate((got_f[:, 0, :], got_f[:, 1, :], got_w)) for h in range(2)])
                to = slice(c * P, (c + 1) * P)
                chain.apart(*[(dve, lambda k=k, v=v: dve.tensor_copy(
                    v[:, to, :].rearrange("p u h -> p h u"), turned[:, 2 * k:2 * k + 2, :]))
                    for k, v in enumerate((unit_src, unit_dst, unit_w))])
                chain.step(dve, lambda: dve.tensor_scalar(got_f[:, 1, :], got_f[:, 1, :], rel0[:, c:c + 1], None, ALU.add))
                chain.step(pe, *[lambda h=h: pe.transpose(turned[:, h, :], got_f[:, 1, h * P:(h + 1) * P], ident[:, :])
                                 for h in range(2)])
                chain.step(dve, lambda: dve.tensor_copy(unit_rel[:, to, :].rearrange("p u h -> p h u"), turned[:, 0:2, :]))
            fresh_chain("chain_first")

        def layer_norm(x3, out3, stat, square, g=GT, eps=1e-5, relu=False, gain=None, shift=None):
            mean, var = stat[:, 0, 0:g], stat[:, 1, 0:g]
            bc = lambda v: v.unsqueeze(2).broadcast_to([P, g, D])
            chain.step(dve, lambda: dve.tensor_reduce(mean, x3, AX, ALU.add))
            chain.step(dve, lambda: dve.tensor_scalar(mean, mean, 1.0 / D, None, ALU.mult))
            chain.step(dve, lambda: dve.tensor_tensor(out3, x3, bc(mean), ALU.subtract))
            chain.step(act, lambda: act.activation(square, out3, ACT.Square))
            chain.step(dve, lambda: dve.tensor_reduce(var, square, AX, ALU.add))
            chain.step(dve, lambda: dve.tensor_scalar(var, var, 1.0 / D, eps, ALU.mult, ALU.add))
            chain.step(act, lambda: act.activation(var, var, ACT.Sqrt))
            chain.step(dve, lambda: dve.reciprocal(var, var))
            chain.step(dve, lambda: dve.tensor_tensor(out3, out3, bc(var), ALU.mult))
            if gain is not None:
                chain.step(dve, lambda: dve.tensor_tensor(out3, out3, gain.unsqueeze(1).broadcast_to([P, g, D]), ALU.mult))
                chain.step(dve, lambda: dve.tensor_tensor(out3, out3, shift.unsqueeze(1).broadcast_to([P, g, D]), ALU.add))
            if relu:
                chain.step(act, lambda: act.activation(out3, out3, ACT.Relu))

        def turn_group(dst4, src3, ps, g=GT):
            for b in range(0, g, 2):
                m = min(2, g - b)
                chain.step(pe, *[lambda k=k, c=c: pe.transpose(ps[:, c, k, :], src3[:, b + k, c * P:(c + 1) * P], ident[:, :])
                                 for k in range(m) for c in range(2)])
                chain.step(act, lambda: act.activation(dst4[:, :, b:b + m, :], ps[:, :, 0:m, :], ACT.Copy))

        def elu(x, tmp, out):
            chain.step(dve, lambda: dve.tensor_scalar(tmp, x, 0.0, None, ALU.min))
            chain.step(act, lambda: act.activation(tmp, tmp, ACT.Exp))
            chain.step(dve, lambda: dve.tensor_scalar(tmp, tmp, -1.0, None, ALU.add))
            chain.step(dve, lambda: dve.scalar_tensor_tensor(out, x, 0.0, tmp, ALU.max, ALU.add))

        def segment_max(name, scores, heads, best):
            with ExitStack() as local:
                lsb, lps = maker(local, "sb"), maker(local, "ps")
                mine = lsb(f"mine_{name}", [P, QP, heads])
                src_q = lsb(f"src_q_{name}", [P, QP], I32)
                dst_q = lsb(f"dst_q_{name}", [P, QP + 1], I32)
                same = lsb(f"same_{name}", [P, QP])
                idx = lsb(f"idx_{name}", [P, 2, QB], I32)
                got = lsb(f"got_{name}", [P, 2, QB, heads])
                fresh = lsb(f"fresh_{name}", [P, 1])
                side = lsb(f"side_{name}", [P, 16])
                side_t = lsb(f"side_t_{name}", [16, 3, P])
                carry = lsb(f"carry_{name}", [P, 16])
                side_ps = lps(f"side_ps_{name}", [P, 2, P])
                chain.dma(sp,
                          lambda: sp.dma_start(src_q[:, :], src_pad[FRONT:FRONT + P * QP].rearrange("(p j) -> p j", j=QP)),
                          lambda: sp.dma_start(dst_q[:, :], at(dst_pad, 0, [[QP, P], [1, QP + 1]])))
                chain.wait(pool), chain.wait(dve)
                arrived = [sem(f"arrived_{name}{b}") for b in range(2)]
                picked, kept = sem(f"picked_{name}"), sem(f"kept_{name}")
                dve.sem_inc(kept, 2)
                with pool.Fori(0, QP // QB // 2) as i:
                    for b in range(2):
                        pool.wait_ge(kept, 2 * i + b + 1)
                        pool.tensor_copy(idx[:, b, :], src_q[:, ds((2 * i + b) * QB, QB)]).then_inc(picked, 1)
                        pool.wait_ge(picked, 2 * i + b + 1)
                        pool.sem_inc(passed, 1)
                        for k in range(QB):
                            pool.indirect_dma_start(got[:, b, k, :], None, scores,
                                                    bass.IndirectOffsetOnAxis(idx[:, b, k:k + 1], 0)
                                                    ).then_inc(arrived[b], 16)
                with dve.Fori(0, QP // QB // 2) as i:
                    for b in range(2):
                        dve.wait_ge(arrived[b], 16 * QB * (i + 1))
                        dve.tensor_copy(mine[:, ds((2 * i + b) * QB, QB), :], got[:, b, :, :]).then_inc(kept, 1)
                dve.wait_ge(kept, QP // QB + 2)
                chain.step(dve, lambda: dve.tensor_tensor(same[:, :], dst_q[:, 1:QP + 1], dst_q[:, 0:QP], ALU.not_equal))
                chain.step(dve, lambda: dve.tensor_reduce(fresh[:, :], same[:, :], AX, ALU.max))
                chain.step(dve, lambda: dve.tensor_scalar(same[:, :], same[:, :], -BIG, None, ALU.mult))
                for h in range(heads):
                    chain.step(dve, lambda: dve.tensor_tensor_scan(mine[:, :, h], same[:, :], mine[:, :, h], -BIG,
                                                                   ALU.add, ALU.max))
                chain.step(dve, lambda: dve.memset(side[:, :], 0.0))
                chain.step(dve, lambda: dve.tensor_copy(side[:, 0:heads], mine[:, QP - 1, :]))
                chain.step(pe, lambda: pe.transpose(side_ps[0:16, 0, :], side[:, :], ident[:, :]))
                chain.step(dve, lambda: dve.tensor_copy(side_t[:, 0, :], side_ps[0:16, 0, :]))
                chain.step(dve, lambda: dve.tensor_scalar(side[:, :], ones[:, 0:16], fresh[:, 0:1], -BIG, ALU.mult, ALU.mult))
                chain.step(pe, lambda: pe.transpose(side_ps[0:16, 1, :], side[:, :], ident[:, :]))
                chain.step(dve, lambda: dve.tensor_copy(side_t[:, 1, :], side_ps[0:16, 1, :]))
                chain.step(dve, lambda: dve.memset(side_t[:, 2, 0:1], -BIG))
                chain.step(dve, lambda: dve.tensor_tensor_scan(side_t[:, 0, :], side_t[:, 1, :], side_t[:, 0, :], -BIG,
                                                               ALU.add, ALU.max))
                chain.step(dve, lambda: dve.tensor_copy(side_t[:, 2, 1:P], side_t[:, 0, 0:P - 1]))
                chain.step(pe, lambda: pe.transpose(side_ps[:, 0, 0:16], side_t[:, 2, :], ident[0:16, 0:16]))
                chain.step(dve, lambda: dve.tensor_copy(carry[:, :], side_ps[:, 0, 0:16]))
                for h in range(heads):
                    chain.step(dve, lambda: dve.tensor_tensor_scan(mine[:, :, h], same[:, :], mine[:, :, h],
                                                                   carry[:, h:h + 1], ALU.add, ALU.max))
                run = at(running, 0, [[QP * heads, P], [1, QP * heads]])
                chain.dma(sp, lambda: sp.dma_start(run, mine[:, :, :].rearrange("p j h -> p (j h)")))
                table_run = at(running, 0, [[heads, P * QP], [1, heads]])
                chain.gathers(pool, [lambda t=t: pool.indirect_dma_start(
                    best[:, t, :], None, table_run, bass.IndirectOffsetOnAxis(last_edge[:, t:t + 1], 0)) for t in range(T)],
                    sem(f"read_{name}"), 16 * T)
                fresh_chain(f"chain_after_{name}")

        def edge_pass(name, width, heads=0, slope=0.0, weighted=False, tab=None, tab_dst=None):
            full = width + heads
            with ExitStack() as local:
                lsb, lps = maker(local, "sb"), maker(local, "ps")
                rows = lsb(f"rows_{name}", [P, UB, 2, full])
                hot = lsb(f"hot_{name}", [P, UB, 2, P])
                sums = lsb(f"sums_{name}", [P, UB, full])
                idx = lsb(f"idx_{name}", [P, 2, UB, 2], I32)
                if heads:
                    at_dst = lsb(f"at_dst_{name}", [P, UB, 2, 2 * heads])
                    idx_d = lsb(f"idx_d_{name}", [P, 2, UB, 2], I32)
                    score = lsb(f"score_{name}", [P, UB, 2, heads])
                acc = lps(f"acc_{name}", [P, 2, -(-full // 512) * 512])
                splits = [(a0, min(a0 + 512, full)) for a0 in range(0, full, 512)]

                landed = [sem(f"landed_{name}{v}") for v in range(UB)]
                stored = [sem(f"stored_{name}{v}") for v in range(UB)]
                s_idx, s_hot, s_score, s_exp, s_mul, s_pe, s_sum, s_free = (
                    sem(f"{n}_{name}") for n in ("idx", "hot", "score", "exp", "mul", "pe", "sum", "free"))
                per_unit = 16 * 2 * (2 if heads else 1)
                rounds = UNITS // UB
                assert UNITS % UB == 0 and rounds % 2 == 0
                pe.sem_inc(s_pe, UB)
                dve.sem_inc(s_sum, 2)
                for v in range(UB):
                    sp.sem_inc(stored[v], 16)

                with pool.Fori(0, rounds // 2) as i:
                    for half in range(2):
                        n = 2 * i + half
                        k = 2 if heads else 1
                        pool.tensor_copy(idx[:, half, :, :], unit_src[:, ds(n * UB, UB), :]).then_inc(s_idx, 1)
                        if heads:
                            pool.tensor_copy(idx_d[:, half, :, :], unit_dst[:, ds(n * UB, UB), :]).then_inc(s_idx, 1)
                        pool.wait_ge(s_idx, k * n + k)
                        for v in range(UB):
                            pool.wait_ge(s_pe, n * UB + v + 1)
                            pool.sem_inc(passed, 1)
                            for e in range(2):
                                pool.indirect_dma_start(rows[:, v, e, :], None, tab,
                                                        bass.IndirectOffsetOnAxis(idx[:, half, v, e:e + 1], 0)
                                                        ).then_inc(landed[v], 16)
                                if heads:
                                    pool.indirect_dma_start(at_dst[:, v, e, :], None, tab_dst,
                                                            bass.IndirectOffsetOnAxis(idx_d[:, half, v, e:e + 1], 0)
                                                            ).then_inc(landed[v], 16)

                def prepare(i, v):
                    u = i * UB + v
                    if not heads:
                        dve.wait_ge(s_pe, u + 1)
                    else:
                        dve.wait_ge(landed[v], per_unit * (i + 1))
                        dve.tensor_tensor(score[:, v, :, :], rows[:, v, :, width:full], at_dst[:, v, :, 0:heads],
                                          ALU.add).then_inc(s_score, 1)
                    dve.tensor_tensor(hot[:, v, :, :], iota[:, :].unsqueeze(1).broadcast_to([P, 2, P]),
                                      unit_rel[:, ds(u, 1), :].rearrange("p o e -> p (o e)").unsqueeze(2).broadcast_to([P, 2, P]),
                                      ALU.is_equal).then_inc(s_hot, 1)
                    if weighted:
                        dve.wait_ge(s_hot, 2 * u + 1)
                        dve.tensor_tensor(hot[:, v, :, :], hot[:, v, :, :],
                                          unit_w[:, ds(u, 1), :].rearrange("p o e -> p (o e)").unsqueeze(2).broadcast_to([P, 2, P]),
                                          ALU.mult).then_inc(s_hot, 1)
                    if heads:
                        dve.wait_ge(s_score, 3 * u + 1)
                        dve.scalar_tensor_tensor(score[:, v, :, :], score[:, v, :, :], slope, score[:, v, :, :],
                                                 ALU.mult, ALU.max).then_inc(s_score, 1)
                        dve.wait_ge(s_score, 3 * u + 2)
                        dve.tensor_tensor(score[:, v, :, :], score[:, v, :, :], at_dst[:, v, :, heads:2 * heads],
                                          ALU.subtract).then_inc(s_score, 1)

                def weigh(i, v):
                    u = i * UB + v
                    dve.wait_ge(s_exp, u + 1)
                    r = rows[:, v, :, 0:width].rearrange("p e (h d) -> p e h d", d=DH)
                    dve.tensor_tensor(r, r, rows[:, v, :, width:full].unsqueeze(3).broadcast_to([P, 2, heads, DH]),
                                      ALU.mult).then_inc(s_mul, 1)

                def collect(i, v):
                    u = i * UB + v
                    before = (v - 1) % UB
                    dve.wait_ge(s_pe, u + UB + 1)
                    dve.wait_ge(stored[v], 16 * (i + 1))
                    dve.wait_ge(s_sum, u + 2)
                    dve.scalar_tensor_tensor(sums[:, v, :], sums[:, before, :], unit_keep[:, ds(u, 1)],
                                             acc[:, v % 2, 0:full], ALU.mult, ALU.add).then_inc(s_sum, 1)

                dve.memset(sums[:, UB - 1, :], 0.0).then_inc(s_free, 1)
                dve.wait_ge(s_free, 1)

                def dve_round(i, first=False):
                    for v in range(UB):
                        prepare(i, v)
                        if heads and not (first and v < 1):
                            weigh(i if v >= 1 else i - 1, (v - 1) % UB)
                        if not (first and v < 2):
                            collect(i if v >= 2 else i - 1, (v - 2) % UB)

                dve_round(0, first=True)
                with dve.Fori(1, rounds) as i:
                    dve_round(i)
                if heads:
                    weigh(rounds - 1, UB - 1)
                collect(rounds - 1, UB - 2)
                collect(rounds - 1, UB - 1)

                if heads:
                    with act.Fori(0, rounds) as i:
                        for v in range(UB):
                            act.wait_ge(s_score, 3 * (i * UB + v) + 3)
                            act.activation(rows[:, v, :, width:full], score[:, v, :, :], ACT.Exp).then_inc(s_exp, 1)

                with pe.Fori(0, rounds) as i:
                    for v in range(UB):
                        u = i * UB + v
                        if heads:
                            pe.wait_ge(s_mul, u + 1)
                            pe.wait_ge(s_hot, u + 1)
                        else:
                            pe.wait_ge(landed[v], per_unit * (i + 1))
                            pe.wait_ge(s_hot, (2 if weighted else 1) * (u + 1))
                        pe.wait_ge(s_sum, u + 1)
                        for a0, a1 in splits:
                            for e in range(2):
                                mm = pe.matmul(acc[:, v % 2, a0:a1], hot[:, v, e, :], rows[:, v, e, a0:a1],
                                               start=(e == 0), stop=(e == 1))
                        mm.then_inc(s_pe, 1)

                dest = summed[:, 0:full]
                with sp.Fori(0, rounds) as i:
                    for v in range(UB):
                        block = sp.value_load(unit_block[0:1, ds(i * UB + v, 1)], min_val=0, max_val=SKIP)
                        sp.wait_ge(s_sum, i * UB + v + 3)
                        sp.dma_start(dest[ds(block * P, P), :], sums[:, v, :], cond=(block < SKIP)).then_inc(stored[v], 16)
                for v in range(UB):
                    sp.wait_ge(stored[v], 16 * (rounds + 1))
                nc.all_engine_barrier()

        stack0 = ExitStack()
        s0 = maker(stack0, "sb")
        hT = s0("hT", [P, 2, NP])
        score_at = s0("score_at", [P, T, 2 * L * H])
        with ExitStack() as local:
            lsb, lps = maker(local, "sb"), maker(local, "ps")
            xg = lsb("xg", [P, GT, D])
            hg = lsb("hg", [P, GT, D])
            sq = lsb("sq", [P, GT, D])
            stat = lsb("stat", [P, 2, GT])
            moments = lps("moments", [P, 2, 2])
            turn = lps("turn", [P, 2, 2, P])
            moment = lsb("moment", [P, 2, 2])
            chain.dma(sp, lambda: sp.dma_start(x_dram[0:N, :], a["x"][:, :]),
                      lambda: sp.dma_start(x_dram[N:NP, :], zeros[0:NP - N, 0:D]))
            chain.step(pe, *[lambda k=k: pe.matmul(moments[:, k, :], zeros[:, 0:P], zeros[:, 0:2], start=(k == 0), stop=False,
                                                   skip_group_check=True) for k in range(2)])
            with chain.loop(NG, 160) as g:
                chain.dma(sp, lambda: sp.dma_start(xg[:, :, :], per_block(x_dram)[:, ds(g * GT, GT), :]))
                layer_norm(xg[:, :, :], hg[:, :, :], stat, sq[:, :, :], relu=True)
                chain.step(act, lambda: act.activation(sq[:, :, :], hg[:, :, :], ACT.Square))
                chain.step(pe, *[lambda c=c, k=k, v=v, b=b: pe.matmul(
                    moments[:, c, k:k + 1], v[:, b, c * P:(c + 1) * P], ones[:, 0:1], start=False, stop=False,
                    skip_group_check=True) for k, v in enumerate((hg, sq)) for b in range(GT) for c in range(2)])
                turn_group(hT[:, :, ds(g * (GT * P), GT * P)].rearrange("p c (b n) -> p c b n", n=P), hg, turn)
            mean, var = lsb("mean", [P, 2]), lsb("var", [P, 2])
            msq = lsb("msq", [P, 2])
            chain.step(dve, lambda: dve.tensor_scalar(moment[:, :, :], moments[:, :, :], 1.0 / N, None, ALU.mult))
            chain.step(dve, lambda: dve.tensor_copy(mean[:, :], moment[:, :, 0]))
            chain.step(dve, lambda: dve.tensor_tensor(msq[:, :], mean[:, :], mean[:, :], ALU.mult))
            chain.step(dve, lambda: dve.tensor_tensor(var[:, :], moment[:, :, 1], msq[:, :], ALU.subtract))
            chain.step(dve, lambda: dve.tensor_scalar(var[:, :], var[:, :], 0.0, 1e-5, ALU.max, ALU.add))
            chain.step(act, lambda: act.activation(var[:, :], var[:, :], ACT.Sqrt))
            chain.step(dve, lambda: dve.reciprocal(var[:, :], var[:, :]))
            fresh_chain("chain_weights")
            NW = L * D
            wt = lsb("wt", [P, 2, 2, NW])
            ws = lsb("ws", [P, 2, 2 * L * H])
            wt_b = lsb("wt_b", [1, 2, NW])
            ws_b = lsb("ws_b", [1, 2 * L * H])
            att = lsb("att", [P, 2, NW])
            prod = lsb("prod", [P, NW])
            gam, bet = lsb("gam", [P, 2, L]), lsb("bet", [P, 2, L])
            scale, shift = lsb("scale", [P, 2, L]), lsb("shift", [P, 2, L])
            tab_ps = lps("tab_ps", [P, 2, 512])
            bias_ps = tab_ps[0:1, :, :]
            loads = []
            for l in range(L):
                for k, w in enumerate((a["L0_gnn_W"], a["L0_gnn_res_W"])):
                    for c in range(2):
                        loads.append(lambda l=l, k=k, w=w, c=c: sp.dma_start(
                            wt[:, c, k, l * D:(l + 1) * D].rearrange("p (h d) -> p h d", h=H),
                            w[l, :, c * P:(c + 1) * P, :].rearrange("h p d -> p h d")))
                for v, g_ in ((gam, a["L0_gnn_bn_gamma"]), (bet, a["L0_gnn_bn_beta"])):
                    for c in range(2):
                        loads.append(lambda l=l, v=v, g_=g_, c=c: sp.dma_start(
                            v[:, c, l:l + 1], g_[l, c * P:(c + 1) * P].rearrange("(p o) -> p o", o=1)))
            for k, v in enumerate((a["L0_gnn_attn_r"], a["L0_gnn_attn_l"])):
                loads.append(lambda k=k, v=v: sp.dma_start(att[:, k, :], v.rearrange("l h d -> (l h d)").partition_broadcast(P)))
            chain.dma(sp, *loads)
            bcl = lambda v: v.unsqueeze(2).broadcast_to([P, 2, L])
            chain.step(dve, lambda: dve.tensor_tensor(scale[:, :, :], gam[:, :, :], bcl(var[:, :]), ALU.mult))
            chain.step(dve, lambda: dve.tensor_tensor(shift[:, :, :], scale[:, :, :], bcl(mean[:, :]), ALU.mult))
            chain.step(dve, lambda: dve.tensor_tensor(shift[:, :, :], bet[:, :, :], shift[:, :, :], ALU.subtract))
            for l in range(L):
                chain.step(pe, *[lambda c=c, k=k: pe.matmul(bias_ps[:, k, 0:D], shift[:, c, l:l + 1],
                                                            wt[:, c, k, l * D:(l + 1) * D], start=(c == 0), stop=(c == 1))
                                 for k in range(2) for c in range(2)])
                chain.step(dve, lambda: dve.tensor_copy(wt_b[:, :, l * D:(l + 1) * D], bias_ps[:, :, 0:D]))
                chain.apart(*[(dve, lambda c=c: dve.tensor_scalar(
                    wt[:, c, :, l * D:(l + 1) * D], wt[:, c, :, l * D:(l + 1) * D], scale[:, c, l:l + 1], None, ALU.mult))
                    for c in range(2)])
            for k in range(2):
                for c in range(3):
                    w_, to_, n_ = (wt[:, c, 0, :], ws[:, c, :], P) if c < 2 else (wt_b[:, 0, :], ws_b[:, :], 1)
                    chain.step(dve, lambda: dve.tensor_tensor(prod[0:n_, :], w_, att[0:n_, k, :], ALU.mult))
                    chain.step(dve, lambda: dve.tensor_reduce(
                        to_[:, k * L * H:(k + 1) * L * H], prod[0:n_, :].rearrange("p (h d) -> p h d", d=DH), AX, ALU.add))
            hblk = lsb("hblk", [P, 2, P])
            orow = lsb("orow", [P, 2, NW + 2 * L * H])
            res_ps = lps("res_ps", [P, 2, 512])
            sc_ps = lps("sc_ps", [P, 512])
            fresh_chain("chain_tables")
            with chain.loop(T, 120) as t:
                chain.step(act, lambda: act.activation(hblk[:, :, :], hT[:, :, ds(t * P, P)], ACT.Copy))
                fs = []
                for k, ps in ((0, tab_ps), (1, res_ps)):
                    for z, (c0, c1) in enumerate(((0, 512), (512, NW))):
                        for c in range(3):
                            lhs = hblk[:, c, :] if c < 2 else ones[0:1, :]
                            rhs = wt[:, c, k, c0:c1] if c < 2 else wt_b[:, k, c0:c1]
                            fs.append(lambda ps=ps, z=z, c=c, lhs=lhs, rhs=rhs, n=c1 - c0: pe.matmul(
                                ps[:, z, 0:n], lhs, rhs, start=(c == 0), stop=(c == 2)))
                for c in range(3):
                    lhs = hblk[:, c, :] if c < 2 else ones[0:1, :]
                    rhs = ws[:, c, :] if c < 2 else ws_b[:, :]
                    fs.append(lambda c=c, lhs=lhs, rhs=rhs: pe.matmul(sc_ps[:, 0:2 * L * H], lhs, rhs, start=(c == 0), stop=(c == 2)))
                chain.step(pe, *fs)
                chain.apart(
                    (act, lambda: act.activation(orow[:, 0, 0:512], tab_ps[:, 0, :], ACT.Copy)),
                    (act, lambda: act.activation(orow[:, 0, 512:NW], tab_ps[:, 1, 0:NW - 512], ACT.Copy)),
                    (dve, lambda: dve.tensor_copy(orow[:, 1, 0:512], res_ps[:, 0, :])),
                    (dve, lambda: dve.tensor_copy(orow[:, 1, 512:NW], res_ps[:, 1, 0:NW - 512])),
                    (dve, lambda: dve.tensor_copy(orow[:, 0, NW:NW + 2 * L * H], sc_ps[:, 0:2 * L * H])),
                    (dve, lambda: dve.tensor_copy(score_at[:, ds(t, 1), 0:L * H].rearrange("p o h -> p (o h)"),
                                                  sc_ps[:, L * H:2 * L * H])))
                chain.dma(sp,
                          lambda: sp.dma_start(table[ds(t * P, P), :], orow[:, 0, 0:AW]),
                          lambda: sp.dma_start(score_src[ds(t * P, P), :], orow[:, 0, NW:NW + L * H]),
                          lambda: sp.dma_start(residual[ds(t * P, P), :], orow[:, 1, 0:NW]))
            fresh_chain("chain_max0")

        best0 = s0("best0", [P, T, L * H])

        def own_and_max(score_at_, best_, heads, slope):
            chain.step(dve, lambda: dve.tensor_tensor(best_, best_, score_at_[:, :, 0:heads], ALU.add))
            chain.step(dve, lambda: dve.scalar_tensor_tensor(score_at_[:, :, heads:2 * heads], best_, slope, best_,
                                                             ALU.mult, ALU.max))

        segment_max("m0", score_src, L * H, best0)
        own_and_max(score_at, best0[:, :, :], L * H, 0.01)
        chain.dma(sp, lambda: sp.dma_start(per_block(score_dst[0:NP, :]), score_at[:, :, :]))
        fresh_chain("chain_pass0")
        stack0.close()
        edge_pass("e0", L * D, L * H, slope=0.01, tab=table, tab_dst=score_dst)

        with ExitStack() as local:
            lsb = maker(local, "sb")
            sg = lsb("sg", [P, GT, AW])
            rg = lsb("rg", [P, GT, L * D])
            xg = lsb("xg0", [P, GT, D])
            tg = lsb("tg0", [P, GT, D])
            stat = lsb("stat0", [P, 2, GT])
            with chain.loop(NG, 200) as g:
                blk = lambda d: per_block(d)[:, ds(g * GT, GT), :]
                chain.dma(sp, lambda: sp.dma_start(sg[:, :, :], blk(summed)),
                          lambda: sp.dma_start(rg[:, :, :], blk(residual)),
                          lambda: sp.dma_start(xg[:, :, :], blk(x_dram)))
                den = sg[:, :, L * D:AW]
                chain.step(dve, lambda: dve.tensor_scalar(den, den, 1e-16, None, ALU.max))
                chain.step(dve, lambda: dve.reciprocal(den, den))
                s4 = sg[:, :, 0:L * D].rearrange("p b (h d) -> p b h d", d=DH)
                for b in range(GT):
                    chain.step(dve, lambda: dve.tensor_tensor(s4[:, b, :, :], s4[:, b, :, :],
                                                              den[:, b, :].unsqueeze(2).broadcast_to([P, L * H, DH]), ALU.mult))
                chain.step(dve, lambda: dve.tensor_tensor(rg[:, :, :], rg[:, :, :], sg[:, :, 0:L * D], ALU.add))
                part = [rg[:, :, l * D:(l + 1) * D] for l in range(L)]
                chain.step(dve, lambda: dve.scalar_tensor_tensor(xg[:, :, :], part[0], 0.0, xg[:, :, :], ALU.max, ALU.add))
                chain.step(act, lambda: act.activation(part[1], part[1], ACT.Tanh))
                chain.step(dve, lambda: dve.tensor_tensor(xg[:, :, :], xg[:, :, :], part[1], ALU.add))
                elu(part[2], tg[:, :, :], part[0])
                chain.step(dve, lambda: dve.tensor_tensor(xg[:, :, :], xg[:, :, :], part[0], ALU.add))
                chain.dma(sp, lambda: sp.dma_start(blk(x_dram), xg[:, :, :]))
                layer_norm(xg[:, :, :], tg[:, :, :], stat, part[0], relu=True)
                chain.dma(sp, lambda: sp.dma_start(blk(h_dram), tg[:, :, :]))
            fresh_chain("chain_l1")

        def load_wT(lsb, name, dram, rows_, cols_):
            v = lsb(name, [P, rows_ // P, cols_])
            return v, lambda: sp.dma_start(v[:, :, :], dram.rearrange("(c p) n -> p c n", p=P))

        def broadcast(lsb, name, dram):
            v = lsb(name, [P, dram.shape[0]])
            return v, lambda: sp.dma_start(v[:, :], dram.partition_broadcast(P))

        def column(lsb, name, dram):
            n = dram.shape[0] // P
            v = lsb(name, [P, n])
            return v, lambda: sp.dma_start(v[:, :], dram.rearrange("(c p) -> p c", p=P), allow_slow_non_contiguous=True)

        with ExitStack() as local:
            lsb, lps = maker(local, "sb"), maker(local, "ps")
            gw, ld = load_wT(lsb, "gw", a["L1_gnn_gat_w"], D, D)
            att = lsb("att1", [P, 2, D])
            prod = lsb("prod1", [P, D])
            ws = lsb("ws1", [P, 2, 2 * H])
            hg = lsb("hg1", [P, GT, D])
            hgT = lsb("hgT1", [P, 2, GT, P])
            og = lsb("og1", [P, GT, D + H])
            sc1 = lsb("score_at1", [P, T, 2 * H])
            best1 = lsb("best1", [P, T, H])
            key = lsb("key", [P, T])
            chain.dma(sp, ld, *[lambda k=k, v=v: sp.dma_start(att[:, k, :], v.rearrange("h d -> (h d)").partition_broadcast(P))
                                for k, v in enumerate((a["L1_gnn_gat_a_src"], a["L1_gnn_gat_a_tgt"]))])
            for k in range(2):
                for c in range(2):
                    chain.step(dve, lambda: dve.tensor_tensor(prod[:, :], gw[:, c, :], att[:, k, :], ALU.mult))
                    chain.step(dve, lambda: dve.tensor_reduce(ws[:, c, k * H:(k + 1) * H],
                                                              prod[:, :].rearrange("p (h d) -> p h d", d=DH), AX, ALU.add))
            table1 = at(table, 0, [[D + H, ROWS], [1, D + H]])
            src1 = at(score_src, 0, [[H, ROWS], [1, H]])
            dst1 = at(score_dst, 0, [[2 * H, ROWS], [1, 2 * H]])
            chain.dma(sp, lambda: sp.dma_start(table1[NP:ROWS, :], zeros[:, 0:D + H]),
                      lambda: sp.dma_start(src1[NP:ROWS, :], zeros[:, 0:H]),
                      lambda: sp.dma_start(dst1[NP:ROWS, :], zeros[:, 0:2 * H]))
            with ExitStack() as inner:
                ips = maker(inner, "ps")
                turn = ips("turn1", [P, 2, 2, P])
                pr_ps = ips("pr_ps", [P, 4, 512])
                sc_ps = ips("sc_ps1", [P, GT, 2 * H])
                with chain.loop(NG, 140) as g:
                    chain.dma(sp, lambda: sp.dma_start(hg[:, :, :], per_block(h_dram)[:, ds(g * GT, GT), :]))
                    turn_group(hgT, hg, turn)
                    pr = pr_ps[:, :, :].rearrange("p b (k d) -> p (b k) d", k=2)
                    chain.step(pe, *[lambda b=b, c=c: pe.matmul(pr[:, b, :], hgT[:, c, b, :], gw[:, c, :],
                                                                start=(c == 0), stop=(c == 1)) for b in range(GT) for c in range(2)])
                    chain.step(pe, *[lambda b=b, c=c: pe.matmul(sc_ps[:, b, :], hgT[:, c, b, :], ws[:, c, :],
                                                                start=(c == 0), stop=(c == 1)) for b in range(GT) for c in range(2)])
                    chain.apart((dve, lambda: dve.tensor_copy(og[:, :, D:D + H], sc_ps[:, :, 0:H])),
                               (dve, lambda: dve.tensor_copy(sc1[:, ds(g * GT, GT), 0:H], sc_ps[:, :, H:2 * H])),
                               (act, lambda: act.activation(og[:, :, 0:D], pr[:, 0:GT, :], ACT.Copy)))
                    chain.dma(sp, lambda: sp.dma_start(per_block(table1)[:, ds(g * GT, GT), :], og[:, :, :]),
                              lambda: sp.dma_start(per_block(src1)[:, ds(g * GT, GT), :], og[:, :, D:D + H]))
                fresh_chain("chain_max1")
            segment_max("m1", src1, H, best1)
            gmax = lsb("gmax", [P, 2])
            some = lsb("some", [P, T])
            off = lsb("off", [P, T])
            val = lsb("val", [P, T, H])
            own_and_max(sc1, best1[:, :, :], H, 0.2)
            chain.step(dve, lambda: dve.tensor_scalar(some[:, :], count_in[:, :], 1.0, None, ALU.min))
            chain.step(dve, lambda: dve.tensor_scalar(off[:, :], some[:, :], -1.0, BIG, ALU.add, ALU.mult))
            bch = lambda v: v.unsqueeze(2).broadcast_to([P, T, H])
            chain.step(dve, lambda: dve.tensor_tensor(val[:, :, :], sc1[:, :, H:2 * H], bch(some[:, :]), ALU.mult))
            chain.step(dve, lambda: dve.tensor_tensor(val[:, :, :], val[:, :, :], bch(off[:, :]), ALU.add))
            chain.step(dve, lambda: dve.tensor_reduce(gmax[:, 0:1], val[:, :, :].rearrange("p t h -> p (t h)"), AX, ALU.max))
            chain.step(pool, lambda: pool.partition_all_reduce(gmax[:, 1:2], gmax[:, 0:1], P, RMAX))
            chain.step(dve, lambda: dve.tensor_scalar(sc1[:, :, H:2 * H], val[:, :, :], 0.0, gmax[:, 1:2], ALU.mult, ALU.add))
            chain.dma(sp, lambda: sp.dma_start(per_block(dst1[0:NP, :]), sc1[:, :, :]))

            noise = lsb("noise", [P, T])
            with nc.allow_non_contiguous_dma(reason="a vector by node onto the partitions"):
                chain.step(dve, lambda: dve.memset(noise[:, :], 0.0))
                chain.dma(sp, lambda: sp.dma_start(noise[:, 0:T - 1], a["node_vec"][0:(T - 1) * P].rearrange("(t p) -> p t", p=P)),
                          lambda: sp.dma_start(noise[0:TAIL, T - 1:T], a["node_vec"][(T - 1) * P:N].rearrange("(p o) -> p o", o=1)))
                chain.step(dve, lambda: dve.tensor_tensor(key[:, :], count_out[:, :], noise[:, :], ALU.add))
                padl = lsb("padl", [P, 1])
                chain.step(dve, lambda: dve.tensor_scalar(padl[:, :], lane[:, :], float(TAIL), BIG, ALU.is_ge, ALU.mult))
                chain.step(dve, lambda: dve.tensor_tensor(key[:, T - 1:T], key[:, T - 1:T], padl[:, :], ALU.add))
                chain.dma(sp, lambda: sp.dma_start(key_row.rearrange("(t p) -> p t", p=P), key[:, :]))
            fresh_chain("chain_rank")
            with ExitStack() as inner:
                isb = maker(inner, "sb")
                keys = isb("keys", [P, NP])
                junk = isb("junk", [P, NP], BF16)
                eq = isb("eq", [P, P])
                tri_low = isb("tri_low", [P, P])
                parts = isb("parts", [P, T, 4])
                rank_f = isb("rank_f", [P, T])
                chain.dma(sp, lambda: sp.dma_start(keys[:, :], key_row.partition_broadcast(P)))
                chain.step(dve, lambda: dve.memset(parts[:, :, :], 0.0))
                chain.step(dve, lambda: dve.tensor_scalar(tri_low[:, :], iota[:, :], lane[:, 0:1], None, ALU.is_lt))
                for t in range(T):
                    own = key[:, t:t + 1]
                    if t:
                        chain.step(dve, lambda: dve.tensor_scalar(junk[:, 0:t * P], keys[:, 0:t * P], own, None, ALU.is_le,
                                                                  ALU.add, accum_out=parts[:, t, 0:1]))
                    chain.step(dve, lambda: dve.tensor_scalar(junk[:, t * P:NP], keys[:, t * P:NP], own, None, ALU.is_lt,
                                                              ALU.add, accum_out=parts[:, t, 1:2]))
                    chain.step(dve, lambda: dve.scalar_tensor_tensor(eq[:, :], keys[:, t * P:(t + 1) * P], own, tri_low[:, :],
                                                                     ALU.is_equal, ALU.mult, accum_out=parts[:, t, 2:3]))
                chain.step(dve, lambda: dve.tensor_reduce(rank_f[:, :], parts[:, :, :], AX, ALU.add))
                chain.step(dve, lambda: dve.tensor_copy(rank_i[:, :], rank_f[:, :]))
                fresh_chain("chain_pass1")
        edge_pass("e1", D, H, slope=0.2, tab=table1, tab_dst=dst1)

        fresh_chain("chain_sort")
        with ExitStack() as local:
            lsb = maker(local, "sb")
            every_h = lsb("every_h", [P, T, D])
            chain.dma(sp, lambda: sp.dma_start(every_h[:, :, :], per_block(h_dram[0:NP, :])))
            chain.gathers(pool, [lambda t=t: pool.indirect_dma_start(
                sorted_h, bass.IndirectOffsetOnAxis(rank_i[:, t:t + 1], 0), every_h[:, t, :], None) for t in range(T)],
                sem("placed"), 16 * T)
            fresh_chain("chain_time")
        with ExitStack() as local:
            lsb, lps = maker(local, "sb"), maker(local, "ps")
            win, ld1 = load_wT(lsb, "win", a["L1_gnn_in_proj_w"], D, 2 * D)
            wx, ld2 = load_wT(lsb, "wx", a["L1_gnn_x_proj_w"], D, 3 * DS)
            wo, ld3 = load_wT(lsb, "wo", a["L1_gnn_out_proj_w"], D, D)
            cb, ld4 = column(lsb, "cb", a["L1_gnn_conv_b"])
            db, ld5 = column(lsb, "db", a["L1_gnn_dt_proj_b"])
            dp, ld6 = column(lsb, "dp", a["L1_gnn_D_param"])
            cw = lsb("cw", [P, 2, 4])
            al = lsb("al", [P, 2, DS])
            wdt = lsb("wdt", [DS, D])
            ld7 = lambda: sp.dma_start(cw[:, :, :], a["L1_gnn_conv_w"].rearrange("(c p) k -> p c k", p=P))
            ld8 = lambda: sp.dma_start(al[:, :, :], a["L1_gnn_A_log"].rearrange("(c p) k -> p c k", p=P))
            ld9 = lambda: sp.dma_start(wdt[:, :], a["L1_gnn_dt_proj_w"])
            chain.dma(sp, ld1, ld2, ld3, ld4, ld5, ld6, ld7, ld8, ld9)
            chain.step(act, lambda: act.activation(al[:, :, :], al[:, :, :], ACT.Exp))
            chain.step(dve, lambda: dve.tensor_scalar(al[:, :, :], al[:, :, :], -1.0, None, ALU.mult))
            pick = lsb("pick", [3 * DS, 3 * DS, P])
            chain.step(dve, lambda: dve.tensor_copy(
                pick[:, :, :], ident[0:3 * DS, 0:3 * DS].unsqueeze(2).broadcast_to([3 * DS, 3 * DS, P])))
            xg, xT = lsb("xg_t", [P, GT, D]), lsb("xT_t", [P, 2, GT, P])
            xin = lsb("xin", [P, 2, 3 + TS])
            xc, zs = lsb("xc", [P, 2, TS]), lsb("zs", [P, 2, TS])
            dbc = lsb("dbc", [3 * DS, TS])
            dt, dtx = lsb("dt", [P, 2, TS]), lsb("dtx", [P, 2, TS])
            u_, q_ = lsb("u_", [P, 2, TS]), lsb("q_", [P, 2, TS])
            decay, inp = lsb("decay", [P, 2, TS]), lsb("inp", [P, 2, TS])
            hs, prod = lsb("hs", [P, 2, TS]), lsb("prod_t", [P, 2, TS])
            state = lsb("state", [P, 2 * DS])
            bc_ps = lps("bc_ps", [P, 4, 512])
            y_ps = lps("y_ps", [P, 4, 512])
            turn = y_ps[:, 0, :].rearrange("p (c k n) -> p c k n", c=2, k=2)
            halves = lambda v: v.rearrange("p (k n) -> p k n", n=HS)
            s_bc, s_decay, s_inp, s_scan, s_prod, s_y, s_state = (
                sem(f"t_{n}") for n in ("bc", "decay", "inp", "scan", "prod", "y", "state"))
            K = 2 * DS
            chain.apart((dve, lambda: dve.memset(xin[:, :, 0:3], 0.0)), (dve, lambda: dve.memset(state[:, :], 0.0)))
            chain.wait(dve)
            dve.sem_inc(s_prod, 1), dve.sem_inc(s_inp, 1), dve.sem_inc(s_scan, 2), dve.sem_inc(s_y, 2)
            dve.sem_inc(s_state, 2)
            with chain.loop(NG, 140) as g:
                chain.dma(sp, lambda: sp.dma_start(xg[:, :, :], per_block(sorted_h)[:, ds(g * GT, GT), :]))
                turn_group(xT, xg, turn)
                xT2 = xT[:, :, :, :].rearrange("p c b n -> p c (b n)")
                for j in range(4):
                    o = y_ps[:, 0:2, 0:HS]
                    chain.step(pe, *[lambda c=c, z=z: pe.matmul(o[:, z, :], win[:, c, j * P:(j + 1) * P],
                                                                xT2[:, c, z * HS:(z + 1) * HS], start=(c == 0), stop=(c == 1))
                                     for z in range(2) for c in range(2)])
                    to = xin[:, j, 3:3 + TS] if j < 2 else zs[:, j - 2, :]
                    chain.step(act, lambda: act.activation(halves(to), o, ACT.Copy if j < 2 else ACT.Silu))
                for c in range(2):
                    chain.step(dve, lambda: dve.tensor_scalar(xc[:, c, :], xin[:, c, 0:TS], cw[:, c, 0:1], cb[:, c:c + 1],
                                                              ALU.mult, ALU.add))
                    for k in range(1, 4):
                        chain.step(dve, lambda: dve.scalar_tensor_tensor(xc[:, c, :], xin[:, c, k:k + TS], cw[:, c, k:k + 1],
                                                                         xc[:, c, :], ALU.mult, ALU.add))
                chain.step(act, lambda: act.activation(xc[:, :, :], xc[:, :, :], ACT.Silu))
                chain.step(dve, lambda: dve.tensor_copy(u_[:, :, 0:3], xin[:, :, TS:TS + 3]))
                chain.step(dve, lambda: dve.tensor_copy(xin[:, :, 0:3], u_[:, :, 0:3]))
                chain.step(pe, *[lambda c=c, z=z: pe.matmul(y_ps[0:3 * DS, z, 0:HS], wx[:, c, :], xc[:, c, z * HS:(z + 1) * HS],
                                                            start=(c == 0), stop=(c == 1)) for z in range(2) for c in range(2)])
                chain.step(act, lambda: act.activation(halves(dbc[:, :]), y_ps[0:3 * DS, 0:2, 0:HS], ACT.Copy))
                for c in range(2):
                    chain.step(pe, *[lambda z=z: pe.matmul(y_ps[:, z, 0:HS], wdt[:, c * P:(c + 1) * P],
                                                           dbc[0:DS, z * HS:(z + 1) * HS], start=True, stop=True) for z in range(2)])
                    chain.step(act, lambda: act.activation(halves(dt[:, c, :]), y_ps[:, 0:2, 0:HS], ACT.Identity,
                                                           bias=db[:, c:c + 1]))
                chain.step(act, lambda: act.activation(u_[:, :, :], dt[:, :, :], ACT.Abs))
                chain.step(act, lambda: act.activation(u_[:, :, :], u_[:, :, :], ACT.Exp, scale=-1.0))
                chain.step(dve, lambda: dve.tensor_scalar(q_[:, :, :], u_[:, :, :], 2.0, None, ALU.add))
                chain.step(dve, lambda: dve.reciprocal(q_[:, :, :], q_[:, :, :]))
                chain.step(dve, lambda: dve.tensor_tensor(u_[:, :, :], u_[:, :, :], q_[:, :, :], ALU.mult))
                chain.step(act, lambda: act.activation(q_[:, :, :], u_[:, :, :], ACT.Square))
                chain.step(dve, lambda: dve.tensor_scalar(dtx[:, :, :], q_[:, :, :], 1.0 / 13, None, ALU.mult))
                for k in (11, 9, 7, 5, 3):
                    chain.step(dve, lambda: dve.scalar_tensor_tensor(dtx[:, :, :], dtx[:, :, :], 1.0 / k, q_[:, :, :],
                                                                     ALU.add, ALU.mult))
                chain.step(dve, lambda: dve.scalar_tensor_tensor(dtx[:, :, :], dtx[:, :, :], 1.0, u_[:, :, :], ALU.add, ALU.mult))
                chain.step(dve, lambda: dve.tensor_scalar(dt[:, :, :], dt[:, :, :], 0.0, None, ALU.max))
                chain.step(dve, lambda: dve.scalar_tensor_tensor(dt[:, :, :], dtx[:, :, :], 2.0, dt[:, :, :], ALU.mult, ALU.add))
                chain.step(dve, lambda: dve.tensor_tensor(dtx[:, :, :], dt[:, :, :], xc[:, :, :], ALU.mult))
                for e in (pe, act, dve):
                    chain.wait(e)

                def bcast(n, which):
                    pe.wait_ge(s_inp if which == 0 else s_prod, g * K + 2 * n + 1)
                    for z in range(2):
                        mm = pe.matmul(bc_ps[:, 2 * which + z, 0:HS], pick[:, DS * (1 + which) + n, :],
                                       dbc[:, z * HS:(z + 1) * HS], start=True, stop=True)
                    mm.then_inc(s_bc, 1)

                def add_up(k):
                    c = k % 2
                    pe.wait_ge(s_prod, g * K + k + 2)
                    for z in range(2):
                        mm = pe.matmul(y_ps[:, 2 * c + z, 0:HS], ident[:, :], prod[:, c, z * HS:(z + 1) * HS],
                                       start=(k < 2), stop=(k >= K - 2))
                    mm.then_inc(s_y, 1)

                for n in range(DS):
                    bcast(n, 0)
                    bcast(n, 1)
                    if n:
                        add_up(2 * n - 2)
                        add_up(2 * n - 1)
                add_up(K - 2)
                add_up(K - 1)
                for k in range(K):
                    n, c = k // 2, k % 2
                    act.wait_ge(s_scan, g * K + k + 1)
                    act.activation(decay[:, c, :], dt[:, c, :], ACT.Exp, scale=al[:, c, n:n + 1]).then_inc(s_decay, 1)
                    if k:
                        m = k - 1
                        act.wait_ge(s_scan, g * K + m + 3)
                        act.activation(state[:, m:m + 1], hs[:, m % 2, TS - 1:TS], ACT.Copy).then_inc(s_state, 1)
                act.wait_ge(s_scan, g * K + K + 2)
                act.activation(state[:, K - 1:K], hs[:, (K - 1) % 2, TS - 1:TS], ACT.Copy).then_inc(s_state, 1)

                def make_input(k):
                    n, c = k // 2, k % 2
                    dve.wait_ge(s_bc, g * K + 2 * n + 1)
                    dve.wait_ge(s_scan, g * K + k + 1)
                    dve.tensor_tensor(halves(inp[:, c, :]), bc_ps[:, 0:2, 0:HS], halves(dtx[:, c, :]), ALU.mult).then_inc(s_inp, 1)

                def scan(k):
                    c = k % 2
                    dve.wait_ge(s_inp, g * K + k + 2)
                    dve.wait_ge(s_decay, g * K + k + 1)
                    dve.wait_ge(s_prod, g * K + k)
                    dve.wait_ge(s_state, g * K + k + 1)
                    dve.tensor_tensor_scan(hs[:, c, :], decay[:, c, :], inp[:, c, :], state[:, k:k + 1],
                                           ALU.mult, ALU.add).then_inc(s_scan, 1)

                def times_c(k):
                    n, c = k // 2, k % 2
                    dve.wait_ge(s_scan, g * K + k + 3)
                    dve.wait_ge(s_bc, g * K + 2 * n + 2)
                    dve.wait_ge(s_y, g * K + k + 1)
                    dve.tensor_tensor(halves(prod[:, c, :]), bc_ps[:, 2:4, 0:HS], halves(hs[:, c, :]), ALU.mult).then_inc(s_prod, 1)

                make_input(0)
                for k in range(K):
                    scan(k)
                    if k + 1 < K:
                        make_input(k + 1)
                    times_c(k)
                for e in (dve, act, pe):
                    e.wait_ge(s_y, g * K + K + 2)
                    e.wait_ge(s_state, g * K + K + 2)
                for c in range(2):
                    chain.step(dve, lambda: dve.scalar_tensor_tensor(halves(u_[:, c, :]), halves(xc[:, c, :]), dp[:, c:c + 1],
                                                                     y_ps[:, 2 * c:2 * c + 2, 0:HS], ALU.mult, ALU.add))
                chain.step(dve, lambda: dve.tensor_tensor(u_[:, :, :], u_[:, :, :], zs[:, :, :], ALU.mult))
                o2 = y_ps[:, :, :].rearrange("p b (k d) -> p (b k) d", k=2)
                chain.step(pe, *[lambda b=b, c=c: pe.matmul(o2[:, b, :], u_[:, c, b * P:(b + 1) * P], wo[:, c, :],
                                                            start=(c == 0), stop=(c == 1)) for b in range(GT) for c in range(2)])
                chain.step(act, lambda: act.activation(xg[:, :, :], o2[:, 0:GT, :], ACT.Copy))
                chain.dma(sp, lambda: sp.dma_start(per_block(sorted_y)[:, ds(g * GT, GT), :], xg[:, :, :]))
            fresh_chain("chain_merge")

        with ExitStack() as local:
            lsb, lps = maker(local, "sb"), maker(local, "ps")
            y_all = lsb("y_all", [P, T, D])
            chain.gathers(pool, [lambda t=t: pool.indirect_dma_start(
                y_all[:, t, :], None, sorted_y, bass.IndirectOffsetOnAxis(rank_i[:, t:t + 1], 0)) for t in range(T)],
                sem("returned"), 16 * T)
            names = ("gat_b", "ln_local_g", "ln_local_b", "ln_global_g", "ln_global_b", "ln2_g", "ln2_b", "ff2_b")
            vecs, loads = {}, []
            for n in names:
                vecs[n], ld = broadcast(lsb, f"v_{n}", a[f"L1_gnn_{n}"])
                loads.append(ld)
            wl, l1 = load_wT(lsb, "wl", a["L1_gnn_wl"], D, D)
            wg, l2 = load_wT(lsb, "wg", a["L1_gnn_wg"], D, D)
            f1, l3 = load_wT(lsb, "f1", a["L1_gnn_ff1_w"], D, 2 * D)
            f2, l4 = load_wT(lsb, "f2", a["L1_gnn_ff2_w"], 2 * D, D)
            fb, l5 = column(lsb, "fb", a["L1_gnn_ff1_b"])
            chain.dma(sp, *loads, l1, l2, l3, l4, l5)
            sg = lsb("sg1", [P, GT, D + H])
            hg, hl, ha = (lsb(n, [P, GT, D]) for n in ("hg2", "hl", "ha"))
            tg = lsb("tg2", [P, GT, D])
            xT, yT = (lsb(n, [P, 2, GT, P]) for n in ("hlT", "haT"))
            ffT = lsb("ffT", [P, 4, TS])
            stat = lsb("stat1", [P, 2, GT])
            turn = lps("turn2", [P, 2, 2, P])
            mm_ps = lps("mm_ps", [P, 4, 512])
            ff_ps = lps("ff_ps", [P, 2, 512])
            o_ps = mm_ps[:, :, :].rearrange("p b (k d) -> p (b k) d", k=2)
            bv = lambda n: vecs[n][:, :].unsqueeze(1).broadcast_to([P, GT, D])
            summed1 = at(summed, 0, [[D + H, SKIP * P], [1, D + H]])
            with chain.loop(NG, 260) as g:
                blk = lambda d: per_block(d[0:NP, :])[:, ds(g * GT, GT), :]
                chain.dma(sp, lambda: sp.dma_start(sg[:, :, :], blk(summed[:, 0:D + H])),
                          lambda: sp.dma_start(hg[:, :, :], blk(h_dram)))
                den = sg[:, :, D:D + H]
                chain.step(dve, lambda: dve.tensor_scalar(den, den, 1e-16, None, ALU.add))
                chain.step(dve, lambda: dve.reciprocal(den, den))
                for b in range(GT):
                    chain.step(dve, lambda: dve.tensor_tensor(
                        hl[:, b, :].rearrange("p (h d) -> p h d", d=DH), sg[:, b, 0:D].rearrange("p (h d) -> p h d", d=DH),
                        den[:, b, :].unsqueeze(2).broadcast_to([P, H, DH]), ALU.mult))
                chain.step(dve, lambda: dve.tensor_tensor(hl[:, :, :], hl[:, :, :], hg[:, :, :], ALU.add))
                chain.step(dve, lambda: dve.tensor_tensor(hl[:, :, :], hl[:, :, :], bv("gat_b"), ALU.add))
                elu(hl[:, :, :], tg[:, :, :], hl[:, :, :])
                layer_norm(hl[:, :, :], hl[:, :, :], stat, tg[:, :, :], gain=vecs["ln_local_g"][:, :], shift=vecs["ln_local_b"][:, :])
                chain.step(dve, lambda: dve.tensor_tensor(ha[:, :, :], hg[:, :, :], y_all[:, ds(g * GT, GT), :], ALU.add))
                layer_norm(ha[:, :, :], ha[:, :, :], stat, tg[:, :, :], gain=vecs["ln_global_g"][:, :], shift=vecs["ln_global_b"][:, :])
                turn_group(xT, hl, turn)
                turn_group(yT, ha, turn)
                chain.step(pe, *[lambda b=b, c=c: pe.matmul(o_ps[:, b, :], (xT, yT)[c // 2][:, c % 2, b, :],
                                                            (wl, wg)[c // 2][:, c % 2, :], start=(c == 0), stop=(c == 3))
                                 for b in range(GT) for c in range(4)])
                chain.step(act, lambda: act.activation(tg[:, :, :], o_ps[:, 0:GT, :], ACT.Sigmoid))
                chain.step(dve, lambda: dve.tensor_tensor(hl[:, :, :], hl[:, :, :], ha[:, :, :], ALU.subtract))
                chain.step(dve, lambda: dve.tensor_tensor(hl[:, :, :], hl[:, :, :], tg[:, :, :], ALU.mult))
                chain.step(dve, lambda: dve.tensor_tensor(hl[:, :, :], hl[:, :, :], ha[:, :, :], ALU.add))
                turn_group(xT, hl, turn)
                xT2 = xT[:, :, :, :].rearrange("p c b n -> p c (b n)")
                for j in range(4):
                    chain.step(pe, *[lambda c=c, z=z: pe.matmul(ff_ps[:, z, 0:HS], f1[:, c, j * P:(j + 1) * P],
                                                                xT2[:, c, z * HS:(z + 1) * HS], start=(c == 0), stop=(c == 1))
                                     for z in range(2) for c in range(2)])
                    chain.step(act, lambda: act.activation(ffT[:, j, :].rearrange("p (k n) -> p k n", n=HS), ff_ps[:, :, 0:HS],
                                                           ACT.Relu, bias=fb[:, j:j + 1]))
                chain.step(pe, *[lambda b=b, j=j: pe.matmul(o_ps[:, b, :], ffT[:, j, b * P:(b + 1) * P], f2[:, j, :],
                                                            start=(j == 0), stop=(j == 3)) for b in range(GT) for j in range(4)])
                chain.step(dve, lambda: dve.tensor_tensor(hl[:, :, :], hl[:, :, :], o_ps[:, 0:GT, :], ALU.add))
                chain.step(dve, lambda: dve.tensor_tensor(hl[:, :, :], hl[:, :, :], bv("ff2_b"), ALU.add))
                layer_norm(hl[:, :, :], hl[:, :, :], stat, tg[:, :, :], gain=vecs["ln2_g"][:, :], shift=vecs["ln2_b"][:, :])
                chain.dma(sp, lambda: sp.dma_start(ha[:, :, :], blk(x_dram)))
                chain.step(dve, lambda: dve.tensor_tensor(ha[:, :, :], ha[:, :, :], hl[:, :, :], ALU.add))
                chain.dma(sp, lambda: sp.dma_start(blk(x_dram), ha[:, :, :]))
                layer_norm(ha[:, :, :], hl[:, :, :], stat, tg[:, :, :], relu=True)
                chain.dma(sp, lambda: sp.dma_start(blk(h_dram), hl[:, :, :]))
            fresh_chain("chain_pass2")

        edge_pass("e2", D, weighted=True, tab=h_dram)
        finish = ExitStack()
        with finish:
            lsb, lps = maker(finish, "sb"), maker(finish, "ps")
            sg, hg, xg, tg, og = (lsb(n, [P, GT, D]) for n in ("sg_f", "hg_f", "xg_f", "tg_f", "og_f"))
            xT, yT = (lsb(n, [P, 2, GT, P]) for n in ("hT_f", "sT_f"))
            stat = lsb("stat_f", [P, 2, GT])
            w1, l1 = load_wT(lsb, "w1", a["L2_gnn_W1"], D, D)
            w2, l2 = load_wT(lsb, "w2", a["L2_gnn_W2"], D, D)
            w3, l3 = load_wT(lsb, "w3", a["L3_gnn_W"], D, D)
            w4, l4 = load_wT(lsb, "w4", a["L3_gnn_M"], D, D)
            b1, l5 = broadcast(lsb, "b1", a["L2_gnn_b1"])
            b2, l6 = broadcast(lsb, "b2", a["L2_gnn_b2"])
            turn = lps("turn3", [P, 2, 2, P])
            mm_ps = lps("mm_ps3", [P, 4, 512])
            o_ps = mm_ps[:, :, :].rearrange("p b (k d) -> p (b k) d", k=2)
            chain.dma(sp, l1, l2, l3, l4, l5, l6)
            chain.step(dve, lambda: dve.tensor_tensor(b1[:, :], b1[:, :], b2[:, :], ALU.add))

            def load_and_multiply(g, wa, wb, interact):
                blk = lambda d: per_block(d[0:NP, :])[:, ds(g * GT, GT), :]
                chain.dma(sp, lambda: sp.dma_start(sg[:, :, :], blk(summed[:, 0:D])),
                          lambda: sp.dma_start(hg[:, :, :], blk(h_dram)),
                          lambda: sp.dma_start(xg[:, :, :], blk(x_dram)))
                if interact:
                    chain.step(dve, lambda: dve.scalar_tensor_tensor(sg[:, :, :], hg[:, :, :], 1.0, sg[:, :, :], ALU.add, ALU.mult))
                turn_group(xT, hg, turn)
                turn_group(yT, sg, turn)
                chain.step(pe, *[lambda b=b, c=c: pe.matmul(o_ps[:, b, :], (xT, yT)[c // 2][:, c % 2, b, :],
                                                            (wa, wb)[c // 2][:, c % 2, :], start=(c == 0), stop=(c == 3))
                                 for b in range(GT) for c in range(4)])

            with chain.loop(NG, 160) as g:
                blk = lambda d: per_block(d[0:NP, :])[:, ds(g * GT, GT), :]
                load_and_multiply(g, w1, w2, True)
                norm = stat[:, 0, 0:GT]
                chain.step(dve, lambda: dve.tensor_tensor(og[:, :, :], o_ps[:, 0:GT, :],
                                                          b1[:, :].unsqueeze(1).broadcast_to([P, GT, D]), ALU.add))
                chain.step(dve, lambda: dve.scalar_tensor_tensor(og[:, :, :], og[:, :, :], 0.2, og[:, :, :], ALU.mult, ALU.max))
                chain.step(act, lambda: act.activation(tg[:, :, :], og[:, :, :], ACT.Square))
                chain.step(dve, lambda: dve.tensor_reduce(norm, tg[:, :, :], AX, ALU.add))
                chain.step(act, lambda: act.activation(norm, norm, ACT.Sqrt))
                chain.step(dve, lambda: dve.tensor_scalar(norm, norm, 1e-12, None, ALU.max))
                chain.step(dve, lambda: dve.reciprocal(norm, norm))
                chain.step(dve, lambda: dve.tensor_tensor(og[:, :, :], og[:, :, :], norm.unsqueeze(2).broadcast_to([P, GT, D]), ALU.mult))
                chain.step(dve, lambda: dve.tensor_tensor(xg[:, :, :], xg[:, :, :], og[:, :, :], ALU.add))
                chain.dma(sp, lambda: sp.dma_start(blk(x_dram), xg[:, :, :]))
                layer_norm(xg[:, :, :], og[:, :, :], stat, tg[:, :, :], relu=True)
                chain.dma(sp, lambda: sp.dma_start(blk(h_dram), og[:, :, :]))
            fresh_chain("chain_pass3")
            edge_pass("e3", D, tab=h_dram)

            def last(g):
                load_and_multiply(g, w3, w4, False)
                chain.step(dve, lambda: dve.scalar_tensor_tensor(xg[:, :, :], o_ps[:, 0:GT, :], 0.0, xg[:, :, :], ALU.max, ALU.add))

            with chain.loop(NG - 1, 100) as g:
                last(g)
                chain.dma(sp, lambda: sp.dma_start(out[0:(T - 1) * P, :].rearrange("(t p) c -> p t c", p=P)[:, ds(g * GT, GT), :],
                                                   xg[:, :, :]))
            last(NG - 1)
            done = (NG - 1) * GT * P
            chain.dma(sp, lambda: sp.dma_start(out[done:(T - 1) * P, :].rearrange("(t p) c -> p t c", p=P), xg[:, 0:GT - 1, :]),
                      lambda: sp.dma_start(out[(T - 1) * P:N, :], xg[0:TAIL, GT - 1, :]))
            chain.wait(sp)


_TURNED = {"L1_gnn_gat_w", "L1_gnn_in_proj_w", "L1_gnn_x_proj_w", "L1_gnn_dt_proj_w", "L1_gnn_out_proj_w",
           "L1_gnn_wl", "L1_gnn_wg", "L1_gnn_ff1_w", "L1_gnn_ff2_w", "L2_gnn_W1", "L2_gnn_W2"}


def kernel(**inputs):
    import numpy as _np
    import concourse.bacc as _bacc
    from concourse import mybir as _mybir
    from concourse.bass_utils import run_bass_kernel_spmd as _run

    nc = _bacc.Bacc("TRN2", target_bir_lowering=False, num_devices=1)
    arrays, args = {}, {}
    for name, given in inputs.items():
        v = _np.asarray(given)
        v = _np.ascontiguousarray(v.T if name in _TURNED else v)
        arrays[f"in_{name}"] = v
        args[name] = nc.dram_tensor(f"in_{name}", v.shape, _mybir.dt.from_np(v.dtype), kind="ExternalInput").ap()
    out = nc.dram_tensor("out_0", [N, D], _mybir.dt.float32, kind="ExternalOutput").ap()
    graph_stack_kernel(nc, args, out)
    result = _run(nc, [arrays], core_ids=[0])
    return result.results[0]["out_0"]
```

```python
from contextlib import ExitStack, contextmanager

import concourse.bass as bass
from concourse import mybir

F32 = mybir.dt.float32
BF16 = mybir.dt.bfloat16
I32 = mybir.dt.int32
ALU = mybir.AluOpType
ACT = mybir.ActivationFunctionType
AX = mybir.AxisListType.X
ENG = mybir.EngineType
RMAX = bass.bass_isa.ReduceOp.max

P = 128
N, D, E = 6250, 256, 106250
T = -(-N // P)
NP = T * P
TAIL = N - (T - 1) * P
STAGGER = 2
LANES = 4
GT = 7
NG = T // GT
SHARES = ((0, 2), (2, 2), (4, 2), (6, 1))
H, DH = 4, 64
L = 3
UE = 256
UNITS = E // UE + T
UB = 8
SB = 4
UC = 512
QP = 832
QB = 8
EPAD = 1 + max(P * QP, E + UE) + 256
FRONT = 1
BIG = 1.0e30
ROWS = NP + P
AW = L * D + L * H
SKIP = T + 1
TS = GT * P
HS = TS // 2
DS = 16


NOT_POOL = (ENG.Activation, ENG.PE, ENG.DVE, ENG.SP)
ALL = (ENG.Pool, *NOT_POOL)


class Chain:

    def __init__(self, nc, sem, carrier=None, landed=None, passed=None):
        self.nc, self.sem, self.carrier, self.landed, self.passed = nc, sem, carrier, landed, passed
        self.base, self.local = 0, 0
        self.landed_base, self.landed_local = 0, 0

    def wait(self, eng):
        value = self.base + self.local
        if not isinstance(value, int) or value:
            eng.wait_ge(self.sem, value)

    def step(self, eng, *instructions):
        self.wait(eng)
        for f in instructions:
            last = f()
        last.then_inc(self.sem, 1)
        self.local += 1

    def apart(self, *pairs):
        for eng in {id(e): e for e, _ in pairs}.values():
            self.wait(eng)
            for e, f in pairs:
                if e is eng:
                    f().then_inc(self.sem, 1)
        self.local += len(pairs)

    def dma(self, eng, *instructions):
        self.wait(eng)
        for f in instructions:
            f().then_inc(self.sem, 16)
        self.local += 16 * len(instructions)

    def move(self, *dmas):
        e = self.carrier
        self.wait(e)
        if self.landed is None:
            for f in dmas:
                f(e).then_inc(self.sem, 16)
            self.local += 16 * len(dmas)
            return
        e.sem_inc(self.passed, 1)
        for f in dmas:
            f(e).then_inc(self.landed, 16)
        self.landed_local += 16 * len(dmas)
        e.wait_ge(self.landed, self.landed_base + self.landed_local)
        e.sem_inc(self.sem, 1)
        self.local += 1

    def gathers(self, pool, instructions, sem, value):
        self.wait(pool)
        for f in instructions:
            f().then_inc(sem, 16)
        pool.wait_ge(sem, value)
        pool.sem_inc(self.sem, 1)
        self.local += 1

    @contextmanager
    def loop(self, n, per, engines=ALL):
        first = self.base + self.local
        assert isinstance(first, int)
        with self.nc.Fori(0, n, engines=engines) as i:
            self.base, self.local = first + i * per, 0
            yield i
            self.close(per)
        self.base, self.local = first + n * per, 0

    def close(self, per):
        assert self.local < per, (self.local, per)
        e = self.carrier or self.nc.sync
        self.wait(e)
        e.sem_inc(self.sem, per - self.local)


def in_lanes(nc, lanes, n, per, moves, stage, last=None, shares=SHARES, engines=ALL):
    def run(i, stage):
        steps = [stage(lane, i, k, *shares[k]) for k, lane in enumerate(lanes)]
        turn = 0
        while steps:
            for s in steps[:1 + turn // STAGGER]:
                if next(s, steps) is steps:
                    steps.remove(s)
            turn += 1

    starts = [c.base + c.local for c in lanes]
    arrived = [c.landed_base + c.landed_local for c in lanes]
    with nc.Fori(0, n, engines=engines) as i:
        for c, first, there in zip(lanes, starts, arrived):
            c.base, c.local = first + i * per, 0
            c.landed_base, c.landed_local = there + i * (16 * moves), 0
        run(i, stage)
        for c in lanes:
            c.close(per)
            assert c.landed is None or c.landed_local == 16 * moves, c.landed_local
    for c, first, there in zip(lanes, starts, arrived):
        c.base, c.local = first + n * per, 0
        if c.landed is not None:
            c.landed_base, c.landed_local = there + n * 16 * moves, 0
    if last:
        run(n, last)


def at(dram, offset, pattern):
    return bass.AP(tensor=dram.tensor, offset=offset, ap=pattern)


def graph_stack_kernel(nc, a, out):
    ds = bass.ds
    sp, act, pool, dve, pe = nc.sync, nc.scalar, nc.gpsimd, nc.vector, nc.tensor

    root = ExitStack()
    with root:
        def sem(name):
            return root.enter_context(nc.semaphore(name))

        def maker(stack, kind):
            make = nc.sbuf_tensor if kind == "sb" else nc.psum_tensor
            return lambda name, shape, dt=F32: stack.enter_context(make(name, shape, dt))

        def scratch(name, shape, dt=F32):
            return nc.dram_tensor(name, shape, dt, kind="Internal").ap()

        def per_block(dram):
            return dram.rearrange("(t p) c -> p t c", p=P)

        sb = maker(root, "sb")

        src_pad = scratch("src_pad", [EPAD], I32)
        dst_pad = scratch("dst_pad", [EPAD], I32)
        w_pad = scratch("w_pad", [EPAD])
        table = scratch("table", [ROWS, AW])
        score_src = scratch("score_src", [ROWS, L * H])
        score_dst = scratch("score_dst", [ROWS, 2 * L * H])
        running = scratch("running", [P * QP, L * H])
        summed = scratch("summed", [(SKIP + 1) * P, AW])
        residual = scratch("residual", [NP, L * D])
        h_dram = scratch("h_dram", [ROWS, D])
        x_dram = scratch("x_dram", [NP, D])
        sorted_h = scratch("sorted_h", [NP, D])
        sorted_y = scratch("sorted_y", [NP, D])
        key_row = scratch("key_row", [NP])
        by_time = {n: scratch(f"scan_{n}", [P, 2, NP]) for n in ("xc", "zs", "dt", "dtx", "y")}
        bc_rows = scratch("bc_rows", [(NG + 1) * DS, 2, TS])
        rel_rows = scratch("rel_rows", [UC * UE])

        passed = sem("passed")
        chain = Chain(nc, sem("chain"))
        lanes = [Chain(nc, sem("lane_0"), sp), Chain(nc, sem("lane_1"), pool, sem("lane_1_landed"), passed),
                 Chain(nc, sem("lane_2"), sp), Chain(nc, sem("lane_3"), pool, sem("lane_3_landed"), passed)]

        def fresh_chain(name):
            for e in (sp, act, pool, dve, pe):
                for c in (chain, *lanes):
                    c.wait(e)
            nc.all_engine_barrier()
            chain.sem, chain.base, chain.local = sem(name), 0, 0

        ident = sb("ident", [P, P])
        iota = sb("iota", [P, P])
        lane = sb("lane", [P, 1])
        ones = sb("ones", [P, P])
        count_in = sb("count_in", [P, T])
        count_out = sb("count_out", [P, T])
        last_edge = sb("last_edge", [P, T], I32)
        unit_src = sb("unit_src", [P, UC, 2], I32)
        unit_rel = sb("unit_rel", [P, UC, 2])
        unit_w = sb("unit_w", [P, UC, 2])
        unit_keep = sb("unit_keep", [P, UC])
        unit_block = sb("unit_block", [1, UC], I32)
        unit_at = sb("unit_at", [1, UC], I32)
        rank_i = sb("rank_i", [P, T], I32)

        zeros = sb("zeros", [P, AW])
        chain.apart((pool, lambda: pool.iota(iota[:, :], [[1, P]], base=0, channel_multiplier=0,
                                            allow_small_or_imprecise_dtypes=True)),
                   (pool, lambda: pool.iota(lane[:, :], [[0, 1]], base=0, channel_multiplier=1,
                                            allow_small_or_imprecise_dtypes=True)),
                   (dve, lambda: dve.memset(ones[:, :], 1.0)),
                   (dve, lambda: dve.memset(zeros[:, :], 0.0)))
        chain.step(dve, lambda: dve.tensor_scalar(ident[:, :], iota[:, :], lane[:, 0:1], None, ALU.is_equal))

        with ExitStack() as local:
            lsb = maker(local, "sb")
            tail = EPAD - FRONT - E
            pad_i = lsb("pad_i", [1, tail], I32)
            pad_front = lsb("pad_front", [1, 2], I32)
            chain.apart((dve, lambda: dve.memset(pad_i[:, :], NP)),
                       (dve, lambda: dve.memset(pad_front[:, :], -1)))
            row = lambda v: v.rearrange("(o n) -> o n", o=1)
            copies = []
            for pad, given in ((src_pad, a["src"]), (dst_pad, a["dst"]), (w_pad, a["edge_weight"])):
                copies.append(lambda pad=pad, given=given: sp.dma_start(
                    pad[FRONT:FRONT + E].rearrange("(q n) -> q n", q=125), given.rearrange("(q n) -> q n", q=125)))
            for pad in (src_pad, dst_pad):
                copies.append(lambda pad=pad: sp.dma_start(row(pad[FRONT + E:EPAD]), pad_i[:, :]))
                copies.append(lambda pad=pad: sp.dma_start(row(pad[0:FRONT]), pad_front[:, 0:1]))
            copies.append(lambda: sp.dma_start(row(w_pad[FRONT + E:EPAD]), zeros[0:1, 0:tail]))
            copies.append(lambda: sp.dma_start(row(w_pad[0:FRONT]), zeros[0:1, 0:1]))
            for t in range(T + 1):
                copies.append(lambda t=t: sp.dma_start(summed[t * P:(t + 1) * P, :], zeros[:, :]))
            for d in (table, score_src, score_dst, h_dram):
                copies.append(lambda d=d: sp.dma_start(d[NP:ROWS, :], zeros[:, 0:d.shape[1]]))
            chain.dma(sp, *copies)
            fresh_chain("chain_setup")

        def count_nodes(name, pad, count):
            with ExitStack() as local:
                lsb, lps = maker(local, "sb"), maker(local, "ps")
                low = lsb(f"low_{name}", [P, QP])
                high = lsb(f"high_{name}", [P, QP])
                raw = lsb(f"raw_{name}", [P, QP], I32)
                part = lsb(f"part_{name}", [P, QP], I32)
                hot_low = lsb(f"hot_low_{name}", [P, 2, QB, P], BF16)
                hot_high = lsb(f"hot_high_{name}", [P, 2, QB, T], BF16)
                hot_zero = lsb(f"hot_zero_{name}", [P, P], BF16)
                counts = lps(f"counts_{name}", [P, T])
                made, summed_up = sem(f"made_{name}"), sem(f"summed_up_{name}")
                chain.step(dve, lambda: dve.memset(hot_zero[:, :], 0.0))
                chain.dma(sp, lambda: sp.dma_start(raw[:, :], pad[FRONT:FRONT + P * QP].rearrange("(p j) -> p j", j=QP)))
                chain.step(dve, lambda: dve.tensor_scalar(part[:, :], raw[:, :], P - 1, None, ALU.bitwise_and))
                chain.step(dve, lambda: dve.tensor_copy(low[:, :], part[:, :]))
                chain.step(dve, lambda: dve.tensor_scalar(part[:, :], raw[:, :], 7, None, ALU.logical_shift_right))
                chain.step(dve, lambda: dve.tensor_copy(high[:, :], part[:, :]))
                chain.step(pe, lambda: pe.matmul(counts[:, :], hot_zero[:, :], hot_zero[:, 0:T], start=True, stop=False,
                                                 skip_group_check=True))
                chain.wait(dve)
                pe.sem_inc(summed_up, 2)
                groups = QP // QB
                with dve.Fori(0, groups // 2) as i:
                    for b in range(2):
                        dve.wait_ge(summed_up, 2 * i + b + 1)
                        for hot, of, width in ((hot_low, low, P), (hot_high, high, T)):
                            dve.tensor_tensor(
                                hot[:, b, :, :],
                                iota[:, 0:width].unsqueeze(1).broadcast_to([P, QB, width]),
                                of[:, ds((2 * i + b) * QB, QB)].unsqueeze(2).broadcast_to([P, QB, width]),
                                ALU.is_equal).then_inc(made, 1)
                with pe.Fori(0, groups // 2) as i:
                    for b in range(2):
                        pe.wait_ge(made, 2 * (2 * i + b) + 2)
                        for k in range(QB):
                            mm = pe.matmul(counts[:, :], hot_low[:, b, k, :], hot_high[:, b, k, :],
                                           start=False, stop=False, skip_group_check=True)
                        mm.then_inc(summed_up, 1)
                dve.wait_ge(summed_up, groups + 2)
                chain.step(dve, lambda: dve.tensor_copy(count[:, :], counts[:, :]))
                for e in (sp, pe, dve):
                    chain.wait(e)

        def rank_nodes():
            with ExitStack() as local:
                lsb = maker(local, "sb")
                key = lsb("key", [P, T])
                noise = lsb("noise", [P, T])
                with nc.allow_non_contiguous_dma(reason="a vector by node onto the partitions"):
                    chain.step(dve, lambda: dve.memset(noise[:, :], 0.0))
                    chain.dma(sp, lambda: sp.dma_start(noise[:, 0:T - 1], a["node_vec"][0:(T - 1) * P].rearrange("(t p) -> p t", p=P)),
                              lambda: sp.dma_start(noise[0:TAIL, T - 1:T], a["node_vec"][(T - 1) * P:N].rearrange("(p o) -> p o", o=1)))
                    chain.step(dve, lambda: dve.tensor_tensor(key[:, :], count_out[:, :], noise[:, :], ALU.add))
                    padl = lsb("padl", [P, 1])
                    chain.step(dve, lambda: dve.tensor_scalar(padl[:, :], lane[:, :], float(TAIL), BIG, ALU.is_ge, ALU.mult))
                    chain.step(dve, lambda: dve.tensor_tensor(key[:, T - 1:T], key[:, T - 1:T], padl[:, :], ALU.add))
                    chain.dma(sp, lambda: sp.dma_start(key_row.rearrange("(t p) -> p t", p=P), key[:, :]))
                keys = lsb("keys", [P, NP])
                junk = lsb("junk", [P, NP], BF16)
                eq = lsb("eq", [P, P])
                tri_low = lsb("tri_low", [P, P])
                parts = lsb("parts", [P, T, 4])
                rank_f = lsb("rank_f", [P, T])
                chain.dma(sp, lambda: sp.dma_start(keys[:, :], key_row.partition_broadcast(P)))
                chain.step(dve, lambda: dve.memset(parts[:, :, :], 0.0))
                chain.step(dve, lambda: dve.tensor_scalar(tri_low[:, :], iota[:, :], lane[:, 0:1], None, ALU.is_lt))
                for t in range(T):
                    own = key[:, t:t + 1]
                    if t:
                        chain.step(dve, lambda: dve.tensor_scalar(junk[:, 0:t * P], keys[:, 0:t * P], own, None, ALU.is_le,
                                                                  ALU.add, accum_out=parts[:, t, 0:1]))
                    chain.step(dve, lambda: dve.tensor_scalar(junk[:, t * P:NP], keys[:, t * P:NP], own, None, ALU.is_lt,
                                                              ALU.add, accum_out=parts[:, t, 1:2]))
                    chain.step(dve, lambda: dve.scalar_tensor_tensor(eq[:, :], keys[:, t * P:(t + 1) * P], own, tri_low[:, :],
                                                                     ALU.is_equal, ALU.mult, accum_out=parts[:, t, 2:3]))
                chain.step(dve, lambda: dve.tensor_reduce(rank_f[:, :], parts[:, :, :], AX, ALU.add))
                chain.step(dve, lambda: dve.tensor_copy(rank_i[:, :], rank_f[:, :]))
                for e in (sp, dve):
                    chain.wait(e)

        count_nodes("dst", dst_pad, count_in)
        fresh_chain("chain_schedule")

        with ExitStack() as local:
            lsb, lps = maker(local, "sb"), maker(local, "ps")
            tri = lsb("tri", [P, P])
            per_t = lsb("per_t", [P, T])
            upto_t = lsb("upto_t", [P, T])
            units_t = lsb("units_t", [P, T])
            units_i = lsb("units_i", [P, T], I32)
            upto_u = lsb("upto_u", [P, T])
            delta = lsb("delta", [P, T])
            pair = lsb("pair", [P, 2, T])
            cols = lsb("cols", [P, 2])
            ones_t = lsb("ones_t", [P, T])
            within = lsb("within", [P, T])
            unit_no = lsb("unit_no", [P, UC])
            past = lsb("past", [P, UC])
            chunk_first = lsb("chunk_first", [P, UC // P])
            block_f = lsb("block_f", [P, UC // P])
            start_f = lsb("start_f", [P, UC // P])
            start_i = lsb("start_i", [P, UC // P], I32)
            rel0 = lsb("rel0", [P, UC // P])
            row_block = lsb("row_block", [P, UC + 1])
            finished = lsb("finished", [P, UC])
            got_i = lsb("got_i", [P, 2, UE], I32)
            got_w = lsb("got_w", [P, UE])
            got_f = lsb("got_f", [P, 2, UE])
            turned = lps("turned", [P, 8, P])
            cut = sem("units_cut")
            small = lps("small", [P, 512])
            row_ps = lps("row_ps", [P, 512])

            chain.apart((dve, lambda: dve.tensor_scalar(tri[:, :], iota[:, :], lane[:, 0:1], None, ALU.is_ge)),
                       (dve, lambda: dve.memset(ones_t[:, :], 1.0)),
                       (pool, lambda: pool.iota(unit_no[:, :], [[1, UC]], base=0, channel_multiplier=0,
                                                allow_small_or_imprecise_dtypes=True)),
                       (pool, lambda: pool.iota(chunk_first[:, :], [[P, UC // P]], base=0, channel_multiplier=1,
                                                allow_small_or_imprecise_dtypes=True)))
            chain.step(pe, lambda: pe.matmul(small[:, 0:T], ones[:, :], count_in[:, :], start=True, stop=True))
            chain.step(pe, lambda: pe.matmul(small[:, 64:64 + T], tri[:, :], count_in[:, :], start=True, stop=True))
            chain.step(dve, lambda: dve.tensor_copy(per_t[:, :], small[:, 0:T]))
            chain.step(dve, lambda: dve.tensor_tensor_scan(upto_t[:, :], ones_t[:, :], per_t[:, :], 0.0, ALU.mult, ALU.add))
            chain.step(dve, lambda: dve.tensor_tensor(within[:, :], upto_t[:, :], per_t[:, :], ALU.subtract))
            chain.step(dve, lambda: dve.tensor_tensor(within[:, :], within[:, :], small[:, 64:64 + T], ALU.add))
            chain.step(dve, lambda: dve.tensor_scalar(within[:, :], within[:, :], -1.0, 0.0, ALU.add, ALU.max))
            chain.step(dve, lambda: dve.tensor_copy(last_edge[:, :], within[:, :]))
            chain.step(dve, lambda: dve.tensor_scalar(units_t[:, :], per_t[:, :], float(UE - 1), None, ALU.add))
            chain.step(dve, lambda: dve.tensor_copy(units_i[:, :], units_t[:, :]))
            chain.step(dve, lambda: dve.tensor_scalar(units_i[:, :], units_i[:, :], 8, None, ALU.logical_shift_right))
            chain.step(dve, lambda: dve.tensor_copy(units_t[:, :], units_i[:, :]))
            chain.step(dve, lambda: dve.tensor_tensor_scan(upto_u[:, :], ones_t[:, :], units_t[:, :], 0.0, ALU.mult, ALU.add))
            chain.step(dve, lambda: dve.scalar_tensor_tensor(delta[:, :], units_t[:, :], -float(UE), per_t[:, :],
                                                             ALU.mult, ALU.add))
            for k, v in enumerate((upto_u, delta)):
                chain.step(dve, lambda: dve.tensor_tensor(pair[:, k, :], v[:, :], ident[:, 0:T], ALU.mult))
                chain.step(dve, lambda: dve.tensor_reduce(cols[:, k:k + 1], pair[:, k, :], AX, ALU.add))
            chain.step(dve, lambda: dve.tensor_scalar(past[:, :], unit_no[:, :], cols[:, 0:1], None, ALU.is_ge))
            chain.step(dve, lambda: dve.memset(cols[:, 0:1], 1.0))
            chain.step(pe, *[lambda c=c: pe.matmul(small[:, 128 + 2 * c:130 + 2 * c], past[0:T, c * P:(c + 1) * P],
                                                   cols[0:T, :], start=True, stop=True) for c in range(UC // P)])
            chain.step(pe, lambda: pe.matmul(row_ps[:, :], ones[0:T, :], past[0:T, :], start=True, stop=True))
            by_chunk = small[:, 128:128 + 2 * (UC // P)].rearrange("p (c k) -> p k c", k=2)
            chain.step(dve, lambda: dve.tensor_copy(block_f[:, :], by_chunk[:, 0, :]))
            chain.step(dve, lambda: dve.scalar_tensor_tensor(start_f[:, :], chunk_first[:, :], float(UE), by_chunk[:, 1, :],
                                                             ALU.mult, ALU.add))
            chain.step(dve, lambda: dve.tensor_scalar(start_f[:, :], start_f[:, :], float(E), float(FRONT), ALU.min, ALU.add))
            chain.step(dve, lambda: dve.tensor_copy(start_i[:, :], start_f[:, :]))
            chain.step(dve, lambda: dve.tensor_scalar(rel0[:, :], block_f[:, :], -float(P), None, ALU.mult))
            chain.apart((dve, lambda: dve.tensor_copy(row_block[:, 0:UC], row_ps[:, :])),
                       (dve, lambda: dve.memset(row_block[:, UC:UC + 1], float(T))))
            chain.step(dve, lambda: dve.memset(unit_keep[:, 0:1], 0.0))
            chain.step(dve, lambda: dve.tensor_tensor(unit_keep[:, 1:UC], row_block[:, 1:UC], row_block[:, 0:UC - 1],
                                                      ALU.is_equal))
            chain.step(dve, lambda: dve.tensor_tensor(finished[:, :], row_block[:, 1:UC + 1], row_block[:, 0:UC],
                                                      ALU.is_equal))
            chain.step(dve, lambda: dve.scalar_tensor_tensor(finished[:, :], finished[:, :], float(SKIP), row_block[:, 0:UC],
                                                             ALU.mult, ALU.add))
            chain.step(dve, lambda: dve.tensor_scalar(finished[:, :], finished[:, :], float(SKIP), None, ALU.min))
            chain.step(dve, lambda: dve.tensor_copy(unit_block[:, :], finished[0:1, :]))
            chain.step(dve, lambda: dve.tensor_copy(unit_at[:, :], row_block[0:1, 0:UC]))
            for c in range(UC // P):
                idx = bass.IndirectOffsetOnAxis(start_i[:, c:c + 1], 0)
                col = lambda v: v.rearrange("(n o) -> n o", o=1)
                chain.gathers(pool, [
                    lambda: pool.indirect_dma_start(got_i[:, 0, :], None, col(src_pad), idx),
                    lambda: pool.indirect_dma_start(got_i[:, 1, :], None, col(dst_pad), idx),
                    lambda: pool.indirect_dma_start(got_w[:, :], None, col(w_pad), idx)], cut, 3 * 16 * (c + 1))
                chain.step(dve, lambda: dve.tensor_copy(got_f[:, :, :], got_i[:, :, :]))
                chain.step(pe, *[lambda k=k, v=v, h=h: pe.transpose(turned[:, 2 * k + h, :], v[:, h * P:(h + 1) * P],
                                                                    ident[:, :])
                                 for k, v in ((0, got_f[:, 0, :]), (2, got_w)) for h in range(2)])
                to = slice(c * P, (c + 1) * P)
                chain.apart(*[(dve, lambda k=k, v=v: dve.tensor_copy(
                    v[:, to, :].rearrange("p u h -> p h u"), turned[:, 2 * k:2 * k + 2, :]))
                    for k, v in ((0, unit_src), (2, unit_w))])
                chain.step(dve, lambda: dve.tensor_scalar(got_f[:, 1, :], got_f[:, 1, :], rel0[:, c:c + 1], None, ALU.add))
                chain.dma(sp, lambda: sp.dma_start(rel_rows.rearrange("(u e) -> u e", e=UE)[to, :], got_f[:, 1, :]))
                chain.step(pe, *[lambda h=h: pe.transpose(turned[:, h, :], got_f[:, 1, h * P:(h + 1) * P], ident[:, :])
                                 for h in range(2)])
                chain.step(dve, lambda: dve.tensor_copy(unit_rel[:, to, :].rearrange("p u h -> p h u"), turned[:, 0:2, :]))
            fresh_chain("chain_first")

        def layer_norm(ch, x3, out3, stat, square, eps=1e-5, relu=False, gain=None, shift=None):
            g = x3.shape[1]
            mean, var = stat[:, 0, 0:g], stat[:, 1, 0:g]
            bc = lambda v: v.unsqueeze(2).broadcast_to([P, g, D])
            yield ch.step(dve, lambda: dve.tensor_reduce(mean, x3, AX, ALU.add))
            yield ch.step(dve, lambda: dve.tensor_scalar(mean, mean, 1.0 / D, None, ALU.mult))
            yield ch.step(dve, lambda: dve.tensor_tensor(out3, x3, bc(mean), ALU.subtract))
            yield ch.step(act, lambda: act.activation(square, out3, ACT.Square))
            yield ch.step(dve, lambda: dve.tensor_reduce(var, square, AX, ALU.add))
            yield ch.step(dve, lambda: dve.tensor_scalar(var, var, 1.0 / D, eps, ALU.mult, ALU.add))
            yield ch.step(act, lambda: act.activation(var, var, ACT.Sqrt))
            yield ch.step(dve, lambda: dve.reciprocal(var, var))
            yield ch.step(dve, lambda: dve.tensor_tensor(out3, out3, bc(var), ALU.mult))
            if gain is not None:
                yield ch.step(dve, lambda: dve.tensor_tensor(out3, out3, gain.unsqueeze(1).broadcast_to([P, g, D]), ALU.mult))
                yield ch.step(dve, lambda: dve.tensor_tensor(out3, out3, shift.unsqueeze(1).broadcast_to([P, g, D]), ALU.add))
            if relu:
                yield ch.step(act, lambda: act.activation(out3, out3, ACT.Relu))

        def turn_blocks(ch, dst4, src3, ps):
            for b in range(0, src3.shape[1], 2):
                m = min(2, src3.shape[1] - b)
                yield ch.step(pe, *[lambda k=k, c=c: pe.transpose(ps[:, c, k, :], src3[:, b + k, c * P:(c + 1) * P], ident[:, :])
                                    for k in range(m) for c in range(2)])
                yield ch.step(act, lambda: act.activation(dst4[:, :, b:b + m, :], ps[:, :, 0:m, :], ACT.Copy))

        def elu(ch, x, tmp, out):
            yield ch.step(dve, lambda: dve.tensor_scalar(tmp, x, 0.0, None, ALU.min))
            yield ch.step(act, lambda: act.activation(tmp, tmp, ACT.Exp))
            yield ch.step(dve, lambda: dve.tensor_scalar(tmp, tmp, -1.0, None, ALU.add))
            yield ch.step(dve, lambda: dve.scalar_tensor_tensor(out, x, 0.0, tmp, ALU.max, ALU.add))

        def one_by_one(steps):
            for _ in steps:
                pass

        class SegmentMax:

            def __init__(self, stack, name, scores, heads):
                lsb = maker(stack, "sb")
                self.name, self.scores, self.heads = name, scores, heads
                self.mine = lsb(f"mine_{name}", [P, QP, heads])
                self.src_q = lsb(f"src_q_{name}", [P, QP], I32)
                self.dst_q = lsb(f"dst_q_{name}", [P, QP + 1], I32)
                self.idx = lsb(f"idx_{name}", [P, 2, QB], I32)
                self.got = lsb(f"got_{name}", [P, 2, QB, heads])
                self.arrived = [sem(f"arrived_{name}{b}") for b in range(2)]
                self.picked, self.kept = sem(f"picked_{name}"), sem(f"kept_{name}")
                chain.dma(sp,
                          lambda: sp.dma_start(self.src_q[:, :], src_pad[FRONT:FRONT + P * QP].rearrange("(p j) -> p j", j=QP)),
                          lambda: sp.dma_start(self.dst_q[:, :], at(dst_pad, 0, [[QP, P], [1, QP + 1]])))
                chain.wait(pool)
                pool.sem_inc(self.kept, 2)

            def gather(self, first, count):
                def issue(n, b):
                    pool.tensor_copy(self.idx[:, b, :], self.src_q[:, ds(n * QB, QB)]).then_inc(self.picked, 1)
                    pool.wait_ge(self.picked, n + 1)
                    pool.wait_ge(self.kept, n + 1)
                    pool.sem_inc(passed, 1)
                    for k in range(QB):
                        pool.indirect_dma_start(self.got[:, b, k, :], None, self.scores,
                                                bass.IndirectOffsetOnAxis(self.idx[:, b, k:k + 1], 0)
                                                ).then_inc(self.arrived[b], 16)

                def store(n, half, b):
                    pool.wait_ge(self.arrived[b], 16 * QB * (half + 1))
                    pool.tensor_copy(self.mine[:, ds(n * QB, QB), :], self.got[:, b, :, :]).then_inc(self.kept, 1)

                h0 = first // 2
                issue(first, 0)
                with pool.Fori(0, count // 2 - 1) as i:
                    n = 2 * i + first
                    issue(n + 1, 1)
                    store(n, i + h0, 0)
                    issue(n + 2, 0)
                    store(n + 1, i + h0, 1)
                n, h = first + count - 2, h0 + count // 2 - 1
                issue(n + 1, 1)
                store(n, h, 0)
                store(n + 1, h, 1)

            def finish(self, best):
                name, heads, mine, dst_q = self.name, self.heads, self.mine, self.dst_q
                with ExitStack() as local:
                    lsb, lps = maker(local, "sb"), maker(local, "ps")
                    same = lsb(f"same_{name}", [P, QP])
                    fresh = lsb(f"fresh_{name}", [P, 1])
                    side = lsb(f"side_{name}", [P, 16])
                    side_t = lsb(f"side_t_{name}", [16, 3, P])
                    carry = lsb(f"carry_{name}", [P, 16])
                    side_ps = lps(f"side_ps_{name}", [P, 2, P])
                    dve.wait_ge(self.kept, QP // QB + 2)
                    chain.step(dve, lambda: dve.tensor_tensor(same[:, :], dst_q[:, 1:QP + 1], dst_q[:, 0:QP], ALU.not_equal))
                    chain.step(dve, lambda: dve.tensor_reduce(fresh[:, :], same[:, :], AX, ALU.max))
                    chain.step(dve, lambda: dve.tensor_scalar(same[:, :], same[:, :], -BIG, None, ALU.mult))
                    chain.apart(*[(dve, lambda h=h: dve.tensor_tensor_scan(mine[:, :, h], same[:, :], mine[:, :, h], -BIG,
                                                                           ALU.add, ALU.max)) for h in range(heads)])
                    chain.step(dve, lambda: dve.memset(side[:, :], 0.0))
                    chain.step(dve, lambda: dve.tensor_copy(side[:, 0:heads], mine[:, QP - 1, :]))
                    chain.step(pe, lambda: pe.transpose(side_ps[0:16, 0, :], side[:, :], ident[:, :]))
                    chain.step(dve, lambda: dve.tensor_copy(side_t[:, 0, :], side_ps[0:16, 0, :]))
                    chain.step(dve, lambda: dve.tensor_scalar(side[:, :], ones[:, 0:16], fresh[:, 0:1], -BIG, ALU.mult, ALU.mult))
                    chain.step(pe, lambda: pe.transpose(side_ps[0:16, 1, :], side[:, :], ident[:, :]))
                    chain.step(dve, lambda: dve.tensor_copy(side_t[:, 1, :], side_ps[0:16, 1, :]))
                    chain.step(dve, lambda: dve.memset(side_t[:, 2, 0:1], -BIG))
                    chain.step(dve, lambda: dve.tensor_tensor_scan(side_t[:, 0, :], side_t[:, 1, :], side_t[:, 0, :], -BIG,
                                                                   ALU.add, ALU.max))
                    chain.step(dve, lambda: dve.tensor_copy(side_t[:, 2, 1:P], side_t[:, 0, 0:P - 1]))
                    chain.step(pe, lambda: pe.transpose(side_ps[:, 0, 0:16], side_t[:, 2, :], ident[0:16, 0:16]))
                    chain.step(dve, lambda: dve.tensor_copy(carry[:, :], side_ps[:, 0, 0:16]))
                    chain.apart(*[(dve, lambda h=h: dve.tensor_tensor_scan(mine[:, :, h], same[:, :], mine[:, :, h],
                                                                           carry[:, h:h + 1], ALU.add, ALU.max))
                                  for h in range(heads)])
                    run = at(running, 0, [[QP * heads, P], [1, QP * heads]])
                    chain.dma(sp, lambda: sp.dma_start(run, mine[:, :, :].rearrange("p j h -> p (j h)")))
                    table_run = at(running, 0, [[heads, P * QP], [1, heads]])
                    chain.gathers(pool, [lambda t=t: pool.indirect_dma_start(
                        best[:, t, :], None, table_run, bass.IndirectOffsetOnAxis(last_edge[:, t:t + 1], 0)) for t in range(T)],
                        sem(f"read_{name}"), 16 * T)
                    for e in (sp, pe, dve):
                        chain.wait(e)

        class EdgePass:

            ROUNDS = UNITS // UB

            def __init__(self, stack, name, width, heads=0, act_heads=0, slope=0.0, weighted=False, tab=None, tab_dst=None):
                lsb, lps = maker(stack, "sb"), maker(stack, "ps")
                full = width + heads
                self.width, self.heads, self.slope, self.weighted = width, heads, slope, weighted
                self.full, self.tab, self.tab_dst = full, tab, tab_dst
                self.dve_heads = heads - act_heads
                assert UNITS % UB == 0 and UB % SB == 0
                self.rows = lsb(f"rows_{name}", [P, UB, 2, full])
                self.hot = lsb(f"hot_{name}", [P, UB, 2, P])
                self.sums = lsb(f"sums_{name}", [P, SB, full])
                self.idx = lsb(f"idx_{name}", [P, 2, UB // 2, 2], I32)
                if heads:
                    self.rel = lsb(f"rel_{name}", [P, UB, UE])
                    self.spread = lsb(f"spread_{name}", [P, UB, UE])
                    self.at_node = lsb(f"at_node_{name}", [P, UB, 2 * heads])
                    self.score = lsb(f"score_{name}", [P, UB, 2, heads])
                    self.ex = lps(f"ex_{name}", [P, 2, 512])
                self.acc = lps(f"acc_{name}", [P, 2, -(-full // 512) * 512])
                self.splits = [(a0, min(a0 + 512, full)) for a0 in range(0, full, 512)]
                self.landed = [sem(f"landed_{name}{v}") for v in range(UB)]
                self.stored = [sem(f"stored_{name}{v}") for v in range(SB)]
                self.beside = [sem(f"beside_{name}{v}") for v in range(UB)] if heads else None
                self.s_idx, self.s_spread, self.s_ex, self.s_hot, self.s_score = (
                    sem(f"{n}_{name}") for n in ("idx", "spread", "ex", "hot", "score"))
                self.s_act = sem(f"act_{name}")
                self.s_exp, self.s_mul, self.s_pe, self.s_sum = (sem(f"{n}_{name}") for n in ("exp", "mul", "pe", "sum"))
                self.lag = (1, 2, 3) if heads else (None, None, 2)
                pe.sem_inc(self.s_pe, UB)
                pe.sem_inc(self.s_ex, UB)
                dve.sem_inc(self.s_sum, 2)
                for v in range(SB):
                    sp.sem_inc(self.stored[v], 16)
                chain.step(dve, lambda: dve.memset(self.sums[:, SB - 1, :], 0.0))
                chain.wait(dve)
                if heads:
                    for v in range(UB // 2):
                        self.load_beside(0, v)

            def pool_half(self, i, half):
                v0 = half * (UB // 2)
                for v in range(v0, v0 + UB // 2):
                    pool.wait_ge(self.landed[v], 32 * i)
                pool.tensor_copy(self.idx[:, half, :, :], unit_src[:, ds(i * UB + v0, UB // 2), :]).then_inc(self.s_idx, 1)
                pool.wait_ge(self.s_idx, 2 * i + half + 1)
                for v in range(v0, v0 + UB // 2):
                    pool.wait_ge(self.s_pe, i * UB + v + 1)
                    pool.sem_inc(passed, 1)
                    for e in range(2):
                        pool.indirect_dma_start(self.rows[:, v, e, :], None, self.tab,
                                                bass.IndirectOffsetOnAxis(self.idx[:, half, v - v0, e:e + 1], 0)
                                                ).then_inc(self.landed[v], 16)

            def pool_round(self, i):
                self.pool_half(i, 0)
                self.pool_half(i, 1)

            def load_beside(self, i, v):
                u = i * UB + v
                block = sp.value_load(unit_at[0:1, ds(u, 1)], min_val=0, max_val=T)
                sp.wait_ge(self.s_ex, u + 1)
                sp.dma_start(self.rel[:, v, :], rel_rows[ds(u * UE, UE)].partition_broadcast(P)).then_inc(self.beside[v], 16)
                sp.dma_start(self.at_node[:, v, :], self.tab_dst[ds(block * P, P), :]).then_inc(self.beside[v], 16)

            def store_sums(self, i, v):
                u = i * UB + v
                block = sp.value_load(unit_block[0:1, ds(u, 1)], min_val=0, max_val=SKIP)
                sp.wait_ge(self.s_sum, u + 3)
                sp.dma_start(summed[:, 0:self.full][ds(block * P, P), :], self.sums[:, v % SB, :],
                             cond=(block < SKIP)).then_inc(self.stored[v % SB], 16)

            def sp_slot(self, i, v, first=False):
                half = UB // 2
                if self.heads:
                    self.load_beside(i if v + half < UB else i + 1, (v + half) % UB)
                if not (first and v < half):
                    self.store_sums(i if v >= half else i - 1, (v - half) % UB)

            def one_hots(self, i, v):
                u = i * UB + v
                if self.heads:
                    dve.wait_ge(self.beside[v], 32 * (i + 1))
                    dve.wait_ge(self.s_ex, u + 1)
                    dve.tensor_scalar(self.spread[:, v, :], self.rel[:, v, :], lane[:, 0:1], None,
                                      ALU.is_equal).then_inc(self.s_spread, 1)
                dve.wait_ge(self.s_pe, u + 1)
                wide = lambda w: w[:, ds(u, 1), :].rearrange("p o e -> p (o e)").unsqueeze(2).broadcast_to([P, 2, P])
                dve.tensor_tensor(self.hot[:, v, :, :], iota[:, :].unsqueeze(1).broadcast_to([P, 2, P]), wide(unit_rel),
                                  ALU.is_equal).then_inc(self.s_hot, 1)
                if self.weighted:
                    dve.wait_ge(self.s_hot, 2 * u + 1)
                    dve.tensor_tensor(self.hot[:, v, :, :], self.hot[:, v, :, :], wide(unit_w), ALU.mult).then_inc(self.s_hot, 1)

            def of_node(self, v):
                return self.ex[:, v % 2, 0:4 * self.heads].rearrange("p (e h) -> p e h", e=2)

            def scores(self, i, v):
                u, heads = i * UB + v, self.heads
                score = self.score[:, v, :, :]
                dve.wait_ge(self.landed[v], 32 * (i + 1))
                dve.wait_ge(self.s_ex, u + UB + 1)
                dve.tensor_tensor(score, self.rows[:, v, :, self.width:], self.of_node(v)[:, :, 0:heads], ALU.add).then_inc(self.s_score, 1)
                dve.wait_ge(self.s_score, 3 * u + 1)
                dve.scalar_tensor_tensor(score, score, self.slope, score, ALU.mult, ALU.max).then_inc(self.s_score, 1)
                dve.wait_ge(self.s_score, 3 * u + 2)
                dve.tensor_tensor(score, score, self.of_node(v)[:, :, heads:2 * heads], ALU.subtract).then_inc(self.s_score, 1)

            def weigh(self, i, v):
                n = self.dve_heads
                if n:
                    dve.wait_ge(self.s_exp, i * UB + v + 1)
                    r = self.rows[:, v, :, 0:n * DH].rearrange("p e (h d) -> p e h d", d=DH)
                    by = self.rows[:, v, :, self.width:self.width + n]
                    dve.tensor_tensor(r, r, by.unsqueeze(3).broadcast_to([P, 2, n, DH]), ALU.mult).then_inc(self.s_mul, 1)

            def collect(self, i, v):
                u = i * UB + v
                dve.wait_ge(self.s_pe, u + UB + 1)
                if isinstance(i, int):
                    dve.wait_ge(self.stored[v % SB], 16 * (u // SB + 1))
                else:
                    dve.wait_ge(self.stored[v % SB], 16 * (UB // SB * i + v // SB + 1))
                dve.wait_ge(self.s_sum, u + 2)
                dve.scalar_tensor_tensor(self.sums[:, v % SB, :], self.sums[:, (v - 1) % SB, :], unit_keep[:, ds(u, 1)],
                                         self.acc[:, v % 2, 0:self.full], ALU.mult, ALU.add).then_inc(self.s_sum, 1)

            def behind(self, part, lag, i, v, first):
                if lag is not None and not (first and v < lag):
                    part(i if v >= lag else i - 1, (v - lag) % UB)

            def dve_slot(self, i, v, first=False):
                self.one_hots(i, v)
                for part, lag in zip((self.scores, self.weigh, self.collect), self.lag):
                    self.behind(part, lag, i, v, first)

            def weights(self, i, v):
                act.wait_ge(self.s_score, 3 * (i * UB + v) + 3)
                act.activation(self.rows[:, v, :, self.width:], self.score[:, v, :, :], ACT.Exp).then_inc(self.s_exp, 1)

            def weigh_rest(self, i, v):
                act.wait_ge(self.s_exp, i * UB + v + 1)
                for e in range(2):
                    for h in range(self.dve_heads, self.heads):
                        r = self.rows[:, v, e, h * DH:(h + 1) * DH]
                        last = act.activation(r, r, ACT.Copy, scale=self.rows[:, v, e, self.width + h:self.width + h + 1])
                last.then_inc(self.s_act, 1)

            def act_slot(self, i, v, first=False):
                self.behind(self.weights, 1, i, v, first)
                self.behind(self.weigh_rest, 1, i, v, first)

            def spread_values(self, i, v):
                u = i * UB + v
                pe.wait_ge(self.s_spread, u + 1)
                if not isinstance(u, int) or u >= 2:
                    pe.wait_ge(self.s_score, 3 * (u - 2) + 3)
                for e in range(2):
                    mm = pe.matmul(self.of_node(v)[:, e, :], self.spread[:, v, e * P:(e + 1) * P], self.at_node[:, v, :],
                                   start=True, stop=True)
                mm.then_inc(self.s_ex, 1)

            def sum_rows(self, i, v):
                u = i * UB + v
                if self.heads:
                    pe.wait_ge(self.s_act, u + 1)
                    if self.dve_heads:
                        pe.wait_ge(self.s_mul, u + 1)
                else:
                    pe.wait_ge(self.landed[v], 32 * (i + 1))
                pe.wait_ge(self.s_hot, (2 if self.weighted else 1) * (u + 1))
                pe.wait_ge(self.s_sum, u + 1)
                for a0, a1 in self.splits:
                    for e in range(2):
                        mm = pe.matmul(self.acc[:, v % 2, a0:a1], self.hot[:, v, e, :], self.rows[:, v, e, a0:a1],
                                       start=(e == 0), stop=(e == 1))
                mm.then_inc(self.s_pe, 1)

            def pe_slot(self, i, v, first=False):
                if self.heads:
                    self.spread_values(i, v)
                self.behind(self.sum_rows, 2 if self.heads else 0, i, v, first)

            def rounds(self, first, count):
                slots = [(sp, self.sp_slot), (dve, self.dve_slot), (pe, self.pe_slot)]
                slots += [(act, self.act_slot)] if self.heads else []
                start = first
                if first == 0:
                    self.pool_round(0)
                    for e, slot in slots:
                        for v in range(UB):
                            slot(0, v, True)
                    start = 1
                if start < first + count:
                    with pool.Fori(start, first + count) as i:
                        self.pool_round(i)
                    for e, slot in slots:
                        with e.Fori(start, first + count) as i:
                            for v in range(UB):
                                slot(i, v)

            def end(self):
                n = self.ROUNDS
                for v in range(3):
                    if self.heads and v < 1:
                        self.scores(n - 1, UB - 1)
                        self.weights(n - 1, UB - 1)
                        self.weigh_rest(n - 1, UB - 1)
                    if self.heads and v < 2:
                        self.weigh(n - 1, UB - 2 + v)
                        self.sum_rows(n - 1, UB - 2 + v)
                    if v < self.lag[2]:
                        self.collect(n - 1, UB - self.lag[2] + v)
                for v in range(UB // 2):
                    self.store_sums(n - 1, UB // 2 + v)
                for v in range(SB):
                    sp.wait_ge(self.stored[v], 16 * (UNITS // SB + 1))
                nc.all_engine_barrier()

        def edge_pass(name, width, **options):
            with ExitStack() as local:
                edges = EdgePass(local, name, width, **options)
                edges.rounds(0, EdgePass.ROUNDS)
                edges.end()

        def own_and_max(score_at_, best_, heads, slope):
            chain.step(dve, lambda: dve.tensor_tensor(best_, best_, score_at_[:, :, 0:heads], ALU.add))
            chain.step(dve, lambda: dve.scalar_tensor_tensor(score_at_[:, :, heads:2 * heads], best_, slope, best_,
                                                             ALU.mult, ALU.max))

        stack0 = ExitStack()
        s0 = maker(stack0, "sb")
        hT = s0("hT", [P, 2, NP])
        score_at = s0("score_at", [P, T, 2 * L * H])
        channel = s0("channel", [P, 3, 2])
        mean, var, msq = channel[:, 0, :], channel[:, 1, :], channel[:, 2, :]
        with ExitStack() as local:
            lsb, lps = maker(local, "sb"), maker(local, "ps")
            xg = lsb("xg", [P, GT, D])
            hg = lsb("hg", [P, GT, D])
            sq = lsb("sq", [P, GT, D])
            stat = lsb("stat", [P, LANES, 2, GT])
            moments = lps("moments", [P, 2, 2])
            turn = lps("turn", [P, LANES, 2, 2, P])
            moment = lsb("moment", [P, 2, 2])
            chain.dma(sp, lambda: sp.dma_start(x_dram[0:N, :], a["x"][:, :]),
                      lambda: sp.dma_start(x_dram[N:NP, :], zeros[0:NP - N, 0:D]))
            chain.step(pe, *[lambda k=k: pe.matmul(moments[:, k, :], zeros[:, 0:P], zeros[:, 0:2], start=(k == 0), stop=False,
                                                   skip_group_check=True) for k in range(2)])
            for e in (sp, pool):
                chain.wait(e)

            def norm_stage(ch, g, k, lo, m):
                x3, h3, s3 = xg[:, lo:lo + m, :], hg[:, lo:lo + m, :], sq[:, lo:lo + m, :]
                yield ch.move(lambda e: e.dma_start(x3, per_block(x_dram)[:, ds(g * GT + lo, m), :]))
                yield from layer_norm(ch, x3, h3, stat[:, k, :, :], s3, relu=True)
                yield ch.step(act, lambda: act.activation(s3, h3, ACT.Square))
                yield ch.step(pe, *[lambda c=c, q=q, v=v, b=b: pe.matmul(
                    moments[:, c, q:q + 1], v[:, b, c * P:(c + 1) * P], ones[:, 0:1], start=False, stop=False,
                    skip_group_check=True) for q, v in enumerate((h3, s3)) for b in range(m) for c in range(2)])
                yield from turn_blocks(ch, hT[:, :, ds((g * GT + lo) * P, m * P)].rearrange("p c (b n) -> p c b n", n=P), h3,
                                       turn[:, k, :, :, :])

            in_lanes(nc, lanes, NG, 80, 1, norm_stage)
            for e in (dve, pe):
                for c in lanes:
                    c.wait(e)
            chain.step(dve, lambda: dve.tensor_scalar(moment[:, :, :], moments[:, :, :], 1.0 / N, None, ALU.mult))
            chain.step(dve, lambda: dve.tensor_copy(mean, moment[:, :, 0]))
            chain.step(dve, lambda: dve.tensor_tensor(msq, mean, mean, ALU.mult))
            chain.step(dve, lambda: dve.tensor_tensor(var, moment[:, :, 1], msq, ALU.subtract))
            chain.step(dve, lambda: dve.tensor_scalar(var, var, 0.0, 1e-5, ALU.max, ALU.add))
            chain.step(act, lambda: act.activation(var, var, ACT.Sqrt))
            chain.step(dve, lambda: dve.reciprocal(var, var))
            fresh_chain("chain_weights")
        NW = L * D
        with ExitStack() as local:
            lsb, lps = maker(local, "sb"), maker(local, "ps")
            wt = lsb("wt", [P, 2, 2, NW])
            ws = lsb("ws", [P, 2, 2 * L * H])
            wt_b = lsb("wt_b", [P, 2, NW])
            ws_b = lsb("ws_b", [P, 2 * L * H])
            with ExitStack() as inner:
                isb, ips = maker(inner, "sb"), maker(inner, "ps")
                att = isb("att", [P, 2, NW])
                prod = isb("prod", [P, NW])
                gam, bet = isb("gam", [P, 2, L]), isb("bet", [P, 2, L])
                scale, shift = isb("scale", [P, 2, L]), isb("shift", [P, 2, L])
                shift_w = isb("shift_w", [P, 2, L, P])
                bias_ps = ips("bias_ps", [P, 2, 512])
                loads = []
                for l in range(L):
                    for k, w in enumerate((a["L0_gnn_W"], a["L0_gnn_res_W"])):
                        for c in range(2):
                            loads.append(lambda l=l, k=k, w=w, c=c: sp.dma_start(
                                wt[:, c, k, l * D:(l + 1) * D].rearrange("p (h d) -> p h d", h=H),
                                w[l, :, c * P:(c + 1) * P, :].rearrange("h p d -> p h d")))
                    for v, g_ in ((gam, a["L0_gnn_bn_gamma"]), (bet, a["L0_gnn_bn_beta"])):
                        for c in range(2):
                            loads.append(lambda l=l, v=v, g_=g_, c=c: sp.dma_start(
                                v[:, c, l:l + 1], g_[l, c * P:(c + 1) * P].rearrange("(p o) -> p o", o=1)))
                for k, v in enumerate((a["L0_gnn_attn_r"], a["L0_gnn_attn_l"])):
                    loads.append(lambda k=k, v=v: sp.dma_start(att[:, k, :], v.rearrange("l h d -> (l h d)").partition_broadcast(P)))
                chain.dma(sp, *loads)
                bcl = lambda v: v.unsqueeze(2).broadcast_to([P, 2, L])
                chain.step(dve, lambda: dve.tensor_tensor(scale[:, :, :], gam[:, :, :], bcl(var), ALU.mult))
                chain.step(dve, lambda: dve.tensor_tensor(shift[:, :, :], scale[:, :, :], bcl(mean), ALU.mult))
                chain.step(dve, lambda: dve.tensor_tensor(shift[:, :, :], bet[:, :, :], shift[:, :, :], ALU.subtract))
                chain.step(dve, lambda: dve.tensor_copy(shift_w[:, :, :, :],
                                                        shift[:, :, :].unsqueeze(3).broadcast_to([P, 2, L, P])))
                for l in range(L):
                    chain.step(pe, *[lambda c=c, k=k: pe.matmul(bias_ps[:, k, 0:D], shift_w[:, c, l, :],
                                                                wt[:, c, k, l * D:(l + 1) * D], start=(c == 0), stop=(c == 1))
                                     for k in range(2) for c in range(2)])
                    chain.step(dve, lambda: dve.tensor_copy(wt_b[:, :, l * D:(l + 1) * D], bias_ps[:, :, 0:D]))
                    chain.apart(*[(dve, lambda c=c: dve.tensor_scalar(
                        wt[:, c, :, l * D:(l + 1) * D], wt[:, c, :, l * D:(l + 1) * D], scale[:, c, l:l + 1], None, ALU.mult))
                        for c in range(2)])
                for k in range(2):
                    for c in range(3):
                        w_, to_ = (wt[:, c, 0, :], ws[:, c, :]) if c < 2 else (wt_b[:, 0, :], ws_b[:, :])
                        chain.step(dve, lambda: dve.tensor_tensor(prod[:, :], w_, att[:, k, :], ALU.mult))
                        chain.step(dve, lambda: dve.tensor_reduce(
                            to_[:, k * L * H:(k + 1) * L * H], prod[:, :].rearrange("p (h d) -> p h d", d=DH), AX, ALU.add))
                fresh_chain("chain_scores")
            srow = lsb("srow", [P, GT, 2 * L * H])
            hb = lsb("hb", [P, 2, GT, P])
            with ExitStack() as inner:
                sc_ps = maker(inner, "ps")("sc_ps", [P, LANES, 512])

                def score_stage(ch, g, k, lo, m):
                    ps = sc_ps[:, k, 0:m * 2 * L * H].rearrange("p (b h) -> p b h", b=m)
                    yield ch.step(act, lambda: act.activation(
                        hb[:, :, lo:lo + m, :], hT[:, :, ds((g * GT + lo) * P, m * P)].rearrange("p c (b n) -> p c b n", n=P), ACT.Copy))
                    yield ch.step(pe, *[lambda b=b, c=c: pe.matmul(ps[:, b, :], hb[:, c, lo + b, :], ws[:, c, :],
                                                                   start=(c == 0), stop=(c == 1)) for b in range(m) for c in range(2)])
                    yield ch.step(dve, lambda: dve.tensor_tensor(srow[:, lo:lo + m, :], ps,
                                                                 ws_b[:, :].unsqueeze(1).broadcast_to([P, m, 2 * L * H]), ALU.add))
                    yield ch.step(dve, lambda: dve.tensor_copy(score_at[:, ds(g * GT + lo, m), 0:L * H],
                                                               srow[:, lo:lo + m, L * H:2 * L * H]))
                    yield ch.move(lambda e: e.dma_start(per_block(score_src[0:NP, :])[:, ds(g * GT + lo, m), :],
                                                        srow[:, lo:lo + m, 0:L * H]),
                                  lambda e: e.dma_start(per_block(table[0:NP, :])[:, ds(g * GT + lo, m), NW:AW],
                                                        srow[:, lo:lo + m, 0:L * H]))

                in_lanes(nc, lanes, NG, 50, 2, score_stage)
                fresh_chain("chain_tables")
            best0 = lsb("best0", [P, T, L * H])
            with ExitStack() as inner:
                top0 = SegmentMax(inner, "m0", score_src, L * H)
                top0.gather(0, QP // QB)
                count_nodes("src", src_pad, count_out)
                rank_nodes()
                tables = inner.enter_context(ExitStack())
                isb, ips = maker(tables, "sb"), maker(tables, "ps")
                orow = isb("orow", [P, 2, 2, NW])
                tab_ps = ips("tab_ps", [P, 2, 4, 512])
                pair = [lanes[0], lanes[2]]

                def table_stage(ch, g, k, lo, m):
                    yield ch.step(act, lambda: act.activation(
                        hb[:, :, lo:lo + m, :], hT[:, :, ds((g * GT + lo) * P, m * P)].rearrange("p c (b n) -> p c b n", n=P), ACT.Copy))
                    for b in range(lo, lo + m):
                        yield ch.step(pe, *[lambda c=c, q=q, z=z, c0=c0, c1=c1: pe.matmul(
                            tab_ps[:, k, 2 * q + z, 0:c1 - c0], hb[:, c, b, :], wt[:, c, q, c0:c1], start=(c == 0), stop=(c == 1))
                            for q in range(2) for z, (c0, c1) in enumerate(((0, 512), (512, NW))) for c in range(2)])
                        yield ch.step(dve, *[lambda q=q, z=z, c0=c0, c1=c1: dve.tensor_tensor(
                            orow[:, k, q, c0:c1], tab_ps[:, k, 2 * q + z, 0:c1 - c0], wt_b[:, q, c0:c1], ALU.add)
                            for q in range(2) for z, (c0, c1) in enumerate(((0, 512), (512, NW)))])
                        yield ch.move(lambda e: e.dma_start(table[ds((g * GT + b) * P, P), 0:NW], orow[:, k, 0, :]),
                                      lambda e: e.dma_start(residual[ds((g * GT + b) * P, P), :], orow[:, k, 1, :]))

                in_lanes(nc, pair, NG, 150, 8, table_stage, shares=((0, 4), (4, 3)), engines=NOT_POOL)
                for c in pair:
                    for e in (sp, dve, pe, act):
                        c.wait(e)
                tables.close()
                nc.all_engine_barrier()
                top0.finish(best0)
                fresh_chain("chain_pass0")
            own_and_max(score_at, best0[:, :, :], L * H, 0.01)
            chain.dma(sp, lambda: sp.dma_start(per_block(score_dst[0:NP, :]), score_at[:, :, :]))
            fresh_chain("chain_edges0")
        stack0.close()
        edge_pass("e0", L * D, heads=L * H, act_heads=6, slope=0.01, tab=table, tab_dst=score_dst)

        with ExitStack() as local:
            lsb = maker(local, "sb")
            sg = lsb("sg", [P, GT, AW])
            rg = lsb("rg", [P, GT, L * D])
            xg = lsb("xg0", [P, GT, D])
            tg = lsb("tg0", [P, GT, D])
            stat = lsb("stat0", [P, LANES, 2, GT])

            def close_stack(ch, g, k, lo, m):
                blk = lambda d: per_block(d[0:NP, :])[:, ds(g * GT + lo, m), :]
                s3, r3, x3, t3 = (v[:, lo:lo + m, :] for v in (sg, rg, xg, tg))
                yield ch.move(lambda e: e.dma_start(s3, blk(summed)), lambda e: e.dma_start(r3, blk(residual)),
                              lambda e: e.dma_start(x3, blk(x_dram)))
                den = s3[:, :, L * D:AW]
                yield ch.step(dve, lambda: dve.tensor_scalar(den, den, 1e-16, None, ALU.max))
                yield ch.step(dve, lambda: dve.reciprocal(den, den))
                for b in range(m):
                    v = s3[:, b, 0:L * D].rearrange("p (h d) -> p h d", d=DH)
                    yield ch.step(dve, lambda: dve.tensor_tensor(
                        v, v, den[:, b, :].unsqueeze(2).broadcast_to([P, L * H, DH]), ALU.mult))
                yield ch.step(dve, lambda: dve.tensor_tensor(r3, r3, s3[:, :, 0:L * D], ALU.add))
                part = [r3[:, :, l * D:(l + 1) * D] for l in range(L)]
                yield ch.step(act, lambda: act.activation(part[1], part[1], ACT.Tanh))
                yield ch.step(dve, lambda: dve.scalar_tensor_tensor(x3, part[0], 0.0, x3, ALU.max, ALU.add))
                yield ch.step(dve, lambda: dve.tensor_tensor(x3, x3, part[1], ALU.add))
                yield from elu(ch, part[2], t3, part[0])
                yield ch.step(dve, lambda: dve.tensor_tensor(x3, x3, part[0], ALU.add))
                yield ch.move(lambda e: e.dma_start(blk(x_dram), x3))
                yield from layer_norm(ch, x3, t3, stat[:, k, :, :], part[0], relu=True)
                yield ch.move(lambda e: e.dma_start(blk(h_dram), t3))

            in_lanes(nc, lanes, NG, 120, 5, close_stack)
            fresh_chain("chain_l1")

        def load_wT(lsb, name, dram, rows_, cols_):
            v = lsb(name, [P, rows_ // P, cols_])
            return v, lambda: sp.dma_start(v[:, :, :], dram.rearrange("(c p) n -> p c n", p=P))

        def broadcast(lsb, name, dram):
            v = lsb(name, [P, dram.shape[0]])
            return v, lambda: sp.dma_start(v[:, :], dram.partition_broadcast(P))

        def column(lsb, name, dram):
            n = dram.shape[0] // P
            v = lsb(name, [P, n])
            return v, lambda: sp.dma_start(v[:, :], dram.rearrange("(c p) -> p c", p=P), allow_slow_non_contiguous=True)

        with ExitStack() as local:
            lsb, lps = maker(local, "sb"), maker(local, "ps")
            gw, ld = load_wT(lsb, "gw", a["L1_gnn_gat_w"], D, D)
            att = lsb("att1", [P, 2, D])
            prod = lsb("prod1", [P, D])
            ws = lsb("ws1", [P, 2, 2 * H])
            hg = lsb("hg1", [P, GT, D])
            hgT = lsb("hgT1", [P, 2, GT, P])
            og = lsb("og1", [P, GT, D + H])
            sc1 = lsb("score_at1", [P, T, 2 * H])
            best1 = lsb("best1", [P, T, H])
            chain.dma(sp, ld, *[lambda k=k, v=v: sp.dma_start(att[:, k, :], v.rearrange("h d -> (h d)").partition_broadcast(P))
                                for k, v in enumerate((a["L1_gnn_gat_a_src"], a["L1_gnn_gat_a_tgt"]))])
            for k in range(2):
                for c in range(2):
                    chain.step(dve, lambda: dve.tensor_tensor(prod[:, :], gw[:, c, :], att[:, k, :], ALU.mult))
                    chain.step(dve, lambda: dve.tensor_reduce(ws[:, c, k * H:(k + 1) * H],
                                                              prod[:, :].rearrange("p (h d) -> p h d", d=DH), AX, ALU.add))
            table1 = at(table, 0, [[D + H, ROWS], [1, D + H]])
            src1 = at(score_src, 0, [[H, ROWS], [1, H]])
            dst1 = at(score_dst, 0, [[2 * H, ROWS], [1, 2 * H]])
            chain.dma(sp, lambda: sp.dma_start(table1[NP:ROWS, :], zeros[:, 0:D + H]),
                      lambda: sp.dma_start(src1[NP:ROWS, :], zeros[:, 0:H]),
                      lambda: sp.dma_start(dst1[NP:ROWS, :], zeros[:, 0:2 * H]))
            with ExitStack() as inner:
                ips = maker(inner, "ps")
                pr_ps = ips("pr_ps", [P, 4, 512])
                sc_ps = ips("sc_ps1", [P, LANES, 512])
                for e in (sp, pool, pe, dve, act):
                    chain.wait(e)

                def project(ch, g, k, lo, m):
                    h3, o3 = hg[:, lo:lo + m, :], og[:, lo:lo + m, :]
                    hT4 = hgT[:, :, lo:lo + m, :]
                    pr = pr_ps[:, k, :].rearrange("p (b d) -> p b d", d=D)
                    sc = sc_ps[:, k, 0:2 * H * m].rearrange("p (b h) -> p b h", b=m)
                    to = lambda d: per_block(d[0:NP, :])[:, ds(g * GT + lo, m), :]
                    yield ch.move(lambda e: e.dma_start(h3, to(h_dram)))
                    yield from turn_blocks(ch, hT4, h3, pr_ps[:, k, :].rearrange("p (c q n) -> p c q n", c=2, q=2))
                    yield ch.step(pe, *[lambda b=b, c=c: pe.matmul(pr[:, b, :], hT4[:, c, b, :], gw[:, c, :],
                                                                   start=(c == 0), stop=(c == 1)) for b in range(m) for c in range(2)])
                    yield ch.step(pe, *[lambda b=b, c=c: pe.matmul(sc[:, b, :], hT4[:, c, b, :], ws[:, c, :],
                                                                   start=(c == 0), stop=(c == 1)) for b in range(m) for c in range(2)])
                    yield ch.apart((dve, lambda: dve.tensor_copy(o3[:, :, D:D + H], sc[:, :, 0:H])),
                                   (dve, lambda: dve.tensor_copy(sc1[:, ds(g * GT + lo, m), 0:H], sc[:, :, H:2 * H])),
                                   (act, lambda: act.activation(o3[:, :, 0:D], pr[:, 0:m, :], ACT.Copy)))
                    yield ch.move(lambda e: e.dma_start(to(table1), o3), lambda e: e.dma_start(to(src1), o3[:, :, D:D + H]))

                in_lanes(nc, lanes, NG, 70, 3, project)
                fresh_chain("chain_rank")
            fresh_chain("chain_sort")
            with ExitStack() as inner:
                every_h = maker(inner, "sb")("every_h", [P, T, D])
                chain.dma(sp, lambda: sp.dma_start(every_h[:, :, :], per_block(h_dram[0:NP, :])))
                chain.gathers(pool, [lambda t=t: pool.indirect_dma_start(
                    sorted_h, bass.IndirectOffsetOnAxis(rank_i[:, t:t + 1], 0), every_h[:, t, :], None) for t in range(T)],
                    sem("placed"), 16 * T)
                fresh_chain("chain_max1")
            top1 = SegmentMax(local, "m1", src1, H)
            top1.gather(0, QP // QB)
            with ExitStack() as inner:
                isb, ips = maker(inner, "sb"), maker(inner, "ps")
                win, ld1 = load_wT(isb, "win", a["L1_gnn_in_proj_w"], D, 2 * D)
                wx, ld2 = load_wT(isb, "wx", a["L1_gnn_x_proj_w"], D, 3 * DS)
                cb, ld4 = column(isb, "cb", a["L1_gnn_conv_b"])
                db, ld5 = column(isb, "db", a["L1_gnn_dt_proj_b"])
                cw = isb("cw", [P, 2, 4])
                wdt = isb("wdt", [DS, D])
                ld7 = lambda: sp.dma_start(cw[:, :, :], a["L1_gnn_conv_w"].rearrange("(c p) k -> p c k", p=P))
                ld9 = lambda: sp.dma_start(wdt[:, :], a["L1_gnn_dt_proj_w"])
                chain.dma(sp, ld1, ld2, ld4, ld5, ld7, ld9)
                xg, xT = isb("xg_t", [P, GT, D]), isb("xT_t", [P, 2, GT, P])
                xin = isb("xin", [P, 2, 3 + TS])
                xc, zs = isb("xc", [P, 2, TS]), isb("zs", [P, 2, TS])
                dbc = isb("dbc", [3 * DS, TS])
                dt, dtx = isb("dt", [P, 2, TS]), isb("dtx", [P, 2, TS])
                u_, q_ = isb("u_", [P, 2, TS]), isb("q_", [P, 2, TS])
                mm_ps = ips("mm_ps_t", [P, 2, 512])
                turn = mm_ps[:, 0, :].rearrange("p (c k n) -> p c k n", c=2, k=2)
                halves = lambda v: v.rearrange("p (k n) -> p k n", n=HS)
                chain.step(dve, lambda: dve.memset(xin[:, :, 0:3], 0.0))
                with chain.loop(NG, 200, engines=NOT_POOL) as g:
                    chain.dma(sp, lambda: sp.dma_start(xg[:, :, :], per_block(sorted_h)[:, ds(g * GT, GT), :]))
                    one_by_one(turn_blocks(chain, xT, xg, turn))
                    xT2 = xT[:, :, :, :].rearrange("p c b n -> p c (b n)")
                    for j in range(4):
                        o = mm_ps[:, 0:2, 0:HS]
                        chain.step(pe, *[lambda c=c, z=z: pe.matmul(o[:, z, :], win[:, c, j * P:(j + 1) * P],
                                                                    xT2[:, c, z * HS:(z + 1) * HS], start=(c == 0), stop=(c == 1))
                                         for z in range(2) for c in range(2)])
                        to = xin[:, j, 3:3 + TS] if j < 2 else zs[:, j - 2, :]
                        chain.step(act, lambda: act.activation(halves(to), o, ACT.Copy if j < 2 else ACT.Silu))
                    for c in range(2):
                        chain.step(dve, lambda: dve.tensor_scalar(xc[:, c, :], xin[:, c, 0:TS], cw[:, c, 0:1], cb[:, c:c + 1],
                                                                  ALU.mult, ALU.add))
                        for k in range(1, 4):
                            chain.step(dve, lambda: dve.scalar_tensor_tensor(xc[:, c, :], xin[:, c, k:k + TS], cw[:, c, k:k + 1],
                                                                             xc[:, c, :], ALU.mult, ALU.add))
                    chain.step(act, lambda: act.activation(xc[:, :, :], xc[:, :, :], ACT.Silu))
                    chain.step(dve, lambda: dve.tensor_copy(u_[:, :, 0:3], xin[:, :, TS:TS + 3]))
                    chain.step(dve, lambda: dve.tensor_copy(xin[:, :, 0:3], u_[:, :, 0:3]))
                    chain.step(pe, *[lambda c=c, z=z: pe.matmul(mm_ps[0:3 * DS, z, 0:HS], wx[:, c, :], xc[:, c, z * HS:(z + 1) * HS],
                                                                start=(c == 0), stop=(c == 1)) for z in range(2) for c in range(2)])
                    chain.step(act, lambda: act.activation(halves(dbc[:, :]), mm_ps[0:3 * DS, 0:2, 0:HS], ACT.Copy))
                    for c in range(2):
                        chain.step(pe, *[lambda z=z: pe.matmul(mm_ps[:, z, 0:HS], wdt[:, c * P:(c + 1) * P],
                                                               dbc[0:DS, z * HS:(z + 1) * HS], start=True, stop=True) for z in range(2)])
                        chain.step(act, lambda: act.activation(halves(dt[:, c, :]), mm_ps[:, 0:2, 0:HS], ACT.Identity,
                                                               bias=db[:, c:c + 1]))
                    chain.step(act, lambda: act.activation(u_[:, :, :], dt[:, :, :], ACT.Abs))
                    chain.step(act, lambda: act.activation(u_[:, :, :], u_[:, :, :], ACT.Exp, scale=-1.0))
                    chain.step(dve, lambda: dve.tensor_scalar(q_[:, :, :], u_[:, :, :], 2.0, None, ALU.add))
                    chain.step(dve, lambda: dve.reciprocal(q_[:, :, :], q_[:, :, :]))
                    chain.step(dve, lambda: dve.tensor_tensor(u_[:, :, :], u_[:, :, :], q_[:, :, :], ALU.mult))
                    chain.step(act, lambda: act.activation(q_[:, :, :], u_[:, :, :], ACT.Square))
                    chain.step(dve, lambda: dve.tensor_scalar(dtx[:, :, :], q_[:, :, :], 1.0 / 13, None, ALU.mult))
                    for k in (11, 9, 7, 5, 3):
                        chain.step(dve, lambda: dve.scalar_tensor_tensor(dtx[:, :, :], dtx[:, :, :], 1.0 / k, q_[:, :, :],
                                                                         ALU.add, ALU.mult))
                    chain.step(dve, lambda: dve.scalar_tensor_tensor(dtx[:, :, :], dtx[:, :, :], 1.0, u_[:, :, :], ALU.add, ALU.mult))
                    chain.step(dve, lambda: dve.tensor_scalar(dt[:, :, :], dt[:, :, :], 0.0, None, ALU.max))
                    chain.step(dve, lambda: dve.scalar_tensor_tensor(dt[:, :, :], dtx[:, :, :], 2.0, dt[:, :, :], ALU.mult, ALU.add))
                    chain.step(dve, lambda: dve.tensor_tensor(dtx[:, :, :], dt[:, :, :], xc[:, :, :], ALU.mult))
                    now = ds(g * TS, TS)
                    chain.dma(sp, *[lambda n=n, v=v: sp.dma_start(by_time[n][:, :, now], v[:, :, :])
                                    for n, v in (("xc", xc), ("zs", zs), ("dt", dt), ("dtx", dtx))],
                              *[lambda k=k: sp.dma_start(bc_rows[ds(g * DS, DS), k, :], dbc[(1 + k) * DS:(2 + k) * DS, :])
                                for k in range(2)])
                for e in (sp, act, dve, pe):
                    chain.wait(e)
            top1.finish(best1)
            gmax = lsb("gmax", [P, 2])
            some = lsb("some", [P, T])
            off = lsb("off", [P, T])
            val = lsb("val", [P, T, H])
            own_and_max(sc1, best1[:, :, :], H, 0.2)
            chain.step(dve, lambda: dve.tensor_scalar(some[:, :], count_in[:, :], 1.0, None, ALU.min))
            chain.step(dve, lambda: dve.tensor_scalar(off[:, :], some[:, :], -1.0, BIG, ALU.add, ALU.mult))
            bch = lambda v: v.unsqueeze(2).broadcast_to([P, T, H])
            chain.step(dve, lambda: dve.tensor_tensor(val[:, :, :], sc1[:, :, H:2 * H], bch(some[:, :]), ALU.mult))
            chain.step(dve, lambda: dve.tensor_tensor(val[:, :, :], val[:, :, :], bch(off[:, :]), ALU.add))
            chain.step(dve, lambda: dve.tensor_reduce(gmax[:, 0:1], val[:, :, :].rearrange("p t h -> p (t h)"), AX, ALU.max))
            chain.step(pool, lambda: pool.partition_all_reduce(gmax[:, 1:2], gmax[:, 0:1], P, RMAX))
            chain.step(dve, lambda: dve.tensor_scalar(sc1[:, :, H:2 * H], val[:, :, :], 0.0, gmax[:, 1:2], ALU.mult, ALU.add))
            chain.dma(sp, lambda: sp.dma_start(per_block(dst1[0:NP, :]), sc1[:, :, :]))

            fresh_chain("chain_pass1")
        with ExitStack() as local:
            edges = EdgePass(local, "e1", D, heads=H, act_heads=4, slope=0.2, tab=table1, tab_dst=dst1)
            lsb, lps = maker(local, "sb"), maker(local, "ps")
            K, STEPS = 2 * DS, UB // 2
            MR = K // STEPS
            al = lsb("al", [P, 2, DS])
            dt, dtx = lsb("dt_s", [P, 2, TS]), lsb("dtx_s", [P, 2, TS])
            bc = lsb("bc", [P, 2, 2, TS])
            decay, inp = lsb("decay", [P, 2, TS]), lsb("inp", [P, 2, TS])
            hs, prod = lsb("hs", [P, 2, TS]), lsb("prod_t", [P, 2, TS])
            y_sb = lsb("y_sb", [P, 2, TS])
            state = lsb("state", [P, K])
            y_ps = lps("y_ps", [P, 4, 512])
            s_decay, s_inp, s_scan, s_prod, s_y, s_state, s_dt, s_copied, s_stored = (
                sem(f"t_{n}") for n in ("decay", "inp", "scan", "prod", "y", "state", "dt", "copied", "stored"))
            s_bc = [sem(f"t_bc{b}") for b in range(2)]
            chain.dma(sp, lambda: sp.dma_start(al[:, :, :], a["L1_gnn_A_log"].rearrange("(c p) k -> p c k", p=P)),
                      *[lambda k=k, z=z: sp.dma_start(bc_rows[NG * DS:NG * DS + 2, k, z * HS:(z + 1) * HS], zeros[0:2, 0:HS])
                        for k in range(2) for z in range(2)])
            chain.step(act, lambda: act.activation(al[:, :, :], al[:, :, :], ACT.Exp))
            chain.step(dve, lambda: dve.tensor_scalar(al[:, :, :], al[:, :, :], -1.0, None, ALU.mult))
            chain.step(dve, lambda: dve.memset(state[:, :], 0.0))
            for e in (sp, act, dve, pe):
                chain.wait(e)
            for s in (s_scan, s_prod, s_y, s_state):
                dve.sem_inc(s, 2)

            def load_bc(r, b):
                if not isinstance(r, int):
                    sp.wait_ge(s_prod, STEPS * (r - 1) + 2 * b + 4)
                sp.dma_start(bc[:, b, :, :], bc_rows[ds(2 * r + b, 1), :, :].rearrange("o k t -> (o k t)").partition_broadcast(P)
                             ).then_inc(s_bc[b], 16)

            def make_input(r, k):
                b, c = k // 2, k % 2
                if c == 0:
                    dve.wait_ge(s_bc[b], 16 * (r + 1))
                dve.wait_ge(s_scan, STEPS * r + k + 1)
                dve.tensor_tensor(inp[:, c, :], bc[:, b, 0, :], dtx[:, c, :], ALU.mult).then_inc(s_inp, 1)

            def scan(r, k, m):
                q, c = STEPS * r + k, k % 2
                dve.wait_ge(s_inp, q + 1)
                dve.wait_ge(s_decay, q + 1)
                dve.wait_ge(s_prod, q + 1)
                dve.wait_ge(s_state, q + 1)
                dve.tensor_tensor_scan(hs[:, c, :], decay[:, c, :], inp[:, c, :], state[:, ds(STEPS * m + k, 1)],
                                       ALU.mult, ALU.add).then_inc(s_scan, 1)

            def times_c(r, k):
                q, b, c = STEPS * r + k, k // 2, k % 2
                dve.wait_ge(s_scan, q + 3)
                dve.wait_ge(s_y, q + 1)
                dve.tensor_tensor(prod[:, c, :], bc[:, b, 1, :], hs[:, c, :], ALU.mult).then_inc(s_prod, 1)

            def make_decay(r, k, m):
                act.wait_ge(s_scan, STEPS * r + k + 1)
                act.activation(decay[:, k % 2, :], dt[:, k % 2, :], ACT.Exp,
                               scale=al[:, k % 2, ds(STEPS // 2 * m + k // 2, 1)]).then_inc(s_decay, 1)

            def keep_state(r, k, m):
                act.wait_ge(s_scan, STEPS * r + k + 3)
                act.activation(state[:, ds(STEPS * m + k, 1)], hs[:, k % 2, TS - 1:TS], ACT.Copy).then_inc(s_state, 1)

            def add_up(r, k):
                c = k % 2
                pe.wait_ge(s_prod, STEPS * r + k + 3)
                for z in range(2):
                    mm = pe.matmul(y_ps[:, 2 * c + z, 0:HS], ident[:, :], prod[:, c, z * HS:(z + 1) * HS],
                                   start=False, stop=False, skip_group_check=True)
                mm.then_inc(s_y, 1)

            for b in range(2):
                load_bc(0, b)
            edges.rounds(0, 1)
            with nc.Fori(0, NG) as g:
                now = ds(g * TS, TS)
                sp.wait_ge(s_decay, g * K)
                sp.dma_start(dt[:, :, :], by_time["dt"][:, :, now]).then_inc(s_dt, 16)
                sp.wait_ge(s_inp, g * K)
                sp.dma_start(dtx[:, :, :], by_time["dtx"][:, :, now]).then_inc(s_dt, 16)
                pe.wait_ge(s_copied, 2 * g)
                for z in range(4):
                    pe.matmul(y_ps[:, z, 0:HS], zeros[:, 0:P], zeros[:, 0:HS], start=True, stop=False, skip_group_check=True)
                with nc.Fori(0, MR) as m:
                    r = g * MR + m
                    i = r + 1
                    edges.pool_round(i)
                    for k in range(STEPS):
                        v = 2 * k
                        edges.sp_slot(i, v)
                        edges.sp_slot(i, v + 1)
                        if k % 2:
                            load_bc(r + 1, k // 2)
                        if k == 0:
                            dve.wait_ge(s_dt, 32 * (g + 1))
                            act.wait_ge(s_dt, 32 * (g + 1))
                        make_input(r, k)
                        edges.dve_slot(i, v)
                        scan(r, k, m)
                        edges.dve_slot(i, v + 1)
                        times_c(r, k)
                        make_decay(r, k, m)
                        edges.act_slot(i, v)
                        edges.act_slot(i, v + 1)
                        keep_state(r, k, m)
                        edges.pe_slot(i, v)
                        edges.pe_slot(i, v + 1)
                        add_up(r, k)
                act.wait_ge(s_y, g * K + K + 2)
                act.wait_ge(s_stored, 16 * g)
                for c in range(2):
                    act.activation(y_sb[:, c, :].rearrange("p (k n) -> p k n", n=HS), y_ps[:, 2 * c:2 * c + 2, 0:HS],
                                   ACT.Copy).then_inc(s_copied, 1)
                sp.wait_ge(s_copied, 2 * g + 2)
                sp.dma_start(by_time["y"][:, :, now], y_sb[:, :, :]).then_inc(s_stored, 16)
            edges.rounds(1 + NG * MR, EdgePass.ROUNDS - 1 - NG * MR)
            for b in range(2):
                sp.wait_ge(s_bc[b], 16 * (NG * MR + 1))
            sp.wait_ge(s_stored, 16 * NG)
            for e in (act, dve, pe):
                e.wait_ge(s_state, NG * K + 2)
                e.wait_ge(s_y, NG * K + 2)
            edges.end()

        fresh_chain("chain_time")
        with ExitStack() as local:
            lsb, lps = maker(local, "sb"), maker(local, "ps")
            wo, ld1 = load_wT(lsb, "wo", a["L1_gnn_out_proj_w"], D, D)
            dp, ld2 = column(lsb, "dp", a["L1_gnn_D_param"])
            chain.dma(sp, ld1, ld2)
            y_t, x_t, z_t = (lsb(f"{n}_t", [P, 2, TS]) for n in "yxz")
            o_t = lsb("o_t", [P, GT, D])
            o_ps = lps("o_ps_t", [P, LANES, 512])
            for e in (sp, pool, pe, dve):
                chain.wait(e)

            def gate_and_project(ch, g, k, lo, m):
                y3, x3, z3 = (v[:, :, lo * P:(lo + m) * P] for v in (y_t, x_t, z_t))
                o2 = o_ps[:, k, :].rearrange("p (b d) -> p b d", d=D)
                now = ds((g * GT + lo) * P, m * P)
                yield ch.move(*[lambda e, n=n, v=v: e.dma_start(v, by_time[n][:, :, now])
                                for n, v in (("y", y3), ("xc", x3), ("zs", z3))])
                yield ch.apart(*[(dve, lambda c=c: dve.scalar_tensor_tensor(y3[:, c, :], x3[:, c, :], dp[:, c:c + 1], y3[:, c, :],
                                                                            ALU.mult, ALU.add)) for c in range(2)])
                yield ch.step(dve, lambda: dve.tensor_tensor(y3, y3, z3, ALU.mult))
                yield ch.step(pe, *[lambda b=b, c=c: pe.matmul(o2[:, b, :], y3[:, c, b * P:(b + 1) * P], wo[:, c, :],
                                                               start=(c == 0), stop=(c == 1)) for b in range(m) for c in range(2)])
                yield ch.step(act, lambda: act.activation(o_t[:, lo:lo + m, :], o2[:, 0:m, :], ACT.Copy))
                yield ch.move(lambda e: e.dma_start(per_block(sorted_y)[:, ds(g * GT + lo, m), :], o_t[:, lo:lo + m, :]))

            in_lanes(nc, lanes, NG, 120, 4, gate_and_project)
            fresh_chain("chain_merge")

        with ExitStack() as local:
            lsb, lps = maker(local, "sb"), maker(local, "ps")
            y_all = lsb("y_all", [P, T, D])
            chain.gathers(pool, [lambda t=t: pool.indirect_dma_start(
                y_all[:, t, :], None, sorted_y, bass.IndirectOffsetOnAxis(rank_i[:, t:t + 1], 0)) for t in range(T)],
                sem("returned"), 16 * T)
            names = ("gat_b", "ln_local_g", "ln_local_b", "ln_global_g", "ln_global_b", "ln2_g", "ln2_b", "ff2_b")
            vecs, loads = {}, []
            for n in names:
                vecs[n], ld = broadcast(lsb, f"v_{n}", a[f"L1_gnn_{n}"])
                loads.append(ld)
            wl, l1 = load_wT(lsb, "wl", a["L1_gnn_wl"], D, D)
            wg, l2 = load_wT(lsb, "wg", a["L1_gnn_wg"], D, D)
            f1, l3 = load_wT(lsb, "f1", a["L1_gnn_ff1_w"], D, 2 * D)
            f2, l4 = load_wT(lsb, "f2", a["L1_gnn_ff2_w"], 2 * D, D)
            fb, l5 = column(lsb, "fb", a["L1_gnn_ff1_b"])
            chain.dma(sp, *loads, l1, l2, l3, l4, l5)
            sg = lsb("sg1", [P, GT, D + H])
            hg, hl, ha = (lsb(n, [P, GT, D]) for n in ("hg2", "hl", "ha"))
            tg = lsb("tg2", [P, GT, D])
            xT, yT = (lsb(n, [P, 2, GT, P]) for n in ("hlT", "haT"))
            ffT = lsb("ffT", [P, 4, TS])
            stat = lsb("stat1", [P, LANES, 2, GT])
            turn = lps("turn2", [P, LANES, 2, 2, P])
            mm_ps = lps("mm_ps", [P, 4, 512])
            for e in (sp, pool, pe, dve, act):
                chain.wait(e)

            def merge(ch, g, k, lo, m):
                blk = lambda d: per_block(d[0:NP, :])[:, ds(g * GT + lo, m), :]
                s3, h3, l3, a3, t3 = (v[:, lo:lo + m, :] for v in (sg, hg, hl, ha, tg))
                lT, aT = xT[:, :, lo:lo + m, :], yT[:, :, lo:lo + m, :]
                fT = ffT[:, :, lo * P:(lo + m) * P]
                st, tn = stat[:, k, :, :], turn[:, k, :, :, :]
                o_ps = mm_ps[:, k, :].rearrange("p (b d) -> p b d", d=D)
                ff = tn.rearrange("p c q n -> p (c q n)")[:, 0:m * P]
                bv = lambda n: vecs[n][:, :].unsqueeze(1).broadcast_to([P, m, D])
                yield ch.move(lambda e: e.dma_start(s3, blk(summed[:, 0:D + H])), lambda e: e.dma_start(h3, blk(h_dram)))
                den = s3[:, :, D:D + H]
                yield ch.step(dve, lambda: dve.tensor_scalar(den, den, 1e-16, None, ALU.add))
                yield ch.step(dve, lambda: dve.reciprocal(den, den))
                for b in range(m):
                    yield ch.step(dve, lambda: dve.tensor_tensor(
                        l3[:, b, :].rearrange("p (h d) -> p h d", d=DH), s3[:, b, 0:D].rearrange("p (h d) -> p h d", d=DH),
                        den[:, b, :].unsqueeze(2).broadcast_to([P, H, DH]), ALU.mult))
                yield ch.step(dve, lambda: dve.tensor_tensor(l3, l3, h3, ALU.add))
                yield ch.step(dve, lambda: dve.tensor_tensor(l3, l3, bv("gat_b"), ALU.add))
                yield from elu(ch, l3, t3, l3)
                yield from layer_norm(ch, l3, l3, st, t3, gain=vecs["ln_local_g"][:, :], shift=vecs["ln_local_b"][:, :])
                yield from turn_blocks(ch, lT, l3, tn)
                yield ch.step(dve, lambda: dve.tensor_tensor(a3, h3, y_all[:, ds(g * GT + lo, m), :], ALU.add))
                yield from layer_norm(ch, a3, a3, st, t3, gain=vecs["ln_global_g"][:, :], shift=vecs["ln_global_b"][:, :])
                yield from turn_blocks(ch, aT, a3, tn)
                yield ch.step(pe, *[lambda b=b, c=c: pe.matmul(o_ps[:, b, :], (lT, aT)[c // 2][:, c % 2, b, :],
                                                               (wl, wg)[c // 2][:, c % 2, :], start=(c == 0), stop=(c == 3))
                                    for b in range(m) for c in range(4)])
                yield ch.step(act, lambda: act.activation(t3, o_ps[:, 0:m, :], ACT.Sigmoid))
                yield ch.step(dve, lambda: dve.tensor_tensor(l3, l3, a3, ALU.subtract))
                yield ch.step(dve, lambda: dve.tensor_tensor(l3, l3, t3, ALU.mult))
                yield ch.step(dve, lambda: dve.tensor_tensor(l3, l3, a3, ALU.add))
                yield from turn_blocks(ch, lT, l3, tn)
                for j in range(4):
                    yield ch.step(pe, *[lambda c=c: pe.matmul(ff, f1[:, c, j * P:(j + 1) * P], lT[:, c, :, :],
                                                              start=(c == 0), stop=(c == 1)) for c in range(2)])
                    yield ch.step(act, lambda: act.activation(fT[:, j, :], ff, ACT.Relu, bias=fb[:, j:j + 1]))
                yield ch.step(pe, *[lambda b=b, j=j: pe.matmul(o_ps[:, b, :], fT[:, j, b * P:(b + 1) * P], f2[:, j, :],
                                                               start=(j == 0), stop=(j == 3)) for b in range(m) for j in range(4)])
                yield ch.step(dve, lambda: dve.tensor_tensor(l3, l3, o_ps[:, 0:m, :], ALU.add))
                yield ch.step(dve, lambda: dve.tensor_tensor(l3, l3, bv("ff2_b"), ALU.add))
                yield from layer_norm(ch, l3, l3, st, t3, gain=vecs["ln2_g"][:, :], shift=vecs["ln2_b"][:, :])
                yield ch.move(lambda e: e.dma_start(a3, blk(x_dram)))
                yield ch.step(dve, lambda: dve.tensor_tensor(a3, a3, l3, ALU.add))
                yield ch.move(lambda e: e.dma_start(blk(x_dram), a3))
                yield from layer_norm(ch, a3, l3, st, t3, relu=True)
                yield ch.move(lambda e: e.dma_start(blk(h_dram), l3))

            in_lanes(nc, lanes, NG, 220, 5, merge)
            fresh_chain("chain_pass2")

        edge_pass("e2", D, weighted=True, tab=h_dram)
        finish = ExitStack()
        with finish:
            lsb = maker(finish, "sb")
            sg, hg, xg, tg, og = (lsb(n, [P, GT, D]) for n in ("sg_f", "hg_f", "xg_f", "tg_f", "og_f"))
            xT, yT = (lsb(n, [P, 2, GT, P]) for n in ("hT_f", "sT_f"))
            stat = lsb("stat_f", [P, LANES, 2, GT])
            w1, l1 = load_wT(lsb, "w1", a["L2_gnn_W1"], D, D)
            w2, l2 = load_wT(lsb, "w2", a["L2_gnn_W2"], D, D)
            w3, l3 = load_wT(lsb, "w3", a["L3_gnn_W"], D, D)
            w4, l4 = load_wT(lsb, "w4", a["L3_gnn_M"], D, D)
            b1, l5 = broadcast(lsb, "b1", a["L2_gnn_b1"])
            b2, l6 = broadcast(lsb, "b2", a["L2_gnn_b2"])
            chain.dma(sp, l1, l2, l3, l4, l5, l6)
            chain.step(dve, lambda: dve.tensor_tensor(b1[:, :], b1[:, :], b2[:, :], ALU.add))
            for e in (sp, pool, pe, dve, act):
                chain.wait(e)

            def load_and_multiply(ch, g, k, lo, m, wa, wb, interact):
                blk = lambda d: per_block(d[0:NP, :])[:, ds(g * GT + lo, m), :]
                s3, h3, x3 = (v[:, lo:lo + m, :] for v in (sg, hg, xg))
                hT4, sT4 = xT[:, :, lo:lo + m, :], yT[:, :, lo:lo + m, :]
                o_ps = mm_ps[:, k, :].rearrange("p (b d) -> p b d", d=D)
                yield ch.move(lambda e: e.dma_start(s3, blk(summed[:, 0:D])), lambda e: e.dma_start(h3, blk(h_dram)),
                              lambda e: e.dma_start(x3, blk(x_dram)))
                if interact:
                    yield ch.step(dve, lambda: dve.scalar_tensor_tensor(s3, h3, 1.0, s3, ALU.add, ALU.mult))
                yield from turn_blocks(ch, hT4, h3, turn[:, k, :, :, :])
                yield from turn_blocks(ch, sT4, s3, turn[:, k, :, :, :])
                yield ch.step(pe, *[lambda b=b, c=c: pe.matmul(o_ps[:, b, :], (hT4, sT4)[c // 2][:, c % 2, b, :],
                                                               (wa, wb)[c // 2][:, c % 2, :], start=(c == 0), stop=(c == 3))
                                    for b in range(m) for c in range(4)])

            def interaction(ch, g, k, lo, m):
                blk = lambda d: per_block(d[0:NP, :])[:, ds(g * GT + lo, m), :]
                x3, t3, o3 = (v[:, lo:lo + m, :] for v in (xg, tg, og))
                o_ps = mm_ps[:, k, :].rearrange("p (b d) -> p b d", d=D)
                yield from load_and_multiply(ch, g, k, lo, m, w1, w2, True)
                norm = stat[:, k, 0, 0:m]
                yield ch.step(dve, lambda: dve.tensor_tensor(o3, o_ps[:, 0:m, :],
                                                             b1[:, :].unsqueeze(1).broadcast_to([P, m, D]), ALU.add))
                yield ch.step(dve, lambda: dve.scalar_tensor_tensor(o3, o3, 0.2, o3, ALU.mult, ALU.max))
                yield ch.step(act, lambda: act.activation(t3, o3, ACT.Square))
                yield ch.step(dve, lambda: dve.tensor_reduce(norm, t3, AX, ALU.add))
                yield ch.step(act, lambda: act.activation(norm, norm, ACT.Sqrt))
                yield ch.step(dve, lambda: dve.tensor_scalar(norm, norm, 1e-12, None, ALU.max))
                yield ch.step(dve, lambda: dve.reciprocal(norm, norm))
                yield ch.step(dve, lambda: dve.tensor_tensor(o3, o3, norm.unsqueeze(2).broadcast_to([P, m, D]), ALU.mult))
                yield ch.step(dve, lambda: dve.tensor_tensor(x3, x3, o3, ALU.add))
                yield ch.move(lambda e: e.dma_start(blk(x_dram), x3))
                yield from layer_norm(ch, x3, o3, stat[:, k, :, :], t3, relu=True)
                yield ch.move(lambda e: e.dma_start(blk(h_dram), o3))

            def banks(stack, n):
                lps = maker(stack, "ps")
                return lps(f"turn{n}", [P, LANES, 2, 2, P]), lps(f"mm_ps{n}", [P, LANES, 512])

            with ExitStack() as inner:
                turn, mm_ps = banks(inner, 3)
                in_lanes(nc, lanes, NG, 120, 5, interaction)
            fresh_chain("chain_pass3")
            edge_pass("e3", D, tab=h_dram)

            def linear(ch, g, k, lo, m):
                x3 = xg[:, lo:lo + m, :]
                o_ps = mm_ps[:, k, :].rearrange("p (b d) -> p b d", d=D)
                yield from load_and_multiply(ch, g, k, lo, m, w3, w4, False)
                yield ch.step(dve, lambda: dve.scalar_tensor_tensor(x3, o_ps[:, 0:m, :], 0.0, x3, ALU.max, ALU.add))

            def store(ch, g, lo, m):
                whole = out[0:(T - 1) * P, :].rearrange("(t p) c -> p t c", p=P)
                return ch.move(lambda e: e.dma_start(whole[:, ds(g * GT + lo, m), :], xg[:, lo:lo + m, :]))

            def linear_and_store(ch, g, k, lo, m):
                yield from linear(ch, g, k, lo, m)
                yield store(ch, g, lo, m)

            def linear_and_store_last(ch, g, k, lo, m):
                yield from linear(ch, g, k, lo, m)
                if lo + m < GT:
                    yield store(ch, g, lo, m)
                else:
                    if m > 1:
                        yield store(ch, g, lo, m - 1)
                    yield ch.move(lambda e: e.dma_start(out[(T - 1) * P:N, :], xg[0:TAIL, GT - 1, :]))

            turn, mm_ps = banks(finish, 4)
            in_lanes(nc, lanes, NG - 1, 80, 4, linear_and_store, last=linear_and_store_last)
            for c in lanes:
                c.wait(sp)


_TURNED = {"L1_gnn_gat_w", "L1_gnn_in_proj_w", "L1_gnn_x_proj_w", "L1_gnn_dt_proj_w", "L1_gnn_out_proj_w",
           "L1_gnn_wl", "L1_gnn_wg", "L1_gnn_ff1_w", "L1_gnn_ff2_w", "L2_gnn_W1", "L2_gnn_W2"}


def kernel(**inputs):
    import numpy as _np
    import concourse.bacc as _bacc
    from concourse import mybir as _mybir
    from concourse.bass_utils import run_bass_kernel_spmd as _run

    nc = _bacc.Bacc("TRN2", target_bir_lowering=False, num_devices=1)
    arrays, args = {}, {}
    for name, given in inputs.items():
        v = _np.asarray(given)
        v = _np.ascontiguousarray(v.T if name in _TURNED else v)
        arrays[f"in_{name}"] = v
        args[name] = nc.dram_tensor(f"in_{name}", v.shape, _mybir.dt.from_np(v.dtype), kind="ExternalInput").ap()
    out = nc.dram_tensor("out_0", [N, D], _mybir.dt.float32, kind="ExternalOutput").ap()
    graph_stack_kernel(nc, args, out)
    result = _run(nc, [arrays], core_ids=[0])
    return result.results[0]["out_0"]
```

```python
from contextlib import ExitStack, contextmanager

import concourse.bass as bass
from concourse import mybir

F32 = mybir.dt.float32
BF16 = mybir.dt.bfloat16
I32 = mybir.dt.int32
ALU = mybir.AluOpType
ACT = mybir.ActivationFunctionType
AX = mybir.AxisListType.X
ENG = mybir.EngineType
RMAX = bass.bass_isa.ReduceOp.max

P = 128
N, D, E = 6250, 256, 106250
T = -(-N // P)
NP = T * P
TAIL = N - (T - 1) * P
LANES = 7
GB = 2 * LANES
SHARES = tuple((2 * k, 2) for k in range(LANES))
REST = tuple((b, min(2, T % GB - b)) for b in range(0, T % GB, 2))
GT = 7
NG = T // GT
H, DH = 4, 64
L = 3
UE = 256
UNITS = E // UE + T
UB = 8
SB = 4
UC = 512
QP = 832
QB = 8
EPAD = 1 + max(P * QP, E + UE) + 256
FRONT = 1
BIG = 1.0e30
ROWS = NP + P
AW = L * D + L * H
SKIP = T + 1
TS = GT * P
HS = TS // 2
DS = 16


NOT_POOL = (ENG.Activation, ENG.PE, ENG.DVE, ENG.SP)
ALL = (ENG.Pool, *NOT_POOL)


class Chain:

    def __init__(self, nc, sem, carrier=None, landed=None, passed=None):
        self.nc, self.sem, self.carrier, self.landed, self.passed = nc, sem, carrier, landed, passed
        self.base, self.local = 0, 0
        self.landed_base, self.landed_local = 0, 0

    def wait(self, eng):
        value = self.base + self.local
        if not isinstance(value, int) or value:
            eng.wait_ge(self.sem, value)

    def step(self, eng, *instructions):
        self.wait(eng)
        for f in instructions:
            last = f()
        last.then_inc(self.sem, 1)
        self.local += 1

    def apart(self, *pairs):
        for eng in {id(e): e for e, _ in pairs}.values():
            self.wait(eng)
            for e, f in pairs:
                if e is eng:
                    f().then_inc(self.sem, 1)
        self.local += len(pairs)

    def dma(self, eng, *instructions):
        self.wait(eng)
        for f in instructions:
            f().then_inc(self.sem, 16)
        self.local += 16 * len(instructions)

    def move(self, *dmas):
        e = self.carrier
        self.wait(e)
        if self.landed is None:
            for f in dmas:
                f(e).then_inc(self.sem, 16)
            self.local += 16 * len(dmas)
            return
        e.sem_inc(self.passed, 1)
        for f in dmas:
            f(e).then_inc(self.landed, 16)
        self.landed_local += 16 * len(dmas)
        e.wait_ge(self.landed, self.landed_base + self.landed_local)
        e.sem_inc(self.sem, 1)
        self.local += 1

    def gathers(self, pool, instructions, sem, value):
        self.wait(pool)
        for f in instructions:
            f().then_inc(sem, 16)
        pool.wait_ge(sem, value)
        pool.sem_inc(self.sem, 1)
        self.local += 1

    @contextmanager
    def loop(self, n, per, engines=ALL):
        first = self.base + self.local
        assert isinstance(first, int)
        with self.nc.Fori(0, n, engines=engines) as i:
            self.base, self.local = first + i * per, 0
            yield i
            self.close(per)
        self.base, self.local = first + n * per, 0

    def close(self, per):
        assert self.local < per, (self.local, per)
        e = self.carrier or self.nc.sync
        self.wait(e)
        e.sem_inc(self.sem, per - self.local)


def in_lanes(nc, lanes, per, moves, stage, last=None, beside=None, behind=2, n=T // GB, shares=SHARES, rest=REST, engines=ALL):
    def run(i, stage, shares):
        steps = [stage(lane, i, k, *share) for k, (lane, share) in enumerate(zip(lanes, shares))]
        others = beside(i) if beside else iter(())
        turn = 0
        while steps:
            for s in steps[:1 + turn // behind]:
                if next(s, steps) is steps:
                    steps.remove(s)
            next(others, None)
            turn += 1
        for _ in others:
            pass

    starts = [c.base + c.local for c in lanes]
    arrived = [c.landed_base + c.landed_local for c in lanes]
    with nc.Fori(0, n, engines=engines) as i:
        for c, first, there in zip(lanes, starts, arrived):
            c.base, c.local = first + i * per, 0
            c.landed_base, c.landed_local = there + i * (16 * moves), 0
        run(i, stage, shares)
        for c in lanes:
            c.close(per)
            assert c.landed is None or c.landed_local == 16 * moves, c.landed_local
    for c, first, there in zip(lanes, starts, arrived):
        c.base, c.local = first + n * per, 0
        if c.landed is not None:
            c.landed_base, c.landed_local = there + n * 16 * moves, 0
    run(n, last or stage, rest)


def at(dram, offset, pattern):
    return bass.AP(tensor=dram.tensor, offset=offset, ap=pattern)


def graph_stack_kernel(nc, a, out):
    ds = bass.ds
    sp, act, pool, dve, pe = nc.sync, nc.scalar, nc.gpsimd, nc.vector, nc.tensor

    root = ExitStack()
    with root:
        def sem(name):
            return root.enter_context(nc.semaphore(name))

        def maker(stack, kind):
            make = nc.sbuf_tensor if kind == "sb" else nc.psum_tensor
            return lambda name, shape, dt=F32: stack.enter_context(make(name, shape, dt))

        def scratch(name, shape, dt=F32):
            return nc.dram_tensor(name, shape, dt, kind="Internal").ap()

        def per_block(dram):
            return dram.rearrange("(t p) c -> p t c", p=P)

        sb = maker(root, "sb")

        src_pad = scratch("src_pad", [EPAD], I32)
        dst_pad = scratch("dst_pad", [EPAD], I32)
        w_pad = scratch("w_pad", [EPAD])
        table = scratch("table", [ROWS, AW])
        score_src = scratch("score_src", [ROWS, L * H])
        score_dst = scratch("score_dst", [ROWS, 2 * L * H])
        running = scratch("running", [P * QP, L * H])
        summed = scratch("summed", [(SKIP + 1) * P, AW])
        residual = scratch("residual", [NP, L * D])
        h_dram = scratch("h_dram", [ROWS, D])
        x_dram = scratch("x_dram", [NP, D])
        sorted_h = scratch("sorted_h", [NP, D])
        sorted_y = scratch("sorted_y", [NP, D])
        key_row = scratch("key_row", [NP])
        by_time = {n: scratch(f"scan_{n}", [P, 2, NP]) for n in ("xc", "zs", "dt", "dtx", "y")}
        bc_rows = scratch("bc_rows", [(NG + 1) * DS, 2, TS])
        rel_rows = scratch("rel_rows", [UC * UE])

        passed = sem("passed")
        cleared = sem("cleared")
        dve_passed = sem("dve_passed")
        chain = Chain(nc, sem("chain"))
        lanes = [Chain(nc, sem(f"lane_{k}"), pool, sem(f"lane_{k}_landed"), passed) if k in (1, 3, 5)
                 else Chain(nc, sem(f"lane_{k}"), sp) for k in range(LANES)]

        def fresh_chain(name):
            for e in (sp, act, pool, dve, pe):
                for c in (chain, *lanes):
                    c.wait(e)
            nc.all_engine_barrier()
            chain.sem, chain.base, chain.local = sem(name), 0, 0

        ident = sb("ident", [P, P])
        iota = sb("iota", [P, P])
        lane = sb("lane", [P, 1])
        ones = sb("ones", [P, P])
        count_in = sb("count_in", [P, T])
        count_out = sb("count_out", [P, T])
        last_edge = sb("last_edge", [P, T], I32)
        unit_src = sb("unit_src", [P, UC, 2], I32)
        unit_rel = sb("unit_rel", [P, UC, 2])
        unit_w = sb("unit_w", [P, UC, 2])
        unit_keep = sb("unit_keep", [P, UC])
        unit_block = sb("unit_block", [1, UC], I32)
        unit_at = sb("unit_at", [1, UC], I32)
        rank_i = sb("rank_i", [P, T], I32)

        zeros = sb("zeros", [P, AW])
        eps = sb("eps", [P, 1])
        chain.apart((pool, lambda: pool.iota(iota[:, :], [[1, P]], base=0, channel_multiplier=0,
                                            allow_small_or_imprecise_dtypes=True)),
                   (pool, lambda: pool.iota(lane[:, :], [[0, 1]], base=0, channel_multiplier=1,
                                            allow_small_or_imprecise_dtypes=True)),
                   (dve, lambda: dve.memset(ones[:, :], 1.0)),
                   (dve, lambda: dve.memset(eps[:, :], 1e-5)),
                   (dve, lambda: dve.memset(zeros[:, :], 0.0)))
        chain.step(dve, lambda: dve.tensor_scalar(ident[:, :], iota[:, :], lane[:, 0:1], None, ALU.is_equal))

        with ExitStack() as local:
            lsb = maker(local, "sb")
            tail = EPAD - FRONT - E
            pad_i = lsb("pad_i", [1, tail], I32)
            pad_front = lsb("pad_front", [1, 2], I32)
            chain.apart((dve, lambda: dve.memset(pad_i[:, :], NP)),
                       (dve, lambda: dve.memset(pad_front[:, :], -1)))
            row = lambda v: v.rearrange("(o n) -> o n", o=1)
            copies = []
            for pad, given in ((src_pad, a["src"]), (dst_pad, a["dst"]), (w_pad, a["edge_weight"])):
                copies.append(lambda pad=pad, given=given: sp.dma_start(
                    pad[FRONT:FRONT + E].rearrange("(q n) -> q n", q=125), given.rearrange("(q n) -> q n", q=125)))
            for pad in (src_pad, dst_pad):
                copies.append(lambda pad=pad: sp.dma_start(row(pad[FRONT + E:EPAD]), pad_i[:, :]))
                copies.append(lambda pad=pad: sp.dma_start(row(pad[0:FRONT]), pad_front[:, 0:1]))
            copies.append(lambda: sp.dma_start(row(w_pad[FRONT + E:EPAD]), zeros[0:1, 0:tail]))
            copies.append(lambda: sp.dma_start(row(w_pad[0:FRONT]), zeros[0:1, 0:1]))
            for d in (table, score_src, score_dst, h_dram):
                copies.append(lambda d=d: sp.dma_start(d[NP:ROWS, :], zeros[:, 0:d.shape[1]]))
            chain.dma(sp, *copies)
            fresh_chain("chain_setup")

        class NodeCount:

            GROUPS = QP // QB

            def __init__(self, stack, name, pad, counts):
                lsb = maker(stack, "sb")
                self.counts = counts
                self.low = lsb(f"low_{name}", [P, QP])
                self.high = lsb(f"high_{name}", [P, QP])
                self.raw = lsb(f"raw_{name}", [P, QP], I32)
                self.part = lsb(f"part_{name}", [P, QP], I32)
                self.hot_low = lsb(f"hot_low_{name}", [P, 2, QB, P], BF16)
                self.hot_high = lsb(f"hot_high_{name}", [P, 2, QB, T], BF16)
                self.hot_zero = lsb(f"hot_zero_{name}", [P, P], BF16)
                self.made, self.summed_up = sem(f"made_{name}"), sem(f"summed_up_{name}")
                chain.step(dve, lambda: dve.memset(self.hot_zero[:, :], 0.0))
                chain.dma(sp, lambda: sp.dma_start(self.raw[:, :], pad[FRONT:FRONT + P * QP].rearrange("(p j) -> p j", j=QP)))

            def open(self):
                raw, part, zero = self.raw[:, :], self.part[:, :], self.hot_zero
                chain.step(dve, lambda: dve.tensor_scalar(part, raw, P - 1, None, ALU.bitwise_and))
                chain.step(dve, lambda: dve.tensor_copy(self.low[:, :], part))
                chain.step(dve, lambda: dve.tensor_scalar(part, raw, 7, None, ALU.logical_shift_right))
                chain.step(dve, lambda: dve.tensor_copy(self.high[:, :], part))
                chain.step(pe, lambda: pe.matmul(self.counts, zero[:, :], zero[:, 0:T], start=True, stop=False,
                                                 skip_group_check=True))
                chain.wait(dve)
                pe.sem_inc(self.summed_up, 2)

            def one_hots(self, n, b):
                dve.wait_ge(self.summed_up, n + 1)
                for hot, of, width in ((self.hot_low, self.low, P), (self.hot_high, self.high, T)):
                    dve.tensor_tensor(hot[:, b, :, :], iota[:, 0:width].unsqueeze(1).broadcast_to([P, QB, width]),
                                      of[:, ds(n * QB, QB)].unsqueeze(2).broadcast_to([P, QB, width]),
                                      ALU.is_equal).then_inc(self.made, 1)

            def products(self, n, b):
                pe.wait_ge(self.made, 2 * n + 2)
                for k in range(QB):
                    mm = pe.matmul(self.counts, self.hot_low[:, b, k, :], self.hot_high[:, b, k, :],
                                   start=False, stop=False, skip_group_check=True)
                mm.then_inc(self.summed_up, 1)

            def close(self, count):
                dve.wait_ge(self.summed_up, self.GROUPS + 2)
                chain.step(dve, lambda: dve.tensor_copy(count[:, :], self.counts))
                for e in (sp, pe, dve):
                    chain.wait(e)

        def rank_nodes():
            with ExitStack() as local:
                lsb = maker(local, "sb")
                key = lsb("key", [P, T])
                noise = lsb("noise", [P, T])
                with nc.allow_non_contiguous_dma(reason="a vector by node onto the partitions"):
                    chain.step(dve, lambda: dve.memset(noise[:, :], 0.0))
                    chain.dma(sp, lambda: sp.dma_start(noise[:, 0:T - 1], a["node_vec"][0:(T - 1) * P].rearrange("(t p) -> p t", p=P)),
                              lambda: sp.dma_start(noise[0:TAIL, T - 1:T], a["node_vec"][(T - 1) * P:N].rearrange("(p o) -> p o", o=1)))
                    chain.step(dve, lambda: dve.tensor_tensor(key[:, :], count_out[:, :], noise[:, :], ALU.add))
                    padl = lsb("padl", [P, 1])
                    chain.step(dve, lambda: dve.tensor_scalar(padl[:, :], lane[:, :], float(TAIL), BIG, ALU.is_ge, ALU.mult))
                    chain.step(dve, lambda: dve.tensor_tensor(key[:, T - 1:T], key[:, T - 1:T], padl[:, :], ALU.add))
                    chain.dma(sp, lambda: sp.dma_start(key_row.rearrange("(t p) -> p t", p=P), key[:, :]))
                keys = lsb("keys", [P, NP])
                junk = lsb("junk", [P, NP], BF16)
                eq = lsb("eq", [P, P])
                tri_low = lsb("tri_low", [P, P])
                parts = lsb("parts", [P, T, 4])
                rank_f = lsb("rank_f", [P, T])
                chain.dma(sp, lambda: sp.dma_start(keys[:, :], key_row.partition_broadcast(P)))
                chain.step(dve, lambda: dve.memset(parts[:, :, :], 0.0))
                chain.step(dve, lambda: dve.tensor_scalar(tri_low[:, :], iota[:, :], lane[:, 0:1], None, ALU.is_lt))
                for t in range(T):
                    own = key[:, t:t + 1]
                    if t:
                        chain.step(dve, lambda: dve.tensor_scalar(junk[:, 0:t * P], keys[:, 0:t * P], own, None, ALU.is_le,
                                                                  ALU.add, accum_out=parts[:, t, 0:1]))
                    chain.step(dve, lambda: dve.tensor_scalar(junk[:, t * P:NP], keys[:, t * P:NP], own, None, ALU.is_lt,
                                                              ALU.add, accum_out=parts[:, t, 1:2]))
                    chain.step(dve, lambda: dve.scalar_tensor_tensor(eq[:, :], keys[:, t * P:(t + 1) * P], own, tri_low[:, :],
                                                                     ALU.is_equal, ALU.mult, accum_out=parts[:, t, 2:3]))
                chain.step(dve, lambda: dve.tensor_reduce(rank_f[:, :], parts[:, :, :], AX, ALU.add))
                chain.step(dve, lambda: dve.tensor_copy(rank_i[:, :], rank_f[:, :]))
                for e in (sp, dve):
                    chain.wait(e)

        def layer_norm(ch, x3, out3, stat, relu=False, gain=None, shift=None):
            g = x3.shape[1]
            mean, var = stat[:, 0:g, 6], stat[:, 0:g, 7]
            bc = lambda v: v[:, :].unsqueeze(1).broadcast_to([P, g, D])
            yield ch.apart(*[(dve, lambda b=b: dve.bn_stats(stat[:, b, 0:6], x3[:, b, :])) for b in range(g)])
            yield ch.step(dve, lambda: dve.sem_inc(dve_passed, 1),
                          *[lambda b=b: dve.bn_aggr(stat[:, b, 6:8], stat[:, b, 0:6]) for b in range(g)])
            yield ch.step(act, lambda: act.activation(var, var, ACT.Sqrt, bias=eps[:, 0:1]))
            yield ch.step(dve, lambda: dve.reciprocal(var, var))
            yield ch.step(dve, lambda: dve.scalar_tensor_tensor(mean, mean, -1.0, var, ALU.mult, ALU.mult))
            yield ch.step(act, *[lambda b=b: act.activation(out3[:, b, :], x3[:, b, :], ACT.Relu if relu else ACT.Identity,
                                                            scale=stat[:, b, 7:8], bias=stat[:, b, 6:7]) for b in range(g)])
            if gain is not None:
                yield ch.step(dve, lambda: dve.tensor_tensor(out3, out3, bc(gain), ALU.mult))
                yield ch.step(dve, lambda: dve.tensor_tensor(out3, out3, bc(shift), ALU.add))

        def turn_blocks(ch, dst4, src3, ps):
            for b in range(0, src3.shape[1], 2):
                m = min(2, src3.shape[1] - b)
                yield ch.step(pe, *[lambda k=k, c=c: pe.transpose(ps[:, c, k, :], src3[:, b + k, c * P:(c + 1) * P], ident[:, :])
                                    for k in range(m) for c in range(2)])
                yield ch.step(act, lambda: act.activation(dst4[:, :, b:b + m, :], ps[:, :, 0:m, :], ACT.Copy))

        def elu(ch, x, tmp, out):
            yield ch.step(dve, lambda: dve.tensor_scalar(tmp, x, 0.0, None, ALU.min))
            yield ch.step(act, lambda: act.activation(tmp, tmp, ACT.Exp))
            yield ch.step(dve, lambda: dve.tensor_scalar(tmp, tmp, -1.0, None, ALU.add))
            yield ch.step(dve, lambda: dve.scalar_tensor_tensor(out, x, 0.0, tmp, ALU.max, ALU.add))

        def one_by_one(steps):
            for _ in steps:
                pass

        class SegmentMax:

            def __init__(self, stack, name, scores, heads):
                lsb = maker(stack, "sb")
                self.name, self.scores, self.heads = name, scores, heads
                self.mine = lsb(f"mine_{name}", [P, QP, heads])
                self.src_q = lsb(f"src_q_{name}", [P, QP], I32)
                self.dst_q = lsb(f"dst_q_{name}", [P, QP + 1], I32)
                self.idx = lsb(f"idx_{name}", [P, 2, QB], I32)
                self.got = lsb(f"got_{name}", [P, 2, QB, heads])
                self.arrived = [sem(f"arrived_{name}{b}") for b in range(2)]
                self.picked, self.kept = sem(f"picked_{name}"), sem(f"kept_{name}")
                chain.dma(sp,
                          lambda: sp.dma_start(self.src_q[:, :], src_pad[FRONT:FRONT + P * QP].rearrange("(p j) -> p j", j=QP)),
                          lambda: sp.dma_start(self.dst_q[:, :], at(dst_pad, 0, [[QP, P], [1, QP + 1]])))
                chain.wait(pool)
                pool.sem_inc(self.kept, 2)

            def gather(self, first, count):
                def issue(n, b):
                    pool.tensor_copy(self.idx[:, b, :], self.src_q[:, ds(n * QB, QB)]).then_inc(self.picked, 1)
                    pool.wait_ge(self.picked, n + 1)
                    pool.wait_ge(self.kept, n + 1)
                    pool.sem_inc(passed, 1)
                    for k in range(QB):
                        pool.indirect_dma_start(self.got[:, b, k, :], None, self.scores,
                                                bass.IndirectOffsetOnAxis(self.idx[:, b, k:k + 1], 0)
                                                ).then_inc(self.arrived[b], 16)

                def store(n, half, b):
                    pool.wait_ge(self.arrived[b], 16 * QB * (half + 1))
                    pool.tensor_copy(self.mine[:, ds(n * QB, QB), :], self.got[:, b, :, :]).then_inc(self.kept, 1)

                h0 = first // 2
                issue(first, 0)
                with pool.Fori(0, count // 2 - 1) as i:
                    n = 2 * i + first
                    issue(n + 1, 1)
                    store(n, i + h0, 0)
                    issue(n + 2, 0)
                    store(n + 1, i + h0, 1)
                n, h = first + count - 2, h0 + count // 2 - 1
                issue(n + 1, 1)
                store(n, h, 0)
                store(n + 1, h, 1)

            def finish(self, best):
                name, heads, mine, dst_q = self.name, self.heads, self.mine, self.dst_q
                with ExitStack() as local:
                    lsb, lps = maker(local, "sb"), maker(local, "ps")
                    same = lsb(f"same_{name}", [P, QP])
                    fresh = lsb(f"fresh_{name}", [P, 1])
                    side = lsb(f"side_{name}", [P, 16])
                    side_t = lsb(f"side_t_{name}", [16, 3, P])
                    carry = lsb(f"carry_{name}", [P, 16])
                    side_ps = lps(f"side_ps_{name}", [P, 2, P])
                    dve.wait_ge(self.kept, QP // QB + 2)
                    chain.step(dve, lambda: dve.tensor_tensor(same[:, :], dst_q[:, 1:QP + 1], dst_q[:, 0:QP], ALU.not_equal))
                    chain.step(dve, lambda: dve.tensor_reduce(fresh[:, :], same[:, :], AX, ALU.max))
                    chain.step(dve, lambda: dve.tensor_scalar(same[:, :], same[:, :], -BIG, None, ALU.mult))
                    chain.apart(*[(dve, lambda h=h: dve.tensor_tensor_scan(mine[:, :, h], same[:, :], mine[:, :, h], -BIG,
                                                                           ALU.add, ALU.max)) for h in range(heads)])
                    chain.step(dve, lambda: dve.memset(side[:, :], 0.0))
                    chain.step(dve, lambda: dve.tensor_copy(side[:, 0:heads], mine[:, QP - 1, :]))
                    chain.step(pe, lambda: pe.transpose(side_ps[0:16, 0, :], side[:, :], ident[:, :]))
                    chain.step(dve, lambda: dve.tensor_copy(side_t[:, 0, :], side_ps[0:16, 0, :]))
                    chain.step(dve, lambda: dve.tensor_scalar(side[:, :], ones[:, 0:16], fresh[:, 0:1], -BIG, ALU.mult, ALU.mult))
                    chain.step(pe, lambda: pe.transpose(side_ps[0:16, 1, :], side[:, :], ident[:, :]))
                    chain.step(dve, lambda: dve.tensor_copy(side_t[:, 1, :], side_ps[0:16, 1, :]))
                    chain.step(dve, lambda: dve.memset(side_t[:, 2, 0:1], -BIG))
                    chain.step(dve, lambda: dve.tensor_tensor_scan(side_t[:, 0, :], side_t[:, 1, :], side_t[:, 0, :], -BIG,
                                                                   ALU.add, ALU.max))
                    chain.step(dve, lambda: dve.tensor_copy(side_t[:, 2, 1:P], side_t[:, 0, 0:P - 1]))
                    chain.step(pe, lambda: pe.transpose(side_ps[:, 0, 0:16], side_t[:, 2, :], ident[0:16, 0:16]))
                    chain.step(dve, lambda: dve.tensor_copy(carry[:, :], side_ps[:, 0, 0:16]))
                    chain.apart(*[(dve, lambda h=h: dve.tensor_tensor_scan(mine[:, :, h], same[:, :], mine[:, :, h],
                                                                           carry[:, h:h + 1], ALU.add, ALU.max))
                                  for h in range(heads)])
                    run = at(running, 0, [[QP * heads, P], [1, QP * heads]])
                    chain.dma(sp, lambda: sp.dma_start(run, mine[:, :, :].rearrange("p j h -> p (j h)")))
                    table_run = at(running, 0, [[heads, P * QP], [1, heads]])
                    chain.gathers(pool, [lambda t=t: pool.indirect_dma_start(
                        best[:, t, :], None, table_run, bass.IndirectOffsetOnAxis(last_edge[:, t:t + 1], 0)) for t in range(T)],
                        sem(f"read_{name}"), 16 * T)
                    for e in (sp, pe, dve):
                        chain.wait(e)

        class EdgePass:

            ROUNDS = UNITS // UB

            def __init__(self, stack, name, width, heads=0, act_heads=0, slope=0.0, weighted=False, tab=None, tab_dst=None):
                lsb, lps = maker(stack, "sb"), maker(stack, "ps")
                full = width + heads
                self.width, self.heads, self.slope, self.weighted = width, heads, slope, weighted
                self.full, self.tab, self.tab_dst = full, tab, tab_dst
                self.dve_heads = heads - act_heads
                assert UNITS % UB == 0 and UB % SB == 0
                self.rows = lsb(f"rows_{name}", [P, UB, 2, full])
                self.hot = lsb(f"hot_{name}", [P, UB, 2, P])
                self.sums = lsb(f"sums_{name}", [P, SB, full])
                self.idx = lsb(f"idx_{name}", [P, 2, UB // 2, 2], I32)
                if heads:
                    self.rel = lsb(f"rel_{name}", [P, UB, UE])
                    self.spread = lsb(f"spread_{name}", [P, UB, UE])
                    self.at_node = lsb(f"at_node_{name}", [P, UB, 2 * heads])
                    self.score = lsb(f"score_{name}", [P, UB, 2, heads])
                    self.ex = lps(f"ex_{name}", [P, 2, 512])
                self.acc = lps(f"acc_{name}", [P, 2, -(-full // 512) * 512])
                self.splits = [(a0, min(a0 + 512, full)) for a0 in range(0, full, 512)]
                self.landed = [sem(f"landed_{name}{v}") for v in range(UB)]
                self.stored = [sem(f"stored_{name}{v}") for v in range(SB)]
                self.beside = [sem(f"beside_{name}{v}") for v in range(UB)] if heads else None
                self.s_idx, self.s_hot, self.s_pe, self.s_sum = (sem(f"{n}_{name}") for n in ("idx", "hot", "pe", "sum"))
                if heads:
                    self.s_spread, self.s_ex, self.s_score, self.s_exp, self.s_mul, self.s_act = (
                        sem(f"{n}_{name}") for n in ("spread", "ex", "score", "exp", "mul", "act"))
                    pe.sem_inc(self.s_ex, UB)
                self.lag = 3 if heads else 2
                pe.sem_inc(self.s_pe, UB)
                dve.sem_inc(self.s_sum, 2)
                for v in range(SB):
                    sp.sem_inc(self.stored[v], 16)
                chain.step(dve, lambda: dve.memset(self.sums[:, SB - 1, :], 0.0))
                chain.wait(dve)
                if heads:
                    for v in range(UB // 2):
                        self.load_beside(0, v)

            def pool_half(self, i, half):
                v0 = half * (UB // 2)
                for v in range(v0, v0 + UB // 2):
                    pool.wait_ge(self.landed[v], 32 * i)
                pool.tensor_copy(self.idx[:, half, :, :], unit_src[:, ds(i * UB + v0, UB // 2), :]).then_inc(self.s_idx, 1)
                pool.wait_ge(self.s_idx, 2 * i + half + 1)
                for v in range(v0, v0 + UB // 2):
                    pool.wait_ge(self.s_pe, i * UB + v + 1)
                    pool.sem_inc(passed, 1)
                    for e in range(2):
                        pool.indirect_dma_start(self.rows[:, v, e, :], None, self.tab,
                                                bass.IndirectOffsetOnAxis(self.idx[:, half, v - v0, e:e + 1], 0)
                                                ).then_inc(self.landed[v], 16)

            def pool_round(self, i):
                self.pool_half(i, 0)
                self.pool_half(i, 1)

            def load_beside(self, i, v):
                u = i * UB + v
                block = sp.value_load(unit_at[0:1, ds(u, 1)], min_val=0, max_val=T)
                sp.wait_ge(self.s_ex, u + 1)
                sp.dma_start(self.rel[:, v, :], rel_rows[ds(u * UE, UE)].partition_broadcast(P)).then_inc(self.beside[v], 16)
                sp.dma_start(self.at_node[:, v, :], self.tab_dst[ds(block * P, P), :]).then_inc(self.beside[v], 16)

            def store_sums(self, i, v):
                u = i * UB + v
                block = sp.value_load(unit_block[0:1, ds(u, 1)], min_val=0, max_val=SKIP)
                sp.wait_ge(self.s_sum, u + 3)
                sp.dma_start(summed[:, 0:self.full][ds(block * P, P), :], self.sums[:, v % SB, :],
                             cond=(block < SKIP)).then_inc(self.stored[v % SB], 16)

            def sp_slot(self, i, v, first=False):
                half = UB // 2
                if self.heads:
                    self.load_beside(i if v + half < UB else i + 1, (v + half) % UB)
                if not (first and v < half):
                    self.store_sums(i if v >= half else i - 1, (v - half) % UB)

            def spread_hot(self, i, v):
                u = i * UB + v
                dve.wait_ge(self.beside[v], 32 * (i + 1))
                dve.wait_ge(self.s_ex, u + 1)
                dve.tensor_scalar(self.spread[:, v, :], self.rel[:, v, :], lane[:, 0:1], None,
                                  ALU.is_equal).then_inc(self.s_spread, 1)

            def one_hot(self, i, v):
                u = i * UB + v
                dve.wait_ge(self.s_pe, u + 1)
                wide = lambda w: w[:, ds(u, 1), :].rearrange("p o e -> p (o e)").unsqueeze(2).broadcast_to([P, 2, P])
                dve.tensor_tensor(self.hot[:, v, :, :], iota[:, :].unsqueeze(1).broadcast_to([P, 2, P]), wide(unit_rel),
                                  ALU.is_equal).then_inc(self.s_hot, 1)
                if self.weighted:
                    dve.wait_ge(self.s_hot, 2 * u + 1)
                    dve.tensor_tensor(self.hot[:, v, :, :], self.hot[:, v, :, :], wide(unit_w), ALU.mult).then_inc(self.s_hot, 1)

            def of_node(self, v):
                return self.ex[:, v % 2, 0:4 * self.heads].rearrange("p (e h) -> p e h", e=2)

            def add_scores(self, i, v):
                u, score = i * UB + v, self.score[:, v, :, :]
                dve.wait_ge(self.landed[v], 32 * (i + 1))
                dve.wait_ge(self.s_ex, u + UB + 1)
                dve.tensor_tensor(score, self.rows[:, v, :, self.width:], self.of_node(v)[:, :, 0:self.heads],
                                  ALU.add).then_inc(self.s_score, 1)

            def leaky(self, i, v):
                score = self.score[:, v, :, :]
                dve.wait_ge(self.s_score, 3 * (i * UB + v) + 1)
                dve.scalar_tensor_tensor(score, score, self.slope, score, ALU.mult, ALU.max).then_inc(self.s_score, 1)

            def less_maximum(self, i, v):
                score = self.score[:, v, :, :]
                dve.wait_ge(self.s_score, 3 * (i * UB + v) + 2)
                dve.tensor_tensor(score, score, self.of_node(v)[:, :, self.heads:2 * self.heads],
                                  ALU.subtract).then_inc(self.s_score, 1)

            def weigh(self, i, v):
                n = self.dve_heads
                if n:
                    dve.wait_ge(self.s_exp, i * UB + v + 1)
                    r = self.rows[:, v, :, 0:n * DH].rearrange("p e (h d) -> p e h d", d=DH)
                    by = self.rows[:, v, :, self.width:self.width + n]
                    dve.tensor_tensor(r, r, by.unsqueeze(3).broadcast_to([P, 2, n, DH]), ALU.mult).then_inc(self.s_mul, 1)

            def collect(self, i, v):
                u = i * UB + v
                dve.wait_ge(self.s_pe, u + UB + 1)
                if isinstance(i, int):
                    dve.wait_ge(self.stored[v % SB], 16 * (u // SB + 1))
                else:
                    dve.wait_ge(self.stored[v % SB], 16 * (UB // SB * i + v // SB + 1))
                dve.wait_ge(self.s_sum, u + 2)
                dve.scalar_tensor_tensor(self.sums[:, v % SB, :], self.sums[:, (v - 1) % SB, :], unit_keep[:, ds(u, 1)],
                                         self.acc[:, v % 2, 0:self.full], ALU.mult, ALU.add).then_inc(self.s_sum, 1)

            def behind(self, part, lag, i, v, first):
                if not (first and v < lag):
                    part(i if v >= lag else i - 1, (v - lag) % UB)

            def dve_slot(self, i, v, first=False):
                if self.heads:
                    self.behind(self.add_scores, 1, i, v, first)
                    self.spread_hot(i, v)
                    self.behind(self.leaky, 1, i, v, first)
                self.one_hot(i, v)
                if self.heads:
                    self.behind(self.less_maximum, 1, i, v, first)
                    self.behind(self.weigh, 2, i, v, first)
                self.behind(self.collect, self.lag, i, v, first)

            def weights(self, i, v):
                act.wait_ge(self.s_score, 3 * (i * UB + v) + 3)
                act.activation(self.rows[:, v, :, self.width:], self.score[:, v, :, :], ACT.Exp).then_inc(self.s_exp, 1)

            def weigh_rest(self, i, v):
                act.wait_ge(self.s_exp, i * UB + v + 1)
                for e in range(2):
                    for h in range(self.dve_heads, self.heads):
                        r = self.rows[:, v, e, h * DH:(h + 1) * DH]
                        last = act.activation(r, r, ACT.Copy, scale=self.rows[:, v, e, self.width + h:self.width + h + 1])
                last.then_inc(self.s_act, 1)

            def act_slot(self, i, v, first=False):
                self.behind(self.weights, 1, i, v, first)
                self.behind(self.weigh_rest, 1, i, v, first)

            def spread_values(self, i, v):
                u = i * UB + v
                pe.wait_ge(self.s_spread, u + 1)
                if not isinstance(u, int) or u >= 2:
                    pe.wait_ge(self.s_score, 3 * (u - 2) + 3)
                for e in range(2):
                    mm = pe.matmul(self.of_node(v)[:, e, :], self.spread[:, v, e * P:(e + 1) * P], self.at_node[:, v, :],
                                   start=True, stop=True)
                mm.then_inc(self.s_ex, 1)

            def sum_rows(self, i, v):
                u = i * UB + v
                if self.heads:
                    pe.wait_ge(self.s_act, u + 1)
                    if self.dve_heads:
                        pe.wait_ge(self.s_mul, u + 1)
                else:
                    pe.wait_ge(self.landed[v], 32 * (i + 1))
                pe.wait_ge(self.s_hot, (2 if self.weighted else 1) * (u + 1))
                pe.wait_ge(self.s_sum, u + 1)
                for a0, a1 in self.splits:
                    for e in range(2):
                        mm = pe.matmul(self.acc[:, v % 2, a0:a1], self.hot[:, v, e, :], self.rows[:, v, e, a0:a1],
                                       start=(e == 0), stop=(e == 1))
                mm.then_inc(self.s_pe, 1)

            def pe_slot(self, i, v, first=False):
                if self.heads:
                    self.spread_values(i, v)
                self.behind(self.sum_rows, 2 if self.heads else 0, i, v, first)

            def rounds(self, first, count):
                slots = [(sp, self.sp_slot), (dve, self.dve_slot), (pe, self.pe_slot)]
                slots += [(act, self.act_slot)] if self.heads else []
                start = first
                if first == 0:
                    self.pool_round(0)
                    for e, slot in slots:
                        for v in range(UB):
                            slot(0, v, True)
                    start = 1
                if start < first + count:
                    with pool.Fori(start, first + count) as i:
                        self.pool_round(i)
                    for e, slot in slots:
                        with e.Fori(start, first + count) as i:
                            for v in range(UB):
                                slot(i, v)

            def end(self):
                n = self.ROUNDS
                if self.heads:
                    for part in (self.add_scores, self.leaky, self.less_maximum, self.weights, self.weigh_rest):
                        part(n - 1, UB - 1)
                    for v in (UB - 2, UB - 1):
                        self.weigh(n - 1, v)
                        self.sum_rows(n - 1, v)
                for v in range(UB - self.lag, UB):
                    self.collect(n - 1, v)
                for v in range(UB // 2):
                    self.store_sums(n - 1, UB // 2 + v)
                for v in range(SB):
                    sp.wait_ge(self.stored[v], 16 * (UNITS // SB + 1))
                if self.heads:
                    for v in range(UB // 2):
                        sp.wait_ge(self.beside[v], 32 * (n + 1))
                nc.all_engine_barrier()

        def edge_pass(name, width, **options):
            with ExitStack() as local:
                edges = EdgePass(local, name, width, **options)
                edges.rounds(0, EdgePass.ROUNDS)
                edges.end()

        def own_and_max(score_at_, best_, heads, slope):
            chain.step(dve, lambda: dve.tensor_tensor(best_, best_, score_at_[:, :, 0:heads], ALU.add))
            chain.step(dve, lambda: dve.scalar_tensor_tensor(score_at_[:, :, heads:2 * heads], best_, slope, best_,
                                                             ALU.mult, ALU.max))

        stack0 = ExitStack()
        s0 = maker(stack0, "sb")
        hT = s0("hT", [P, 2, NP])
        score_at = s0("score_at", [P, T, 2 * L * H])
        channel = s0("channel", [P, 3, 2])
        mean, var, msq = channel[:, 0, :], channel[:, 1, :], channel[:, 2, :]
        with ExitStack() as local:
            lsb, lps = maker(local, "sb"), maker(local, "ps")
            xg = lsb("xg", [P, GB, D])
            hg = lsb("hg", [P, GB, D])
            sq = lsb("sq", [P, GB, D])
            stat = lsb("stat", [P, LANES, 2, 8])
            added = lps("added", [P, 512])
            moments = added[:, 0:4].rearrange("p (c q) -> p c q", q=2)
            turn = lps("turn", [P, LANES, 2, 2, P])
            moment = lsb("moment", [P, 2, 2])
            chain.dma(sp, lambda: sp.dma_start(x_dram[0:N, :], a["x"][:, :]),
                      lambda: sp.dma_start(x_dram[N:NP, :], zeros[0:NP - N, 0:D]))
            chain.step(pe, *[lambda k=k: pe.matmul(moments[:, k, :], zeros[:, 0:P], zeros[:, 0:2], start=(k == 0), stop=False,
                                                   skip_group_check=True) for k in range(2)])
            targets = NodeCount(local, "dst", dst_pad, added[:, 64:64 + T])
            targets.open()
            for e in (sp, pool):
                chain.wait(e)
            per_round = -(-NodeCount.GROUPS * GB // T // 2) * 2

            def count_beside(i):
                n = min(per_round, NodeCount.GROUPS - per_round * i) if isinstance(i, int) else per_round
                for k in range(n):
                    targets.one_hots(i * per_round + k, k % 2)
                    targets.products(i * per_round + k, k % 2)
                    yield

            def norm_stage(ch, g, k, lo, m):
                x3, h3, s3 = xg[:, lo:lo + m, :], hg[:, lo:lo + m, :], sq[:, lo:lo + m, :]
                yield ch.move(lambda e: e.dma_start(x3, per_block(x_dram)[:, ds(g * GB + lo, m), :]))
                yield from layer_norm(ch, x3, h3, stat[:, k, :, :], relu=True)
                yield ch.step(act, lambda: act.activation(s3, h3, ACT.Square))
                yield ch.step(pe, *[lambda c=c, q=q, v=v, b=b: pe.matmul(
                    moments[:, c, q:q + 1], v[:, b, c * P:(c + 1) * P], ones[:, 0:1], start=False, stop=False,
                    skip_group_check=True) for q, v in enumerate((h3, s3)) for b in range(m) for c in range(2)])
                yield from turn_blocks(ch, hT[:, :, ds((g * GB + lo) * P, m * P)].rearrange("p c (b n) -> p c b n", n=P), h3,
                                       turn[:, k, :, :, :])

            in_lanes(nc, lanes, 80, 1, norm_stage, beside=count_beside)
            for e in (dve, pe):
                for c in lanes:
                    c.wait(e)
            targets.close(count_in)
            chain.step(dve, lambda: dve.tensor_scalar(moment[:, :, :], moments[:, :, :], 1.0 / N, None, ALU.mult))
            chain.step(dve, lambda: dve.tensor_copy(mean, moment[:, :, 0]))
            chain.step(dve, lambda: dve.tensor_tensor(msq, mean, mean, ALU.mult))
            chain.step(dve, lambda: dve.tensor_tensor(var, moment[:, :, 1], msq, ALU.subtract))
            chain.step(dve, lambda: dve.tensor_scalar(var, var, 0.0, 1e-5, ALU.max, ALU.add))
            chain.step(act, lambda: act.activation(var, var, ACT.Sqrt))
            chain.step(dve, lambda: dve.reciprocal(var, var))
            fresh_chain("chain_schedule")

        with ExitStack() as local:
            lsb, lps = maker(local, "sb"), maker(local, "ps")
            tri = lsb("tri", [P, P])
            per_t = lsb("per_t", [P, T])
            upto_t = lsb("upto_t", [P, T])
            units_t = lsb("units_t", [P, T])
            units_i = lsb("units_i", [P, T], I32)
            upto_u = lsb("upto_u", [P, T])
            delta = lsb("delta", [P, T])
            pair = lsb("pair", [P, 2, T])
            cols = lsb("cols", [P, 2])
            ones_t = lsb("ones_t", [P, T])
            within = lsb("within", [P, T])
            unit_no = lsb("unit_no", [P, UC])
            past = lsb("past", [P, UC])
            chunk_first = lsb("chunk_first", [P, UC // P])
            block_f = lsb("block_f", [P, UC // P])
            start_f = lsb("start_f", [P, UC // P])
            start_i = lsb("start_i", [P, UC // P], I32)
            rel0 = lsb("rel0", [P, UC // P])
            row_block = lsb("row_block", [P, UC + 1])
            finished = lsb("finished", [P, UC])
            got_i = lsb("got_i", [P, 2, UE], I32)
            got_w = lsb("got_w", [P, UE])
            got_f = lsb("got_f", [P, 2, UE])
            turned = lps("turned", [P, 8, P])
            cut = sem("units_cut")
            small = lps("small", [P, 512])
            row_ps = lps("row_ps", [P, 512])

            chain.apart((dve, lambda: dve.tensor_scalar(tri[:, :], iota[:, :], lane[:, 0:1], None, ALU.is_ge)),
                       (dve, lambda: dve.memset(ones_t[:, :], 1.0)),
                       (pool, lambda: pool.iota(unit_no[:, :], [[1, UC]], base=0, channel_multiplier=0,
                                                allow_small_or_imprecise_dtypes=True)),
                       (pool, lambda: pool.iota(chunk_first[:, :], [[P, UC // P]], base=0, channel_multiplier=1,
                                                allow_small_or_imprecise_dtypes=True)))
            chain.step(pe, lambda: pe.matmul(small[:, 0:T], ones[:, :], count_in[:, :], start=True, stop=True))
            chain.step(pe, lambda: pe.matmul(small[:, 64:64 + T], tri[:, :], count_in[:, :], start=True, stop=True))
            chain.step(dve, lambda: dve.tensor_copy(per_t[:, :], small[:, 0:T]))
            chain.step(dve, lambda: dve.tensor_tensor_scan(upto_t[:, :], ones_t[:, :], per_t[:, :], 0.0, ALU.mult, ALU.add))
            chain.step(dve, lambda: dve.tensor_tensor(within[:, :], upto_t[:, :], per_t[:, :], ALU.subtract))
            chain.step(dve, lambda: dve.tensor_tensor(within[:, :], within[:, :], small[:, 64:64 + T], ALU.add))
            chain.step(dve, lambda: dve.tensor_scalar(within[:, :], within[:, :], -1.0, 0.0, ALU.add, ALU.max))
            chain.step(dve, lambda: dve.tensor_copy(last_edge[:, :], within[:, :]))
            chain.step(dve, lambda: dve.tensor_scalar(units_t[:, :], per_t[:, :], float(UE - 1), None, ALU.add))
            chain.step(dve, lambda: dve.tensor_copy(units_i[:, :], units_t[:, :]))
            chain.step(dve, lambda: dve.tensor_scalar(units_i[:, :], units_i[:, :], 8, None, ALU.logical_shift_right))
            chain.step(dve, lambda: dve.tensor_copy(units_t[:, :], units_i[:, :]))
            chain.step(dve, lambda: dve.tensor_tensor_scan(upto_u[:, :], ones_t[:, :], units_t[:, :], 0.0, ALU.mult, ALU.add))
            chain.step(dve, lambda: dve.scalar_tensor_tensor(delta[:, :], units_t[:, :], -float(UE), per_t[:, :],
                                                             ALU.mult, ALU.add))
            for k, v in enumerate((upto_u, delta)):
                chain.step(dve, lambda: dve.tensor_tensor(pair[:, k, :], v[:, :], ident[:, 0:T], ALU.mult))
                chain.step(dve, lambda: dve.tensor_reduce(cols[:, k:k + 1], pair[:, k, :], AX, ALU.add))
            chain.step(dve, lambda: dve.tensor_scalar(past[:, :], unit_no[:, :], cols[:, 0:1], None, ALU.is_ge))
            chain.step(dve, lambda: dve.memset(cols[:, 0:1], 1.0))
            chain.step(pe, *[lambda c=c: pe.matmul(small[:, 128 + 2 * c:130 + 2 * c], past[0:T, c * P:(c + 1) * P],
                                                   cols[0:T, :], start=True, stop=True) for c in range(UC // P)])
            chain.step(pe, lambda: pe.matmul(row_ps[:, :], ones[0:T, :], past[0:T, :], start=True, stop=True))
            by_chunk = small[:, 128:128 + 2 * (UC // P)].rearrange("p (c k) -> p k c", k=2)
            chain.step(dve, lambda: dve.tensor_copy(block_f[:, :], by_chunk[:, 0, :]))
            chain.step(dve, lambda: dve.scalar_tensor_tensor(start_f[:, :], chunk_first[:, :], float(UE), by_chunk[:, 1, :],
                                                             ALU.mult, ALU.add))
            chain.step(dve, lambda: dve.tensor_scalar(start_f[:, :], start_f[:, :], float(E), float(FRONT), ALU.min, ALU.add))
            chain.step(dve, lambda: dve.tensor_copy(start_i[:, :], start_f[:, :]))
            chain.step(dve, lambda: dve.tensor_scalar(rel0[:, :], block_f[:, :], -float(P), None, ALU.mult))
            chain.apart((dve, lambda: dve.tensor_copy(row_block[:, 0:UC], row_ps[:, :])),
                       (dve, lambda: dve.memset(row_block[:, UC:UC + 1], float(T))))
            chain.step(dve, lambda: dve.memset(unit_keep[:, 0:1], 0.0))
            chain.step(dve, lambda: dve.tensor_tensor(unit_keep[:, 1:UC], row_block[:, 1:UC], row_block[:, 0:UC - 1],
                                                      ALU.is_equal))
            chain.step(dve, lambda: dve.tensor_tensor(finished[:, :], row_block[:, 1:UC + 1], row_block[:, 0:UC],
                                                      ALU.is_equal))
            chain.step(dve, lambda: dve.scalar_tensor_tensor(finished[:, :], finished[:, :], float(SKIP), row_block[:, 0:UC],
                                                             ALU.mult, ALU.add))
            chain.step(dve, lambda: dve.tensor_scalar(finished[:, :], finished[:, :], float(SKIP), None, ALU.min))
            chain.step(dve, lambda: dve.tensor_copy(unit_block[:, :], finished[0:1, :]))
            chain.step(dve, lambda: dve.tensor_copy(unit_at[:, :], row_block[0:1, 0:UC]))
            for c in range(UC // P):
                idx = bass.IndirectOffsetOnAxis(start_i[:, c:c + 1], 0)
                col = lambda v: v.rearrange("(n o) -> n o", o=1)
                chain.gathers(pool, [
                    lambda: pool.indirect_dma_start(got_i[:, 0, :], None, col(src_pad), idx),
                    lambda: pool.indirect_dma_start(got_i[:, 1, :], None, col(dst_pad), idx),
                    lambda: pool.indirect_dma_start(got_w[:, :], None, col(w_pad), idx)], cut, 3 * 16 * (c + 1))
                chain.step(dve, lambda: dve.tensor_copy(got_f[:, :, :], got_i[:, :, :]))
                chain.step(pe, *[lambda k=k, v=v, h=h: pe.transpose(turned[:, 2 * k + h, :], v[:, h * P:(h + 1) * P],
                                                                    ident[:, :])
                                 for k, v in ((0, got_f[:, 0, :]), (2, got_w)) for h in range(2)])
                to = slice(c * P, (c + 1) * P)
                chain.apart(*[(dve, lambda k=k, v=v: dve.tensor_copy(
                    v[:, to, :].rearrange("p u h -> p h u"), turned[:, 2 * k:2 * k + 2, :]))
                    for k, v in ((0, unit_src), (2, unit_w))])
                chain.step(dve, lambda: dve.tensor_scalar(got_f[:, 1, :], got_f[:, 1, :], rel0[:, c:c + 1], None, ALU.add))
                chain.dma(sp, lambda: sp.dma_start(rel_rows.rearrange("(u e) -> u e", e=UE)[to, :], got_f[:, 1, :]))
                chain.step(pe, *[lambda h=h: pe.transpose(turned[:, h, :], got_f[:, 1, h * P:(h + 1) * P], ident[:, :])
                                 for h in range(2)])
                chain.step(dve, lambda: dve.tensor_copy(unit_rel[:, to, :].rearrange("p u h -> p h u"), turned[:, 0:2, :]))
            fresh_chain("chain_weights")

        NW = L * D
        with ExitStack() as local:
            lsb, lps = maker(local, "sb"), maker(local, "ps")
            wt = lsb("wt", [P, 2, 2, NW])
            ws = lsb("ws", [P, 2, 2 * L * H])
            wt_b = lsb("wt_b", [P, 2, NW])
            ws_b = lsb("ws_b", [P, 2 * L * H])
            with ExitStack() as inner:
                isb, ips = maker(inner, "sb"), maker(inner, "ps")
                att = isb("att", [P, 2, NW])
                prod = isb("prod", [P, NW])
                gam, bet = isb("gam", [P, 2, L]), isb("bet", [P, 2, L])
                scale, shift = isb("scale", [P, 2, L]), isb("shift", [P, 2, L])
                shift_w = isb("shift_w", [P, 2, L, P])
                bias_ps = ips("bias_ps", [P, 2, 512])
                loads = []
                for l in range(L):
                    for k, w in enumerate((a["L0_gnn_W"], a["L0_gnn_res_W"])):
                        for c in range(2):
                            loads.append(lambda l=l, k=k, w=w, c=c: sp.dma_start(
                                wt[:, c, k, l * D:(l + 1) * D].rearrange("p (h d) -> p h d", h=H),
                                w[l, :, c * P:(c + 1) * P, :].rearrange("h p d -> p h d")))
                    for v, g_ in ((gam, a["L0_gnn_bn_gamma"]), (bet, a["L0_gnn_bn_beta"])):
                        for c in range(2):
                            loads.append(lambda l=l, v=v, g_=g_, c=c: sp.dma_start(
                                v[:, c, l:l + 1], g_[l, c * P:(c + 1) * P].rearrange("(p o) -> p o", o=1)))
                for k, v in enumerate((a["L0_gnn_attn_r"], a["L0_gnn_attn_l"])):
                    loads.append(lambda k=k, v=v: sp.dma_start(att[:, k, :], v.rearrange("l h d -> (l h d)").partition_broadcast(P)))
                chain.dma(sp, *loads)
                bcl = lambda v: v.unsqueeze(2).broadcast_to([P, 2, L])
                chain.step(dve, lambda: dve.tensor_tensor(scale[:, :, :], gam[:, :, :], bcl(var), ALU.mult))
                chain.step(dve, lambda: dve.tensor_tensor(shift[:, :, :], scale[:, :, :], bcl(mean), ALU.mult))
                chain.step(dve, lambda: dve.tensor_tensor(shift[:, :, :], bet[:, :, :], shift[:, :, :], ALU.subtract))
                chain.step(dve, lambda: dve.tensor_copy(shift_w[:, :, :, :],
                                                        shift[:, :, :].unsqueeze(3).broadcast_to([P, 2, L, P])))
                for l in range(L):
                    chain.step(pe, *[lambda c=c, k=k: pe.matmul(bias_ps[:, k, 0:D], shift_w[:, c, l, :],
                                                                wt[:, c, k, l * D:(l + 1) * D], start=(c == 0), stop=(c == 1))
                                     for k in range(2) for c in range(2)])
                    chain.step(dve, lambda: dve.tensor_copy(wt_b[:, :, l * D:(l + 1) * D], bias_ps[:, :, 0:D]))
                    chain.apart(*[(dve, lambda c=c: dve.tensor_scalar(
                        wt[:, c, :, l * D:(l + 1) * D], wt[:, c, :, l * D:(l + 1) * D], scale[:, c, l:l + 1], None, ALU.mult))
                        for c in range(2)])
                for k in range(2):
                    for c in range(3):
                        w_, to_ = (wt[:, c, 0, :], ws[:, c, :]) if c < 2 else (wt_b[:, 0, :], ws_b[:, :])
                        chain.step(dve, lambda: dve.tensor_tensor(prod[:, :], w_, att[:, k, :], ALU.mult))
                        chain.step(dve, lambda: dve.tensor_reduce(
                            to_[:, k * L * H:(k + 1) * L * H], prod[:, :].rearrange("p (h d) -> p h d", d=DH), AX, ALU.add))
                fresh_chain("chain_scores")
            srow = lsb("srow", [P, GB, 2 * L * H])
            hb = lsb("hb", [P, 2, GB, P])
            with ExitStack() as inner:
                sc_ps = maker(inner, "ps")("sc_ps", [P, LANES, 512])

                def score_stage(ch, g, k, lo, m):
                    ps = sc_ps[:, k, 0:m * 2 * L * H].rearrange("p (b h) -> p b h", b=m)
                    yield ch.step(act, lambda: act.activation(
                        hb[:, :, lo:lo + m, :], hT[:, :, ds((g * GB + lo) * P, m * P)].rearrange("p c (b n) -> p c b n", n=P), ACT.Copy))
                    yield ch.step(pe, *[lambda b=b, c=c: pe.matmul(ps[:, b, :], hb[:, c, lo + b, :], ws[:, c, :],
                                                                   start=(c == 0), stop=(c == 1)) for b in range(m) for c in range(2)])
                    yield ch.step(dve, lambda: dve.tensor_tensor(srow[:, lo:lo + m, :], ps,
                                                                 ws_b[:, :].unsqueeze(1).broadcast_to([P, m, 2 * L * H]), ALU.add))
                    yield ch.step(dve, lambda: dve.tensor_copy(score_at[:, ds(g * GB + lo, m), 0:L * H],
                                                               srow[:, lo:lo + m, L * H:2 * L * H]))
                    yield ch.move(lambda e: e.dma_start(per_block(score_src[0:NP, :])[:, ds(g * GB + lo, m), :],
                                                        srow[:, lo:lo + m, 0:L * H]),
                                  lambda e: e.dma_start(per_block(table[0:NP, :])[:, ds(g * GB + lo, m), NW:AW],
                                                        srow[:, lo:lo + m, 0:L * H]))

                in_lanes(nc, lanes, 50, 2, score_stage)
                fresh_chain("chain_tables")
            best0 = lsb("best0", [P, T, L * H])
            with ExitStack() as inner:
                top0 = SegmentMax(inner, "m0", score_src, L * H)
                top0.gather(0, QP // QB)
                for t in range(T + 1):
                    act.dma_start(summed[t * P:(t + 1) * P, :], zeros[:, :]).then_inc(cleared, 16)
                with ExitStack() as counting:
                    sources = NodeCount(counting, "src", src_pad, maker(counting, "ps")("counts_src", [P, T])[:, :])
                    sources.open()
                    for e, part in ((dve, sources.one_hots), (pe, sources.products)):
                        with e.Fori(0, NodeCount.GROUPS // 2) as i:
                            for b in range(2):
                                part(2 * i + b, b)
                    sources.close(count_out)
                rank_nodes()
                tables = inner.enter_context(ExitStack())
                isb, ips = maker(tables, "sb"), maker(tables, "ps")
                orow = isb("orow", [P, 2, 2, NW])
                tab_ps = ips("tab_ps", [P, 2, 4, 512])
                pair = [lanes[0], lanes[2]]

                def table_stage(ch, g, k, lo, m):
                    yield ch.step(act, lambda: act.activation(
                        hb[:, :, lo:lo + m, :], hT[:, :, ds((g * GT + lo) * P, m * P)].rearrange("p c (b n) -> p c b n", n=P), ACT.Copy))
                    for b in range(lo, lo + m):
                        yield ch.step(pe, *[lambda c=c, q=q, z=z, c0=c0, c1=c1: pe.matmul(
                            tab_ps[:, k, 2 * q + z, 0:c1 - c0], hb[:, c, b, :], wt[:, c, q, c0:c1], start=(c == 0), stop=(c == 1))
                            for q in range(2) for z, (c0, c1) in enumerate(((0, 512), (512, NW))) for c in range(2)])
                        yield ch.step(dve, *[lambda q=q, z=z, c0=c0, c1=c1: dve.tensor_tensor(
                            orow[:, k, q, c0:c1], tab_ps[:, k, 2 * q + z, 0:c1 - c0], wt_b[:, q, c0:c1], ALU.add)
                            for q in range(2) for z, (c0, c1) in enumerate(((0, 512), (512, NW)))])
                        yield ch.move(lambda e: e.dma_start(table[ds((g * GT + b) * P, P), 0:NW], orow[:, k, 0, :]),
                                      lambda e: e.dma_start(residual[ds((g * GT + b) * P, P), :], orow[:, k, 1, :]))

                in_lanes(nc, pair, 150, 8, table_stage, n=NG, shares=((0, 4), (4, 3)), rest=(), engines=NOT_POOL)
                act.wait_ge(cleared, 16 * (T + 1))
                for c in pair:
                    for e in (sp, dve, pe, act):
                        c.wait(e)
                tables.close()
                nc.all_engine_barrier()
                top0.finish(best0)
                fresh_chain("chain_pass0")
            own_and_max(score_at, best0[:, :, :], L * H, 0.01)
            chain.dma(sp, lambda: sp.dma_start(per_block(score_dst[0:NP, :]), score_at[:, :, :]))
            fresh_chain("chain_edges0")
        stack0.close()
        edge_pass("e0", L * D, heads=L * H, act_heads=5, slope=0.01, tab=table, tab_dst=score_dst)

        with ExitStack() as local:
            lsb = maker(local, "sb")
            sg = lsb("sg", [P, GB, AW])
            rg = lsb("rg", [P, GB, L * D])
            xg = lsb("xg0", [P, GB, D])
            tg = lsb("tg0", [P, GB, D])
            stat = lsb("stat0", [P, LANES, 2, 8])

            def close_stack(ch, g, k, lo, m):
                blk = lambda d: per_block(d[0:NP, :])[:, ds(g * GB + lo, m), :]
                s3, r3, x3, t3 = (v[:, lo:lo + m, :] for v in (sg, rg, xg, tg))
                yield ch.move(lambda e: e.dma_start(s3, blk(summed)), lambda e: e.dma_start(r3, blk(residual)),
                              lambda e: e.dma_start(x3, blk(x_dram)))
                den = s3[:, :, L * D:AW]
                yield ch.step(dve, lambda: dve.tensor_scalar(den, den, 1e-16, None, ALU.max))
                yield ch.step(dve, lambda: dve.reciprocal(den, den))
                by_head = [s3[:, b, 0:L * D].rearrange("p (h d) -> p h d", d=DH) for b in range(m)]
                yield ch.apart(*[(dve, lambda b=b, v=v: dve.tensor_tensor(
                    v, v, den[:, b, :].unsqueeze(2).broadcast_to([P, L * H, DH]), ALU.mult)) for b, v in enumerate(by_head)])
                yield ch.step(dve, lambda: dve.tensor_tensor(r3, r3, s3[:, :, 0:L * D], ALU.add))
                part = [r3[:, :, l * D:(l + 1) * D] for l in range(L)]
                yield ch.step(act, lambda: act.activation(part[1], part[1], ACT.Tanh))
                yield ch.step(dve, lambda: dve.scalar_tensor_tensor(x3, part[0], 0.0, x3, ALU.max, ALU.add))
                yield ch.step(dve, lambda: dve.tensor_tensor(x3, x3, part[1], ALU.add))
                yield from elu(ch, part[2], t3, part[0])
                yield ch.step(dve, lambda: dve.tensor_tensor(x3, x3, part[0], ALU.add))
                yield ch.move(lambda e: e.dma_start(blk(x_dram), x3))
                yield from layer_norm(ch, x3, t3, stat[:, k, :, :], relu=True)
                yield ch.move(lambda e: e.dma_start(blk(h_dram), t3))

            in_lanes(nc, lanes, 120, 5, close_stack, behind=3)
            fresh_chain("chain_l1")

        def load_wT(lsb, name, dram, rows_, cols_):
            v = lsb(name, [P, rows_ // P, cols_])
            return v, lambda: sp.dma_start(v[:, :, :], dram.rearrange("(c p) n -> p c n", p=P))

        def broadcast(lsb, name, dram):
            v = lsb(name, [P, dram.shape[0]])
            return v, lambda: sp.dma_start(v[:, :], dram.partition_broadcast(P))

        def column(lsb, name, dram):
            n = dram.shape[0] // P
            v = lsb(name, [P, n])
            return v, lambda: sp.dma_start(v[:, :], dram.rearrange("(c p) -> p c", p=P), allow_slow_non_contiguous=True)

        with ExitStack() as local:
            lsb, lps = maker(local, "sb"), maker(local, "ps")
            gw, ld = load_wT(lsb, "gw", a["L1_gnn_gat_w"], D, D)
            att = lsb("att1", [P, 2, D])
            prod = lsb("prod1", [P, D])
            ws = lsb("ws1", [P, 2, 2 * H])
            hg = lsb("hg1", [P, GB, D])
            hgT = lsb("hgT1", [P, 2, GB, P])
            og = lsb("og1", [P, GB, D + H])
            sc1 = lsb("score_at1", [P, T, 2 * H])
            best1 = lsb("best1", [P, T, H])
            chain.dma(sp, ld, *[lambda k=k, v=v: sp.dma_start(att[:, k, :], v.rearrange("h d -> (h d)").partition_broadcast(P))
                                for k, v in enumerate((a["L1_gnn_gat_a_src"], a["L1_gnn_gat_a_tgt"]))])
            for k in range(2):
                for c in range(2):
                    chain.step(dve, lambda: dve.tensor_tensor(prod[:, :], gw[:, c, :], att[:, k, :], ALU.mult))
                    chain.step(dve, lambda: dve.tensor_reduce(ws[:, c, k * H:(k + 1) * H],
                                                              prod[:, :].rearrange("p (h d) -> p h d", d=DH), AX, ALU.add))
            table1 = at(table, 0, [[D + H, ROWS], [1, D + H]])
            src1 = at(score_src, 0, [[H, ROWS], [1, H]])
            dst1 = at(score_dst, 0, [[2 * H, ROWS], [1, 2 * H]])
            chain.dma(sp, lambda: sp.dma_start(table1[NP:ROWS, :], zeros[:, 0:D + H]),
                      lambda: sp.dma_start(src1[NP:ROWS, :], zeros[:, 0:H]),
                      lambda: sp.dma_start(dst1[NP:ROWS, :], zeros[:, 0:2 * H]))
            with ExitStack() as inner:
                every_h = maker(inner, "sb")("every_h", [P, T, D])
                every, placed = sem("every_h_loaded"), sem("placed")
                sp.dma_start(every_h[:, :, :], per_block(h_dram[0:NP, :])).then_inc(every, 16)
                pool.wait_ge(every, 16)
                for t in range(T):
                    pool.indirect_dma_start(sorted_h, bass.IndirectOffsetOnAxis(rank_i[:, t:t + 1], 0), every_h[:, t, :],
                                            None).then_inc(placed, 16)
                ips = maker(inner, "ps")
                pr_ps = ips("pr_ps", [P, LANES, 512])
                for e in (sp, pool, pe, dve, act):
                    chain.wait(e)

                def project(ch, g, k, lo, m):
                    h3, o3 = hg[:, lo:lo + m, :], og[:, lo:lo + m, :]
                    hT4 = hgT[:, :, lo:lo + m, :]
                    pr = pr_ps[:, k, :].rearrange("p (b d) -> p b d", d=D)
                    sc = pr_ps[:, k, 0:2 * H * m].rearrange("p (b h) -> p b h", b=m)
                    to = lambda d: per_block(d[0:NP, :])[:, ds(g * GB + lo, m), :]
                    yield ch.move(lambda e: e.dma_start(h3, to(h_dram)))
                    yield from turn_blocks(ch, hT4, h3, pr_ps[:, k, :].rearrange("p (c q n) -> p c q n", c=2, q=2))
                    yield ch.step(pe, *[lambda b=b, c=c: pe.matmul(pr[:, b, :], hT4[:, c, b, :], gw[:, c, :],
                                                                   start=(c == 0), stop=(c == 1)) for b in range(m) for c in range(2)])
                    yield ch.step(act, lambda: act.activation(o3[:, :, 0:D], pr[:, 0:m, :], ACT.Copy))
                    yield ch.step(pe, *[lambda b=b, c=c: pe.matmul(sc[:, b, :], hT4[:, c, b, :], ws[:, c, :],
                                                                   start=(c == 0), stop=(c == 1)) for b in range(m) for c in range(2)])
                    yield ch.apart((dve, lambda: dve.tensor_copy(o3[:, :, D:D + H], sc[:, :, 0:H])),
                                   (dve, lambda: dve.tensor_copy(sc1[:, ds(g * GB + lo, m), 0:H], sc[:, :, H:2 * H])))
                    yield ch.move(lambda e: e.dma_start(to(table1), o3), lambda e: e.dma_start(to(src1), o3[:, :, D:D + H]))

                in_lanes(nc, lanes, 70, 3, project, behind=1)
                pool.wait_ge(placed, 16 * T)
                fresh_chain("chain_max1")
            top1 = SegmentMax(local, "m1", src1, H)
            top1.gather(0, QP // QB)
            with ExitStack() as inner:
                isb, ips = maker(inner, "sb"), maker(inner, "ps")
                win, ld1 = load_wT(isb, "win", a["L1_gnn_in_proj_w"], D, 2 * D)
                wx, ld2 = load_wT(isb, "wx", a["L1_gnn_x_proj_w"], D, 3 * DS)
                cb, ld4 = column(isb, "cb", a["L1_gnn_conv_b"])
                db, ld5 = column(isb, "db", a["L1_gnn_dt_proj_b"])
                cw = isb("cw", [P, 2, 4])
                wdt = isb("wdt", [DS, D])
                ld7 = lambda: sp.dma_start(cw[:, :, :], a["L1_gnn_conv_w"].rearrange("(c p) k -> p c k", p=P))
                ld9 = lambda: sp.dma_start(wdt[:, :], a["L1_gnn_dt_proj_w"])
                chain.dma(sp, ld1, ld2, ld4, ld5, ld7, ld9)
                xg, xT = isb("xg_t", [P, GT, D]), isb("xT_t", [P, 2, GT, P])
                xin = isb("xin", [P, 2, 3 + TS])
                xc, zs = isb("xc", [P, 2, TS]), isb("zs", [P, 2, TS])
                dbc = isb("dbc", [3 * DS, TS])
                dt, dtx = isb("dt", [P, 2, TS]), isb("dtx", [P, 2, TS])
                u_, q_ = isb("u_", [P, 2, TS]), isb("q_", [P, 2, TS])
                mm_ps = ips("mm_ps_t", [P, 2, 512])
                turn = mm_ps[:, 0, :].rearrange("p (c k n) -> p c k n", c=2, k=2)
                halves = lambda v: v.rearrange("p (k n) -> p k n", n=HS)
                chain.step(dve, lambda: dve.memset(xin[:, :, 0:3], 0.0))
                with chain.loop(NG, 200, engines=NOT_POOL) as g:
                    chain.dma(sp, lambda: sp.dma_start(xg[:, :, :], per_block(sorted_h)[:, ds(g * GT, GT), :]))
                    one_by_one(turn_blocks(chain, xT, xg, turn))
                    xT2 = xT[:, :, :, :].rearrange("p c b n -> p c (b n)")
                    for j in range(4):
                        o = mm_ps[:, 0:2, 0:HS]
                        chain.step(pe, *[lambda c=c, z=z: pe.matmul(o[:, z, :], win[:, c, j * P:(j + 1) * P],
                                                                    xT2[:, c, z * HS:(z + 1) * HS], start=(c == 0), stop=(c == 1))
                                         for z in range(2) for c in range(2)])
                        to = xin[:, j, 3:3 + TS] if j < 2 else zs[:, j - 2, :]
                        chain.step(act, lambda: act.activation(halves(to), o, ACT.Copy if j < 2 else ACT.Silu))
                    for c in range(2):
                        chain.step(dve, lambda: dve.tensor_scalar(xc[:, c, :], xin[:, c, 0:TS], cw[:, c, 0:1], cb[:, c:c + 1],
                                                                  ALU.mult, ALU.add))
                        for k in range(1, 4):
                            chain.step(dve, lambda: dve.scalar_tensor_tensor(xc[:, c, :], xin[:, c, k:k + TS], cw[:, c, k:k + 1],
                                                                             xc[:, c, :], ALU.mult, ALU.add))
                    chain.step(act, lambda: act.activation(xc[:, :, :], xc[:, :, :], ACT.Silu))
                    chain.step(dve, lambda: dve.tensor_copy(u_[:, :, 0:3], xin[:, :, TS:TS + 3]))
                    chain.step(dve, lambda: dve.tensor_copy(xin[:, :, 0:3], u_[:, :, 0:3]))
                    chain.step(pe, *[lambda c=c, z=z: pe.matmul(mm_ps[0:3 * DS, z, 0:HS], wx[:, c, :], xc[:, c, z * HS:(z + 1) * HS],
                                                                start=(c == 0), stop=(c == 1)) for z in range(2) for c in range(2)])
                    chain.step(act, lambda: act.activation(halves(dbc[:, :]), mm_ps[0:3 * DS, 0:2, 0:HS], ACT.Copy))
                    for c in range(2):
                        chain.step(pe, *[lambda z=z: pe.matmul(mm_ps[:, z, 0:HS], wdt[:, c * P:(c + 1) * P],
                                                               dbc[0:DS, z * HS:(z + 1) * HS], start=True, stop=True) for z in range(2)])
                        chain.step(act, lambda: act.activation(halves(dt[:, c, :]), mm_ps[:, 0:2, 0:HS], ACT.Identity,
                                                               bias=db[:, c:c + 1]))
                    chain.step(act, lambda: act.activation(u_[:, :, :], dt[:, :, :], ACT.Abs))
                    chain.step(act, lambda: act.activation(u_[:, :, :], u_[:, :, :], ACT.Exp, scale=-1.0))
                    chain.step(dve, lambda: dve.tensor_scalar(q_[:, :, :], u_[:, :, :], 2.0, None, ALU.add))
                    chain.step(dve, lambda: dve.reciprocal(q_[:, :, :], q_[:, :, :]))
                    chain.step(dve, lambda: dve.tensor_tensor(u_[:, :, :], u_[:, :, :], q_[:, :, :], ALU.mult))
                    chain.step(act, lambda: act.activation(q_[:, :, :], u_[:, :, :], ACT.Square))
                    chain.step(dve, lambda: dve.tensor_scalar(dtx[:, :, :], q_[:, :, :], 1.0 / 13, None, ALU.mult))
                    for k in (11, 9, 7, 5, 3):
                        chain.step(dve, lambda: dve.scalar_tensor_tensor(dtx[:, :, :], dtx[:, :, :], 1.0 / k, q_[:, :, :],
                                                                         ALU.add, ALU.mult))
                    chain.step(dve, lambda: dve.scalar_tensor_tensor(dtx[:, :, :], dtx[:, :, :], 1.0, u_[:, :, :], ALU.add, ALU.mult))
                    chain.step(dve, lambda: dve.tensor_scalar(dt[:, :, :], dt[:, :, :], 0.0, None, ALU.max))
                    chain.step(dve, lambda: dve.scalar_tensor_tensor(dt[:, :, :], dtx[:, :, :], 2.0, dt[:, :, :], ALU.mult, ALU.add))
                    chain.step(dve, lambda: dve.tensor_tensor(dtx[:, :, :], dt[:, :, :], xc[:, :, :], ALU.mult))
                    now = ds(g * TS, TS)
                    chain.dma(sp, *[lambda n=n, v=v: sp.dma_start(by_time[n][:, :, now], v[:, :, :])
                                    for n, v in (("xc", xc), ("zs", zs), ("dt", dt), ("dtx", dtx))],
                              *[lambda k=k: sp.dma_start(bc_rows[ds(g * DS, DS), k, :], dbc[(1 + k) * DS:(2 + k) * DS, :])
                                for k in range(2)])
                for e in (sp, act, dve, pe):
                    chain.wait(e)
            top1.finish(best1)
            gmax = lsb("gmax", [P, 2])
            some = lsb("some", [P, T])
            off = lsb("off", [P, T])
            val = lsb("val", [P, T, H])
            own_and_max(sc1, best1[:, :, :], H, 0.2)
            chain.step(dve, lambda: dve.tensor_scalar(some[:, :], count_in[:, :], 1.0, None, ALU.min))
            chain.step(dve, lambda: dve.tensor_scalar(off[:, :], some[:, :], -1.0, BIG, ALU.add, ALU.mult))
            bch = lambda v: v.unsqueeze(2).broadcast_to([P, T, H])
            chain.step(dve, lambda: dve.tensor_tensor(val[:, :, :], sc1[:, :, H:2 * H], bch(some[:, :]), ALU.mult))
            chain.step(dve, lambda: dve.tensor_tensor(val[:, :, :], val[:, :, :], bch(off[:, :]), ALU.add))
            chain.step(dve, lambda: dve.tensor_reduce(gmax[:, 0:1], val[:, :, :].rearrange("p t h -> p (t h)"), AX, ALU.max))
            chain.step(pool, lambda: pool.partition_all_reduce(gmax[:, 1:2], gmax[:, 0:1], P, RMAX))
            chain.step(dve, lambda: dve.tensor_scalar(sc1[:, :, H:2 * H], val[:, :, :], 0.0, gmax[:, 1:2], ALU.mult, ALU.add))
            chain.dma(sp, lambda: sp.dma_start(per_block(dst1[0:NP, :]), sc1[:, :, :]))

            fresh_chain("chain_pass1")
        with ExitStack() as local:
            edges = EdgePass(local, "e1", D, heads=H, act_heads=4, slope=0.2, tab=table1, tab_dst=dst1)
            lsb, lps = maker(local, "sb"), maker(local, "ps")
            K, STEPS = 2 * DS, UB // 2
            MR = K // STEPS
            al = lsb("al", [P, 2, DS])
            dt, dtx = lsb("dt_s", [P, 2, TS]), lsb("dtx_s", [P, 2, TS])
            bc = lsb("bc", [P, 2, 2, TS])
            decay, inp = lsb("decay", [P, 2, TS]), lsb("inp", [P, 2, TS])
            hs, prod = lsb("hs", [P, 2, TS]), lsb("prod_t", [P, 2, TS])
            y_sb = lsb("y_sb", [P, 2, TS])
            state = lsb("state", [P, K])
            y_ps = lps("y_ps", [P, 4, 512])
            s_decay, s_inp, s_scan, s_prod, s_y, s_state, s_dt, s_copied, s_stored = (
                sem(f"t_{n}") for n in ("decay", "inp", "scan", "prod", "y", "state", "dt", "copied", "stored"))
            s_bc = [sem(f"t_bc{b}") for b in range(2)]
            chain.dma(sp, lambda: sp.dma_start(al[:, :, :], a["L1_gnn_A_log"].rearrange("(c p) k -> p c k", p=P)),
                      *[lambda k=k, z=z: sp.dma_start(bc_rows[NG * DS:NG * DS + 2, k, z * HS:(z + 1) * HS], zeros[0:2, 0:HS])
                        for k in range(2) for z in range(2)])
            chain.step(act, lambda: act.activation(al[:, :, :], al[:, :, :], ACT.Exp))
            chain.step(dve, lambda: dve.tensor_scalar(al[:, :, :], al[:, :, :], -1.0, None, ALU.mult))
            chain.step(dve, lambda: dve.memset(state[:, :], 0.0))
            for e in (sp, act, dve, pe):
                chain.wait(e)
            for s in (s_scan, s_prod, s_y, s_state):
                dve.sem_inc(s, 2)

            def load_bc(r, b):
                if not isinstance(r, int):
                    sp.wait_ge(s_prod, STEPS * (r - 1) + 2 * b + 4)
                sp.dma_start(bc[:, b, :, :], bc_rows[ds(2 * r + b, 1), :, :].rearrange("o k t -> (o k t)").partition_broadcast(P)
                             ).then_inc(s_bc[b], 16)

            def make_input(r, k):
                b, c = k // 2, k % 2
                if c == 0:
                    dve.wait_ge(s_bc[b], 16 * (r + 1))
                dve.wait_ge(s_scan, STEPS * r + k + 1)
                dve.tensor_tensor(inp[:, c, :], bc[:, b, 0, :], dtx[:, c, :], ALU.mult).then_inc(s_inp, 1)

            def scan(r, k, m):
                q, c = STEPS * r + k, k % 2
                dve.wait_ge(s_inp, q + 1)
                dve.wait_ge(s_decay, q + 1)
                dve.wait_ge(s_prod, q + 1)
                dve.wait_ge(s_state, q + 1)
                dve.tensor_tensor_scan(hs[:, c, :], decay[:, c, :], inp[:, c, :], state[:, ds(STEPS * m + k, 1)],
                                       ALU.mult, ALU.add).then_inc(s_scan, 1)

            def times_c(r, k):
                q, b, c = STEPS * r + k, k // 2, k % 2
                dve.wait_ge(s_scan, q + 3)
                dve.wait_ge(s_y, q + 1)
                dve.tensor_tensor(prod[:, c, :], bc[:, b, 1, :], hs[:, c, :], ALU.mult).then_inc(s_prod, 1)

            def make_decay(r, k, m):
                act.wait_ge(s_scan, STEPS * r + k + 1)
                act.activation(decay[:, k % 2, :], dt[:, k % 2, :], ACT.Exp,
                               scale=al[:, k % 2, ds(STEPS // 2 * m + k // 2, 1)]).then_inc(s_decay, 1)

            def keep_state(r, k, m):
                act.wait_ge(s_scan, STEPS * r + k + 3)
                act.activation(state[:, ds(STEPS * m + k, 1)], hs[:, k % 2, TS - 1:TS], ACT.Copy).then_inc(s_state, 1)

            def add_up(r, k):
                c = k % 2
                pe.wait_ge(s_prod, STEPS * r + k + 3)
                for z in range(2):
                    mm = pe.matmul(y_ps[:, 2 * c + z, 0:HS], ident[:, :], prod[:, c, z * HS:(z + 1) * HS],
                                   start=False, stop=False, skip_group_check=True)
                mm.then_inc(s_y, 1)

            for b in range(2):
                load_bc(0, b)
            edges.rounds(0, 1)
            with nc.Fori(0, NG) as g:
                now = ds(g * TS, TS)
                sp.wait_ge(s_decay, g * K)
                sp.dma_start(dt[:, :, :], by_time["dt"][:, :, now]).then_inc(s_dt, 16)
                sp.wait_ge(s_inp, g * K)
                sp.dma_start(dtx[:, :, :], by_time["dtx"][:, :, now]).then_inc(s_dt, 16)
                pe.wait_ge(s_copied, 2 * g)
                for z in range(4):
                    pe.matmul(y_ps[:, z, 0:HS], zeros[:, 0:P], zeros[:, 0:HS], start=True, stop=False, skip_group_check=True)
                with nc.Fori(0, MR) as m:
                    r = g * MR + m
                    i = r + 1
                    edges.pool_round(i)
                    for k in range(STEPS):
                        v = 2 * k
                        edges.sp_slot(i, v)
                        edges.sp_slot(i, v + 1)
                        if k % 2:
                            load_bc(r + 1, k // 2)
                        if k == 0:
                            dve.wait_ge(s_dt, 32 * (g + 1))
                            act.wait_ge(s_dt, 32 * (g + 1))
                        make_input(r, k)
                        edges.dve_slot(i, v)
                        scan(r, k, m)
                        edges.dve_slot(i, v + 1)
                        times_c(r, k)
                        make_decay(r, k, m)
                        edges.act_slot(i, v)
                        edges.act_slot(i, v + 1)
                        keep_state(r, k, m)
                        edges.pe_slot(i, v)
                        edges.pe_slot(i, v + 1)
                        add_up(r, k)
                act.wait_ge(s_y, g * K + K + 2)
                act.wait_ge(s_stored, 16 * g)
                for c in range(2):
                    act.activation(y_sb[:, c, :].rearrange("p (k n) -> p k n", n=HS), y_ps[:, 2 * c:2 * c + 2, 0:HS],
                                   ACT.Copy).then_inc(s_copied, 1)
                sp.wait_ge(s_copied, 2 * g + 2)
                sp.dma_start(by_time["y"][:, :, now], y_sb[:, :, :]).then_inc(s_stored, 16)
            edges.rounds(1 + NG * MR, EdgePass.ROUNDS - 1 - NG * MR)
            for b in range(2):
                sp.wait_ge(s_bc[b], 16 * (NG * MR + 1))
            sp.wait_ge(s_stored, 16 * NG)
            for e in (act, dve, pe):
                e.wait_ge(s_state, NG * K + 2)
                e.wait_ge(s_y, NG * K + 2)
            edges.end()

        fresh_chain("chain_time")
        with ExitStack() as local:
            lsb, lps = maker(local, "sb"), maker(local, "ps")
            wo, ld1 = load_wT(lsb, "wo", a["L1_gnn_out_proj_w"], D, D)
            dp, ld2 = column(lsb, "dp", a["L1_gnn_D_param"])
            chain.dma(sp, ld1, ld2)
            y_t, x_t, z_t = (lsb(f"{n}_t", [P, 2, GB * P]) for n in "yxz")
            o_t = lsb("o_t", [P, GB, D])
            o_ps = lps("o_ps_t", [P, LANES, 512])
            for e in (sp, pool, pe, dve):
                chain.wait(e)

            def gate_and_project(ch, g, k, lo, m):
                y3, x3, z3 = (v[:, :, lo * P:(lo + m) * P] for v in (y_t, x_t, z_t))
                o2 = o_ps[:, k, :].rearrange("p (b d) -> p b d", d=D)
                now = ds((g * GB + lo) * P, m * P)
                yield ch.move(*[lambda e, n=n, v=v: e.dma_start(v, by_time[n][:, :, now])
                                for n, v in (("y", y3), ("xc", x3), ("zs", z3))])
                yield ch.apart(*[(dve, lambda c=c: dve.scalar_tensor_tensor(y3[:, c, :], x3[:, c, :], dp[:, c:c + 1], y3[:, c, :],
                                                                            ALU.mult, ALU.add)) for c in range(2)])
                yield ch.step(dve, lambda: dve.tensor_tensor(y3, y3, z3, ALU.mult))
                yield ch.step(pe, *[lambda b=b, c=c: pe.matmul(o2[:, b, :], y3[:, c, b * P:(b + 1) * P], wo[:, c, :],
                                                               start=(c == 0), stop=(c == 1)) for b in range(m) for c in range(2)])
                yield ch.step(act, lambda: act.activation(o_t[:, lo:lo + m, :], o2[:, 0:m, :], ACT.Copy))
                yield ch.move(lambda e: e.dma_start(per_block(sorted_y)[:, ds(g * GB + lo, m), :], o_t[:, lo:lo + m, :]))

            in_lanes(nc, lanes, 120, 4, gate_and_project, behind=1)
            fresh_chain("chain_merge")

        with ExitStack() as local:
            lsb, lps = maker(local, "sb"), maker(local, "ps")
            y_all = lsb("y_all", [P, T, D])
            returned = sem("returned")
            for t in range(T):
                pool.indirect_dma_start(y_all[:, t, :], None, sorted_y, bass.IndirectOffsetOnAxis(rank_i[:, t:t + 1], 0)
                                        ).then_inc(returned, 16)
            names = ("gat_b", "ln_local_g", "ln_local_b", "ln_global_g", "ln_global_b", "ln2_g", "ln2_b", "ff2_b")
            vecs, loads = {}, []
            for n in names:
                vecs[n], ld = broadcast(lsb, f"v_{n}", a[f"L1_gnn_{n}"])
                loads.append(ld)
            wl, l1 = load_wT(lsb, "wl", a["L1_gnn_wl"], D, D)
            wg, l2 = load_wT(lsb, "wg", a["L1_gnn_wg"], D, D)
            f1, l3 = load_wT(lsb, "f1", a["L1_gnn_ff1_w"], D, 2 * D)
            f2, l4 = load_wT(lsb, "f2", a["L1_gnn_ff2_w"], 2 * D, D)
            fb, l5 = column(lsb, "fb", a["L1_gnn_ff1_b"])
            chain.dma(sp, *loads, l1, l2, l3, l4, l5)
            sg = lsb("sg1", [P, GB, D + H])
            hg, hl, ha = (lsb(n, [P, GB, D]) for n in ("hg2", "hl", "ha"))
            tg = lsb("tg2", [P, GB, D])
            xT, yT = (lsb(n, [P, 2, GB, P]) for n in ("hlT", "haT"))
            stat = lsb("stat1", [P, LANES, 2, 8])
            bank = lps("bank2", [P, LANES, 512])
            for e in (sp, pool, pe, dve, act):
                chain.wait(e)

            def merge(ch, g, k, lo, m):
                blk = lambda d: per_block(d[0:NP, :])[:, ds(g * GB + lo, m), :]
                s3, h3, l3, a3, t3 = (v[:, lo:lo + m, :] for v in (sg, hg, hl, ha, tg))
                lT, aT = xT[:, :, lo:lo + m, :], yT[:, :, lo:lo + m, :]
                fT = [aT[:, j, :, :].rearrange("p b n -> p (b n)") for j in range(2)]
                fT += [t3.rearrange("p b d -> p (b d)")[:, j * m * P:(j + 1) * m * P] for j in range(2)]
                st, tn = stat[:, k, :, :], bank[:, k, :].rearrange("p (c q n) -> p c q n", c=2, q=2)
                o_ps = bank[:, k, :].rearrange("p (b d) -> p b d", d=D)
                ff = bank[:, k, 0:m * P]
                bv = lambda n: vecs[n][:, :].unsqueeze(1).broadcast_to([P, m, D])
                yield ch.move(lambda e: e.dma_start(s3, blk(summed[:, 0:D + H])), lambda e: e.dma_start(h3, blk(h_dram)))
                den = s3[:, :, D:D + H]
                yield ch.step(dve, lambda: dve.tensor_scalar(den, den, 1e-16, None, ALU.add))
                yield ch.step(dve, lambda: dve.reciprocal(den, den))
                heads = lambda v, b: v[:, b, 0:D].rearrange("p (h d) -> p h d", d=DH)
                yield ch.apart(*[(dve, lambda b=b: dve.tensor_tensor(
                    heads(l3, b), heads(s3, b), den[:, b, :].unsqueeze(2).broadcast_to([P, H, DH]), ALU.mult)) for b in range(m)])
                yield ch.step(dve, lambda: dve.tensor_tensor(l3, l3, h3, ALU.add))
                yield ch.step(dve, lambda: dve.tensor_tensor(l3, l3, bv("gat_b"), ALU.add))
                yield from elu(ch, l3, t3, l3)
                yield from layer_norm(ch, l3, l3, st, gain=vecs["ln_local_g"][:, :], shift=vecs["ln_local_b"][:, :])
                yield from turn_blocks(ch, lT, l3, tn)
                dve.wait_ge(returned, 16 * T)
                yield ch.step(dve, lambda: dve.tensor_tensor(a3, h3, y_all[:, ds(g * GB + lo, m), :], ALU.add))
                yield from layer_norm(ch, a3, a3, st, gain=vecs["ln_global_g"][:, :], shift=vecs["ln_global_b"][:, :])
                yield from turn_blocks(ch, aT, a3, tn)
                yield ch.step(pe, *[lambda b=b, c=c: pe.matmul(o_ps[:, b, :], (lT, aT)[c // 2][:, c % 2, b, :],
                                                               (wl, wg)[c // 2][:, c % 2, :], start=(c == 0), stop=(c == 3))
                                    for b in range(m) for c in range(4)])
                yield ch.step(act, lambda: act.activation(t3, o_ps[:, 0:m, :], ACT.Sigmoid))
                yield ch.step(dve, lambda: dve.tensor_tensor(l3, l3, a3, ALU.subtract))
                yield ch.step(dve, lambda: dve.tensor_tensor(l3, l3, t3, ALU.mult))
                yield ch.step(dve, lambda: dve.tensor_tensor(l3, l3, a3, ALU.add))
                yield from turn_blocks(ch, lT, l3, tn)
                for j in range(4):
                    yield ch.step(pe, *[lambda c=c: pe.matmul(ff, f1[:, c, j * P:(j + 1) * P], lT[:, c, :, :],
                                                              start=(c == 0), stop=(c == 1)) for c in range(2)])
                    yield ch.step(act, lambda: act.activation(fT[j], ff, ACT.Relu, bias=fb[:, j:j + 1]))
                yield ch.step(pe, *[lambda b=b, j=j: pe.matmul(o_ps[:, b, :], fT[j][:, b * P:(b + 1) * P], f2[:, j, :],
                                                               start=(j == 0), stop=(j == 3)) for b in range(m) for j in range(4)])
                yield ch.step(dve, lambda: dve.tensor_tensor(l3, l3, o_ps[:, 0:m, :], ALU.add))
                yield ch.step(dve, lambda: dve.tensor_tensor(l3, l3, bv("ff2_b"), ALU.add))
                yield from layer_norm(ch, l3, l3, st, gain=vecs["ln2_g"][:, :], shift=vecs["ln2_b"][:, :])
                yield ch.move(lambda e: e.dma_start(a3, blk(x_dram)))
                yield ch.step(dve, lambda: dve.tensor_tensor(a3, a3, l3, ALU.add))
                yield ch.move(lambda e: e.dma_start(blk(x_dram), a3))
                yield from layer_norm(ch, a3, l3, st, relu=True)
                yield ch.move(lambda e: e.dma_start(blk(h_dram), l3))

            in_lanes(nc, lanes, 220, 5, merge, behind=3)
            fresh_chain("chain_pass2")

        edge_pass("e2", D, weighted=True, tab=h_dram)
        finish = ExitStack()
        with finish:
            lsb = maker(finish, "sb")
            sg, hg, xg, tg, og = (lsb(n, [P, GB, D]) for n in ("sg_f", "hg_f", "xg_f", "tg_f", "og_f"))
            xT, yT = (lsb(n, [P, 2, GB, P]) for n in ("hT_f", "sT_f"))
            stat = lsb("stat_f", [P, LANES, 2, 8])
            w1, l1 = load_wT(lsb, "w1", a["L2_gnn_W1"], D, D)
            w2, l2 = load_wT(lsb, "w2", a["L2_gnn_W2"], D, D)
            w3, l3 = load_wT(lsb, "w3", a["L3_gnn_W"], D, D)
            w4, l4 = load_wT(lsb, "w4", a["L3_gnn_M"], D, D)
            b1, l5 = broadcast(lsb, "b1", a["L2_gnn_b1"])
            b2, l6 = broadcast(lsb, "b2", a["L2_gnn_b2"])
            chain.dma(sp, l1, l2, l3, l4, l5, l6)
            chain.step(dve, lambda: dve.tensor_tensor(b1[:, :], b1[:, :], b2[:, :], ALU.add))
            for e in (sp, pool, pe, dve, act):
                chain.wait(e)

            def load_and_multiply(ch, g, k, lo, m, wa, wb, interact):
                blk = lambda d: per_block(d[0:NP, :])[:, ds(g * GB + lo, m), :]
                s3, h3, x3 = (v[:, lo:lo + m, :] for v in (sg, hg, xg))
                hT4, sT4 = xT[:, :, lo:lo + m, :], yT[:, :, lo:lo + m, :]
                o_ps = mm_ps[:, k, :].rearrange("p (b d) -> p b d", d=D)
                yield ch.move(lambda e: e.dma_start(s3, blk(summed[:, 0:D])), lambda e: e.dma_start(h3, blk(h_dram)),
                              lambda e: e.dma_start(x3, blk(x_dram)))
                if interact:
                    yield ch.step(dve, lambda: dve.scalar_tensor_tensor(s3, h3, 1.0, s3, ALU.add, ALU.mult))
                yield from turn_blocks(ch, hT4, h3, turn[:, k, :, :, :])
                yield from turn_blocks(ch, sT4, s3, turn[:, k, :, :, :])
                yield ch.step(pe, *[lambda b=b, c=c: pe.matmul(o_ps[:, b, :], (hT4, sT4)[c // 2][:, c % 2, b, :],
                                                               (wa, wb)[c // 2][:, c % 2, :], start=(c == 0), stop=(c == 3))
                                    for b in range(m) for c in range(4)])

            def interaction(ch, g, k, lo, m):
                blk = lambda d: per_block(d[0:NP, :])[:, ds(g * GB + lo, m), :]
                x3, t3, o3 = (v[:, lo:lo + m, :] for v in (xg, tg, og))
                o_ps = mm_ps[:, k, :].rearrange("p (b d) -> p b d", d=D)
                yield from load_and_multiply(ch, g, k, lo, m, w1, w2, True)
                norm = stat[:, k, 0:m, 0]
                yield ch.step(dve, lambda: dve.tensor_tensor(o3, o_ps[:, 0:m, :],
                                                             b1[:, :].unsqueeze(1).broadcast_to([P, m, D]), ALU.add))
                yield ch.step(dve, lambda: dve.scalar_tensor_tensor(o3, o3, 0.2, o3, ALU.mult, ALU.max))
                yield ch.step(act, lambda: act.activation(t3, o3, ACT.Square))
                yield ch.step(dve, lambda: dve.tensor_reduce(norm, t3, AX, ALU.add))
                yield ch.step(act, lambda: act.activation(norm, norm, ACT.Sqrt))
                yield ch.step(dve, lambda: dve.tensor_scalar(norm, norm, 1e-12, None, ALU.max))
                yield ch.step(dve, lambda: dve.reciprocal(norm, norm))
                yield ch.step(dve, lambda: dve.tensor_tensor(o3, o3, norm.unsqueeze(2).broadcast_to([P, m, D]), ALU.mult))
                yield ch.step(dve, lambda: dve.tensor_tensor(x3, x3, o3, ALU.add))
                yield ch.move(lambda e: e.dma_start(blk(x_dram), x3))
                yield from layer_norm(ch, x3, o3, stat[:, k, :, :], relu=True)
                yield ch.move(lambda e: e.dma_start(blk(h_dram), o3))

            def banks(stack, n):
                bank = maker(stack, "ps")(f"bank{n}", [P, LANES, 512])
                return bank[:, :, :].rearrange("p k (c q n) -> p k c q n", c=2, q=2), bank

            with ExitStack() as inner:
                turn, mm_ps = banks(inner, 3)
                in_lanes(nc, lanes, 120, 5, interaction)
            fresh_chain("chain_pass3")
            edge_pass("e3", D, tab=h_dram)

            def linear(ch, g, k, lo, m):
                x3 = xg[:, lo:lo + m, :]
                o_ps = mm_ps[:, k, :].rearrange("p (b d) -> p b d", d=D)
                yield from load_and_multiply(ch, g, k, lo, m, w3, w4, False)
                yield ch.step(dve, lambda: dve.scalar_tensor_tensor(x3, o_ps[:, 0:m, :], 0.0, x3, ALU.max, ALU.add))

            def store(ch, g, lo, m):
                whole = out[0:(T - 1) * P, :].rearrange("(t p) c -> p t c", p=P)
                return ch.move(lambda e: e.dma_start(whole[:, ds(g * GB + lo, m), :], xg[:, lo:lo + m, :]))

            def linear_and_store(ch, g, k, lo, m):
                yield from linear(ch, g, k, lo, m)
                yield store(ch, g, lo, m)

            def linear_and_store_last(ch, g, k, lo, m):
                yield from linear(ch, g, k, lo, m)
                if lo + m < T % GB:
                    yield store(ch, g, lo, m)
                else:
                    if m > 1:
                        yield store(ch, g, lo, m - 1)
                    yield ch.move(lambda e: e.dma_start(out[(T - 1) * P:N, :], xg[0:TAIL, lo + m - 1, :]))

            turn, mm_ps = banks(finish, 4)
            in_lanes(nc, lanes, 80, 4, linear_and_store, last=linear_and_store_last, behind=1)
            for c in lanes:
                c.wait(sp)


_TURNED = {"L1_gnn_gat_w", "L1_gnn_in_proj_w", "L1_gnn_x_proj_w", "L1_gnn_dt_proj_w", "L1_gnn_out_proj_w",
           "L1_gnn_wl", "L1_gnn_wg", "L1_gnn_ff1_w", "L1_gnn_ff2_w", "L2_gnn_W1", "L2_gnn_W2"}


def kernel(**inputs):
    import numpy as _np
    import concourse.bacc as _bacc
    from concourse import mybir as _mybir
    from concourse.bass_utils import run_bass_kernel_spmd as _run

    nc = _bacc.Bacc("TRN2", target_bir_lowering=False, num_devices=1)
    arrays, args = {}, {}
    for name, given in inputs.items():
        v = _np.asarray(given)
        v = _np.ascontiguousarray(v.T if name in _TURNED else v)
        arrays[f"in_{name}"] = v
        args[name] = nc.dram_tensor(f"in_{name}", v.shape, _mybir.dt.from_np(v.dtype), kind="ExternalInput").ap()
    out = nc.dram_tensor("out_0", [N, D], _mybir.dt.float32, kind="ExternalOutput").ap()
    graph_stack_kernel(nc, args, out)
    result = _run(nc, [arrays], core_ids=[0])
    return result.results[0]["out_0"]
```
